# Optimizing a Trainium2 kernel written in Bass

```python
import numpy as np
import jax
import jax.numpy as jnp

def _softmax(x, axis=-1):
    return jax.nn.softmax(x, axis=axis)

def _gelu(x):
    return jax.nn.gelu(x, approximate=True)

def _silu(x):
    return jax.nn.silu(x)

def _sigmoid(x):
    return jax.nn.sigmoid(x)

def _layernorm(x, axis=-1, eps=1e-05):
    m = jnp.mean(x, axis=axis, keepdims=True)
    v = jnp.var(x, axis=axis, keepdims=True)
    return (x - m) / jnp.sqrt(v + eps)

def _scatter_add(tgt, idx, src, axis=0):
    return tgt.at[idx].add(src)

def _segment_sum(src, seg, n):
    return jax.ops.segment_sum(src, seg, n)
kernel_name = 'mk_adaln_d1_jaxref_r8_f835c7'

def setup_inputs(seed: int=0):
    np.random.seed(seed)
    _w = jnp.asarray

    def _L0_attn_setup():
        import jax, jax.numpy as jnp
        import numpy as np
        HEADS, HEAD_SIZE, FREQS, MAX_PERIOD = (16, 64, 32, 1250)
        D_MODEL = 128
        NEG_INF = -1000000000.0

        def sinusoid_embedding(seq_len, frequencies, max_period):
            pos = np.arange(seq_len, dtype=np.float64)[:, None]
            idx = np.arange(frequencies)[None, :]
            inv_freq = max_period ** (-(idx // 2 * 2) / frequencies)
            angle = pos * inv_freq
            table = np.where(idx % 2 == 0, np.sin(angle), np.cos(angle))
            return table.astype(np.float32)

        def relative_causal(scores):
            L = scores.shape[-1]
            d = jnp.clip(jnp.arange(L)[:, None] - jnp.arange(L)[None, :], 0, L - 1)
            return jnp.take_along_axis(scores, d[None, None, :, :], axis=-1)
        key = jax.random.key(seed)
        ks = jax.random.split(key, 4)
        u = np.sqrt(3.0)
        inp = jax.random.normal(ks[0], (2, 256, D_MODEL), dtype=jnp.float32)
        qkv = jax.random.uniform(ks[1], (D_MODEL, 3, HEADS, HEAD_SIZE), jnp.float32, -u, u)
        q_bias = jnp.zeros((HEADS, HEAD_SIZE), jnp.float32)
        positional = jax.random.uniform(ks[2], (FREQS, HEADS, HEAD_SIZE), jnp.float32, -u, u)
        out_kernel = jax.random.uniform(ks[3], (HEADS * HEAD_SIZE, D_MODEL), jnp.float32, -u, u)
        out_bias = jnp.zeros((D_MODEL,), jnp.float32)
        return {'input': inp, 'qkv': qkv, 'q_bias': q_bias, 'positional': positional, 'out_kernel': out_kernel, 'out_bias': out_bias}
    _L0_attn_in = _L0_attn_setup()

    def _L0_ffn_setup():
        import jax, jax.numpy as jnp
        import numpy as np
        DIM = 128
        DEPTH = 2
        HEADS = 8
        DIM_HEAD = 64
        WINDOW = 64
        INNER = HEADS * DIM_HEAD
        HID = int(DIM * 4 * 2 / 3)
        B, N = (2, 1024)
        QK_SCALE = 8.0

        def shift_token(t):
            t1, t2 = jnp.split(t, 2, axis=-1)
            t2 = jnp.pad(t2, ((0, 0), (1, 0), (0, 0)))[:, :-1]
            return jnp.concatenate([t1, t2], axis=-1)

        def l2norm(t):
            return t / jnp.clip(jnp.linalg.norm(t, axis=-1, keepdims=True), 1e-12)

        def rotate_half(x):
            x1, x2 = jnp.split(x, 2, axis=-1)
            return jnp.concatenate([-x2, x1], axis=-1)

        def rotary_xpos(q, k):
            n = q.shape[-2]
            half_idx = jnp.arange(0, DIM_HEAD, 2, dtype=jnp.float32)
            inv_freq = 1.0 / 10000.0 ** (half_idx / DIM_HEAD)
            t = jnp.arange(n, dtype=jnp.float32)
            freqs = t[:, None] * inv_freq[None, :]
            freqs = jnp.concatenate([freqs, freqs], axis=-1)
            base = (half_idx + 0.4 * DIM_HEAD) / (1.4 * DIM_HEAD)
            power = (t - n // 2) / float(WINDOW // 2)
            scale = base[None, :] ** power[:, None]
            scale = jnp.concatenate([scale, scale], axis=-1)
            cos, sin = (jnp.cos(freqs), jnp.sin(freqs))
            q = q * cos * scale + rotate_half(q) * sin * scale
            k = k * cos / scale + rotate_half(k) * sin / scale
            return (q, k)

        def local_attention(q, k, v):
            b, h, n, d = q.shape
            w = n // WINDOW
            bq = q.reshape(b, h, w, WINDOW, d) * QK_SCALE
            bk = k.reshape(b, h, w, WINDOW, d)
            bv = v.reshape(b, h, w, WINDOW, d)

            def look_around(t):
                p = jnp.pad(t, ((0, 0), (0, 0), (1, 0), (0, 0), (0, 0)))
                return jnp.concatenate([p[:, :, :w], p[:, :, 1:]], axis=3)
            bk, bv = (look_around(bk), look_around(bv))
            bt = jnp.arange(n).reshape(w, WINDOW)
            btp = jnp.pad(bt, ((1, 0), (0, 0)), constant_values=-1)
            btk = jnp.concatenate([btp[:w], btp[1:]], axis=1)
            sim = jnp.einsum('bhwid,bhwjd->bhwij', bq, bk)
            i = bt[:, :, None]
            j = btk[:, None, :]
            mask = (i < j) | (i > j + WINDOW) | (j == -1)
            sim = jnp.where(mask, -jnp.finfo(sim.dtype).max, sim)
            attn = jax.nn.softmax(sim, axis=-1)
            out = jnp.einsum('bhwij,bhwjd->bhwid', attn, bv)
            return out.reshape(b, h, n, d)

        def _layer(x, wqkv, qs, ksc, wo, lg, lb, w1, b1, w2, b2):
            b, n, _ = x.shape
            h = shift_token(x)
            qkv = h @ wqkv
            q, k, v = jnp.split(qkv, 3, axis=-1)
            to_heads = lambda t: t.reshape(b, n, HEADS, DIM_HEAD).transpose(0, 2, 1, 3)
            q, k, v = (to_heads(q), to_heads(k), to_heads(v))
            q = l2norm(q) * qs
            k = l2norm(k) * ksc
            q, k = rotary_xpos(q, k)
            o = local_attention(q, k, v)
            o = o.transpose(0, 2, 1, 3).reshape(b, n, INNER)
            x = x + o @ wo
            h = shift_token(x)
            mu = h.mean(-1, keepdims=True)
            var = h.var(-1, keepdims=True)
            h = (h - mu) / jnp.sqrt(var + 1e-05) * lg + lb
            h = h @ w1 + b1
            a, g = jnp.split(h, 2, axis=-1)
            h = a * jax.nn.gelu(g, approximate=False)
            x = x + h @ w2 + b2
            return x
        key = jax.random.key(seed)
        ks = jax.random.split(key, 6)
        return {'x': jax.random.normal(ks[0], (B, N, DIM), jnp.float32), 'wqkv': jax.random.normal(ks[1], (DEPTH, DIM, 3 * INNER), jnp.float32) * 0.02, 'q_scale': jnp.ones((DEPTH, DIM_HEAD), jnp.float32), 'k_scale': jnp.ones((DEPTH, DIM_HEAD), jnp.float32), 'wo': jax.random.normal(ks[2], (DEPTH, INNER, DIM), jnp.float32) * 0.02, 'ln_g': jnp.ones((DEPTH, DIM), jnp.float32), 'ln_b': jnp.zeros((DEPTH, DIM), jnp.float32), 'w1': jax.random.normal(ks[3], (DEPTH, DIM, 2 * HID), jnp.float32) * 0.02, 'b1': jnp.zeros((DEPTH, 2 * HID), jnp.float32), 'w2': jax.random.normal(ks[4], (DEPTH, HID, DIM), jnp.float32) * 0.02, 'b2': jnp.zeros((DEPTH, DIM), jnp.float32)}
    _L0_ffn_in = _L0_ffn_setup()
    _L0_c = _w((lambda *s: np.random.randn(*s).astype(np.float32) * 0.05)(4, 128))
    _L0_wmod = _w((lambda *s: np.random.randn(*s).astype(np.float32) * 0.05)(128, 6 * 128) * 128 ** (-0.5))
    _d = {'L0_attn_input': _L0_attn_in['input'], 'L0_attn_qkv': _L0_attn_in['qkv'], 'L0_attn_q_bias': _L0_attn_in['q_bias'], 'L0_attn_positional': _L0_attn_in['positional'], 'L0_attn_out_kernel': _L0_attn_in['out_kernel'], 'L0_attn_out_bias': _L0_attn_in['out_bias'], 'L0_ffn_wqkv': _L0_ffn_in['wqkv'], 'L0_ffn_q_scale': _L0_ffn_in['q_scale'], 'L0_ffn_k_scale': _L0_ffn_in['k_scale'], 'L0_ffn_wo': _L0_ffn_in['wo'], 'L0_ffn_ln_g': _L0_ffn_in['ln_g'], 'L0_ffn_ln_b': _L0_ffn_in['ln_b'], 'L0_ffn_w1': _L0_ffn_in['w1'], 'L0_ffn_b1': _L0_ffn_in['b1'], 'L0_ffn_w2': _L0_ffn_in['w2'], 'L0_ffn_b2': _L0_ffn_in['b2'], 'L0_c': _L0_c, 'L0_wmod': _L0_wmod}
    _x0 = _d['L0_attn_input']
    _d['L0_attn_input'] = jax.random.normal(jax.random.fold_in(jax.random.key(seed), 1), (4, 1024, 128), dtype=_x0.dtype)
    del _x0
    return _d

def reference(L0_attn_input, L0_attn_qkv, L0_attn_q_bias, L0_attn_positional, L0_attn_out_kernel, L0_attn_out_bias, L0_ffn_wqkv, L0_ffn_q_scale, L0_ffn_k_scale, L0_ffn_wo, L0_ffn_ln_g, L0_ffn_ln_b, L0_ffn_w1, L0_ffn_b1, L0_ffn_w2, L0_ffn_b2, L0_c, L0_wmod):

    def _L0_attn_ref(input, qkv, q_bias, positional, out_kernel, out_bias):
        import jax, jax.numpy as jnp
        import numpy as np
        HEADS, HEAD_SIZE, FREQS, MAX_PERIOD = (16, 64, 32, 1250)
        D_MODEL = 128
        NEG_INF = -1000000000.0

        def sinusoid_embedding(seq_len, frequencies, max_period):
            pos = np.arange(seq_len, dtype=np.float64)[:, None]
            idx = np.arange(frequencies)[None, :]
            inv_freq = max_period ** (-(idx // 2 * 2) / frequencies)
            angle = pos * inv_freq
            table = np.where(idx % 2 == 0, np.sin(angle), np.cos(angle))
            return table.astype(np.float32)

        def relative_causal(scores):
            L = scores.shape[-1]
            d = jnp.clip(jnp.arange(L)[:, None] - jnp.arange(L)[None, :], 0, L - 1)
            return jnp.take_along_axis(scores, d[None, None, :, :], axis=-1)
        b, s, x = input.shape
        n, h = (HEADS, HEAD_SIZE)
        w = qkv * (3.0 * x * h * n) ** (-0.25)
        q, k, v = jnp.einsum('bsx,xAnh->Abnsh', input, w)
        q = q + q_bias[:, None, :]
        a = jnp.einsum('bnqh,bnkh->bnqk', q, k) * h ** (-0.5)
        sins = jnp.asarray(np.sqrt(2.0) * sinusoid_embedding(s, FREQS, MAX_PERIOD))
        emb = jnp.einsum('sf,fnh->nsh', sins, positional * FREQS ** (-0.5))
        pos_scores = jnp.einsum('bnqh,nvh->bnqv', q, emb) * h ** (-0.5)
        a = a + relative_causal(pos_scores)
        mask = jnp.tril(jnp.ones((s, s), dtype=bool))
        a = jax.nn.softmax(jnp.where(mask, a, NEG_INF), axis=-1)
        o = jnp.einsum('bnqk,bnkh->bqnh', a, v).reshape(b, s, n * h)
        fan_in, fan_out = out_kernel.shape
        out = o @ (out_kernel * (fan_in * fan_out) ** (-0.25)) + out_bias
        return out

    def _L0_ffn_ref(x, wqkv, q_scale, k_scale, wo, ln_g, ln_b, w1, b1, w2, b2):
        import jax, jax.numpy as jnp
        import numpy as np
        DIM = 128
        DEPTH = 2
        HEADS = 8
        DIM_HEAD = 64
        WINDOW = 64
        INNER = HEADS * DIM_HEAD
        HID = int(DIM * 4 * 2 / 3)
        B, N = (2, 1024)
        QK_SCALE = 8.0

        def shift_token(t):
            t1, t2 = jnp.split(t, 2, axis=-1)
            t2 = jnp.pad(t2, ((0, 0), (1, 0), (0, 0)))[:, :-1]
            return jnp.concatenate([t1, t2], axis=-1)

        def l2norm(t):
            return t / jnp.clip(jnp.linalg.norm(t, axis=-1, keepdims=True), 1e-12)

        def rotate_half(x):
            x1, x2 = jnp.split(x, 2, axis=-1)
            return jnp.concatenate([-x2, x1], axis=-1)

        def rotary_xpos(q, k):
            n = q.shape[-2]
            half_idx = jnp.arange(0, DIM_HEAD, 2, dtype=jnp.float32)
            inv_freq = 1.0 / 10000.0 ** (half_idx / DIM_HEAD)
            t = jnp.arange(n, dtype=jnp.float32)
            freqs = t[:, None] * inv_freq[None, :]
            freqs = jnp.concatenate([freqs, freqs], axis=-1)
            base = (half_idx + 0.4 * DIM_HEAD) / (1.4 * DIM_HEAD)
            power = (t - n // 2) / float(WINDOW // 2)
            scale = base[None, :] ** power[:, None]
            scale = jnp.concatenate([scale, scale], axis=-1)
            cos, sin = (jnp.cos(freqs), jnp.sin(freqs))
            q = q * cos * scale + rotate_half(q) * sin * scale
            k = k * cos / scale + rotate_half(k) * sin / scale
            return (q, k)

        def local_attention(q, k, v):
            b, h, n, d = q.shape
            w = n // WINDOW
            bq = q.reshape(b, h, w, WINDOW, d) * QK_SCALE
            bk = k.reshape(b, h, w, WINDOW, d)
            bv = v.reshape(b, h, w, WINDOW, d)

            def look_around(t):
                p = jnp.pad(t, ((0, 0), (0, 0), (1, 0), (0, 0), (0, 0)))
                return jnp.concatenate([p[:, :, :w], p[:, :, 1:]], axis=3)
            bk, bv = (look_around(bk), look_around(bv))
            bt = jnp.arange(n).reshape(w, WINDOW)
            btp = jnp.pad(bt, ((1, 0), (0, 0)), constant_values=-1)
            btk = jnp.concatenate([btp[:w], btp[1:]], axis=1)
            sim = jnp.einsum('bhwid,bhwjd->bhwij', bq, bk)
            i = bt[:, :, None]
            j = btk[:, None, :]
            mask = (i < j) | (i > j + WINDOW) | (j == -1)
            sim = jnp.where(mask, -jnp.finfo(sim.dtype).max, sim)
            attn = jax.nn.softmax(sim, axis=-1)
            out = jnp.einsum('bhwij,bhwjd->bhwid', attn, bv)
            return out.reshape(b, h, n, d)

        def _layer(x, wqkv, qs, ksc, wo, lg, lb, w1, b1, w2, b2):
            b, n, _ = x.shape
            h = shift_token(x)
            qkv = h @ wqkv
            q, k, v = jnp.split(qkv, 3, axis=-1)
            to_heads = lambda t: t.reshape(b, n, HEADS, DIM_HEAD).transpose(0, 2, 1, 3)
            q, k, v = (to_heads(q), to_heads(k), to_heads(v))
            q = l2norm(q) * qs
            k = l2norm(k) * ksc
            q, k = rotary_xpos(q, k)
            o = local_attention(q, k, v)
            o = o.transpose(0, 2, 1, 3).reshape(b, n, INNER)
            x = x + o @ wo
            h = shift_token(x)
            mu = h.mean(-1, keepdims=True)
            var = h.var(-1, keepdims=True)
            h = (h - mu) / jnp.sqrt(var + 1e-05) * lg + lb
            h = h @ w1 + b1
            a, g = jnp.split(h, 2, axis=-1)
            h = a * jax.nn.gelu(g, approximate=False)
            x = x + h @ w2 + b2
            return x
        for l in range(DEPTH):
            x = _layer(x, wqkv[l], q_scale[l], k_scale[l], wo[l], ln_g[l], ln_b[l], w1[l], b1[l], w2[l], b2[l])
        return x
    x = L0_attn_input
    mod = (_silu(L0_c) @ L0_wmod).reshape(L0_c.shape[0], 6, 1, -1)
    sa, ca, ga, sb, cb, gb = (mod[:, 0], mod[:, 1], mod[:, 2], mod[:, 3], mod[:, 4], mod[:, 5])
    ga = (2 * (ga >= 0) - 1) * jnp.maximum(jnp.abs(ga), 0.25)
    gb = (2 * (gb >= 0) - 1) * jnp.maximum(jnp.abs(gb), 0.25)
    h = _layernorm(x, axis=-1) * (1 + ca) + sa
    x = x + ga * _L0_attn_ref(h, L0_attn_qkv, L0_attn_q_bias, L0_attn_positional, L0_attn_out_kernel, L0_attn_out_bias)
    h = _layernorm(x, axis=-1) * (1 + cb) + sb
    x = x + gb * _L0_ffn_ref(h, L0_ffn_wqkv, L0_ffn_q_scale, L0_ffn_k_scale, L0_ffn_wo, L0_ffn_ln_g, L0_ffn_ln_b, L0_ffn_w1, L0_ffn_b1, L0_ffn_w2, L0_ffn_b2)
    return x

_drawn_inputs = setup_inputs


def setup_inputs(seed=0):
    import zlib

    import numpy as np

    out = dict(_drawn_inputs(seed))
    spreads = {'L0_attn_q_bias': (0.0, 0.8),
     'L0_attn_out_bias': (0.0, 0.342),
     'L0_ffn_q_scale': (1.0, 0.6),
     'L0_ffn_k_scale': (1.0, 0.6),
     'L0_ffn_ln_g': (1.0, 0.6),
     'L0_ffn_ln_b': (0.0, 0.8),
     'L0_ffn_b1': (0.0, 0.8),
     'L0_ffn_b2': (0.0, 0.8)}
    factors = {'L0_attn_qkv': 3.264,
     'L0_attn_positional': 8.0,
     'L0_attn_out_kernel': 3.253,
     'L0_ffn_wqkv': 8.0,
     'L0_ffn_wo': 7.963,
     'L0_ffn_w1': 8.0,
     'L0_ffn_w2': 8.0}
    for name, (base, spread) in spreads.items():
        noise = np.random.default_rng([zlib.crc32(name.encode()), seed]).standard_normal(out[name].shape)
        drawn = base * np.exp(spread * noise) if base else spread * noise
        out[name] = jnp.asarray(drawn.astype(out[name].dtype))
    for name, factor in factors.items():
        out[name] = (out[name] * factor).astype(out[name].dtype)
    return out
```

```python
import numpy as np
import concourse.bass as bass
from concourse import mybir
from contextlib import ExitStack, contextmanager

F32 = mybir.dt.float32
F32R = mybir.dt.float32r
BF16 = mybir.dt.bfloat16
ALU = mybir.AluOpType
ACT = mybir.ActivationFunctionType
AX = mybir.AxisListType

P = 128
B, S, D = 4, 1024, 128
H, DH, FREQS = 16, 64, 32
PAIRS = H // 2
TILES = S // P
CH = 512
DEPTH = 2
LH, LD = 8, 64
WIN = 64
HID = int(D * 4 * 2 / 3)
NHID = -(-HID // P)
BIG = -1e30
QKV_C = (3.0 * D * DH * H) ** -0.25
OUT_C = (H * DH * D) ** -0.25
ZW = S + 4

STEPS = [(c, j) for c in range(S // CH) for j in range(4 * (c + 1))]
PIECES = [(i, 0, min(P * (i + 1), CH)) for i in range(TILES)] + [(i, CH, P * (i + 1) - CH) for i in range(4, TILES)]
NS, NPC = len(STEPS), len(PIECES)


def _half(c, j):
    return max(0, P * j - CH * c)


@contextmanager
def semaphores(nc, suffix=""):
    held = []

    def sem(name):
        held.append(nc.alloc_semaphore(name=name + suffix))
        return held[-1]
    yield sem
    nc.clear_and_free_semaphores(held)
    nc.all_engine_barrier()


class Mem:
    pass


def add_mod_and_weights(nc, m, i, scratch):
    with ExitStack() as ctx:
        sb = lambda n, s, d=F32: ctx.enter_context(nc.sbuf_tensor(n, s, d))
        ps = lambda n, s: ctx.enter_context(nc.psum_tensor(n, s, F32))
        sem = ctx.enter_context(semaphores(nc))
        w3 = sb("w3", [P, 3, H * DH])
        wqT = sb("wqT", [DH, H, P])
        posT = sb("posT", [DH, H, 2 * FREQS])
        biasT = sb("biasT", [P, H])
        cT = sb("cT", [P, B])
        sT = sb("sT", [P, B])
        wmod = sb("wmod", [P, 6 * D])
        wc = sb("wc", [P, PAIRS, 4, P])
        whl = sb("whl", [P, PAIRS, 2, 4 * P], F32R)
        sg = sb("sg", [P, 2, B])
        ab = sb("ab", [P, 2, B])
        masks = sb("masks32", [P, 2 * P + 2 * 192])
        comp = [ps(f"comp{k}", [P, CH]) for k in range(2)]
        modp = ps("modp", [P, CH])
        biasp = ps("biasp", [P, CH])
        loaded, consts, weights_out = sem("loaded"), sem("consts_in"), sem("weights_out")
        silu_done, mod_ready, comp_ready, pos_bias = sem("silu_done"), sem("mod_ready"), sem("comp_ready"), sem("pos_bias")
        chain, wc_ready, lo_ready = sem("chain"), sem("wc_ready"), sem("lo_ready")
        block = ctx.enter_context(nc.Block())
        NC = 8

        @block.sync
        def _(sp):
            sp.dma_start(w3[:, :, :], i["qkv"].rearrange("x a n h -> x a (n h)")).then_inc(loaded, 16)
            sp.dma_start(wqT[:, :, :], i["wqT"]).then_inc(loaded, 16)
            sp.dma_start(posT[:, :, :], i["posT"]).then_inc(loaded, 16)
            sp.dma_start(biasT[0:DH, :], i["biasT"]).then_inc(loaded, 16)
            sp.dma_start(cT[:, :], i["cT"]).then_inc(loaded, 16)
            sp.dma_start(wmod[:, :], i["wmod"]).then_inc(loaded, 16)
            sp.dma_start(m.ident[:, :], i["ident"]).then_inc(consts, 16)
            sp.dma_start(m.mean[:, :], i["mean"]).then_inc(consts, 16)
            sp.dma_start(m.oneh[:, :, :], i["oneh"]).then_inc(consts, 16)
            sp.dma_start(m.sel[:, :, :], i["sel"]).then_inc(consts, 16)
            sp.dma_start(masks[:, :], i["masks"]).then_inc(consts, 16)
            sp.dma_start(m.vecs[:, :], i["vecs"]).then_inc(consts, 16)
            sp.dma_start(m.b1[:, :, :, :], i["b1"]).then_inc(consts, 16)
            sp.dma_start(m.X[:, :], i["xT"]).then_inc(consts, 16)
            sp.wait_ge(consts, 16 * NC)
            sp.wait_ge(wc_ready, 5)
            sp.wait_ge(lo_ready, 1)
            sp.dma_start(scratch.rearrange("q p w -> p q w"),
                         whl[:, :, :, :].bitcast(F32).rearrange("p q a w -> p q (a w)")).then_inc(weights_out, 16)
            sp.wait_ge(weights_out, 16)

        @block.scalar
        def _(act):
            act.wait_ge(loaded, 96)
            act.activation(sT[:, :], cT[:, :], ACT.Silu).then_inc(silu_done, 1)

        @block.tensor
        def _(pe):
            pe.wait_ge(loaded, 96)
            for h in range(H):
                mm = pe.matmul(comp[h // 8][:, 64 * (h % 8):64 * (h % 8) + 64], wqT[:, h, :], posT[:, h, :],
                               start=(h % 8 == 0), stop=True, skip_group_check=True)
            mm.then_inc(comp_ready, 1)
            for h in range(H):
                mm = pe.matmul(biasp[64:128, h:1 + h], posT[:, h, :], biasT[0:DH, h:h + 1],
                               start=(h == 0), stop=True, skip_group_check=True)
            mm.then_inc(pos_bias, 1)
            pe.wait_ge(silu_done, 1)
            for k in range(6):
                mm = pe.matmul(modp[:, B * k:B * k + B], wmod[:, P * k:P * k + P], sT[:, :],
                               start=(k == 0), stop=True, skip_group_check=True)
            mm.then_inc(mod_ready, 1)

        @block.vector
        def _(dve):
            dve.wait_ge(loaded, 96)
            src = w3[:, :, :].rearrange("p a (q n) -> p a q n", n=P)
            q2 = w3[:, 0, :].rearrange("p (q e d) -> p q e d", e=2, d=DH)
            dve.tensor_copy(wc[:, :, 0:2, 0:DH], q2).then_inc(wc_ready, 1)
            dve.tensor_copy(wc[:, :, 2, :], src[:, 1]).then_inc(wc_ready, 1)
            dve.tensor_copy(wc[:, :, 3, :], src[:, 2]).then_inc(wc_ready, 1)
            dve.wait_ge(comp_ready, 1)
            for k in range(2):
                last = dve.tensor_copy(wc[:, 4 * k:4 * k + 4, 0:2, DH:P],
                                       comp[k][:, :].rearrange("p (q e d) -> p q e d", e=2, d=DH))
            last.then_inc(wc_ready, 1)
            dve.wait_ge(wc_ready, 4)
            dve.tensor_copy(whl[:, :, 0, :], wc[:, :, :, :].rearrange("p q a w -> p q (a w)")).then_inc(wc_ready, 1)
            dve.wait_ge(wc_ready, 5)
            dve.tensor_tensor(whl[:, :, 1, :], wc[:, :, :, :].rearrange("p q a w -> p q (a w)"),
                              whl[:, :, 0, :].bitcast(F32), ALU.subtract).then_inc(lo_ready, 1)
            dve.tensor_scalar(m.bias[0:DH, :], biasT[0:DH, :], 1.0 / QKV_C, None, ALU.mult)
            dve.wait_ge(pos_bias, 1)
            dve.tensor_scalar(m.bias[DH:P, :], biasp[DH:P, 0:H], 1.0 / QKV_C, None, ALU.mult)
            dve.wait_ge(consts, 16 * NC)
            dve.tensor_copy(m.identb[:, :], m.ident[:, :])
            dve.tensor_copy(m.masks[:, :], masks[:, :])
            for k in range(2):
                for e in range(2):
                    dve.tensor_copy(m.lmask[:, k, 192 * e:192 * e + 192], masks[:, 2 * P + 192 * k:2 * P + 192 * k + 192])
            dve.wait_ge(mod_ready, 1)
            dve.tensor_copy(m.mod[:, :, :], modp[:, 0:6 * B].rearrange("p (k b) -> p k b", b=B)).then_inc(chain, 1)
            dve.wait_ge(chain, 1)
            mod2 = m.mod[:, :, :].rearrange("p (a t) b -> p a t b", t=3)
            dve.tensor_scalar(mod2[:, :, 1, :], mod2[:, :, 1, :], 1.0, None, ALU.add)
            dve.tensor_scalar(sg[:, :, :], mod2[:, :, 2, :], 0.0, 2.0, ALU.is_ge, ALU.mult).then_inc(chain, 1)
            dve.scalar_tensor_tensor(out=ab[:, :, :], in0=mod2[:, :, 2, :], scalar=-1.0, in1=mod2[:, :, 2, :],
                                     op0=ALU.mult, op1=ALU.max).then_inc(chain, 1)
            dve.wait_ge(chain, 3)
            dve.tensor_scalar(sg[:, :, :], sg[:, :, :], -1.0, None, ALU.add).then_inc(chain, 1)
            dve.tensor_scalar(ab[:, :, :], ab[:, :, :], 0.25, None, ALU.max).then_inc(chain, 1)
            dve.wait_ge(chain, 5)
            dve.tensor_tensor(mod2[:, :, 2, :], ab[:, :, :], sg[:, :, :], ALU.mult)


def add_layernorm(nc, m, name, src, scale, shift, dst):
    N = B * S // CH
    with ExitStack() as ctx:
        sb = lambda n, s, d=F32: ctx.enter_context(nc.sbuf_tensor(f"{name}_{n}", s, d))
        ps = lambda n, s: ctx.enter_context(nc.psum_tensor(f"{name}_{n}", s, F32))
        sem = ctx.enter_context(semaphores(nc, f"_{name}"))
        dev = sb("dev", [P, N, CH])
        sq = sb("sq", [P, 2, CH])
        sd = sb("sd", [N, CH])
        rstd = sb("rstd", [N, CH])
        meanp = [ps(f"meanp{k}", [P, CH]) for k in range(2)]
        varp = ps("varp", [P, CH])
        rb = [ps(f"rb{k}", [P, CH]) for k in range(2)]
        mean_ready, dev_ready, sq_ready, sq_used, var_ready = (
            sem("mean_ready"), sem("dev_ready"), sem("sq_ready"), sem("sq_used"), sem("var_ready"))
        sd_ready, rstd_ready, rb_ready, norm_ready, mod_ready, hi_ready = (
            sem("sd_ready"), sem("rstd_ready"), sem("rb_ready"), sem("norm_ready"), sem("mod_ready"), sem("hi_ready"))
        block = ctx.enter_context(nc.Block())

        @block.tensor
        def _(pe):
            for n in range(N + 1):
                if n < N:
                    if n >= 2:
                        pe.wait_ge(dev_ready, n - 1)
                    pe.matmul(meanp[n % 2][:, :], m.mean[:, :], src(n), start=True, stop=True).then_inc(mean_ready, 1)
                if n >= 1:
                    pe.wait_ge(sq_ready, n)
                    mm = pe.matmul(varp[0:N, :], m.oneh[:, n - 1, :], sq[:, (n - 1) % 2, :],
                                   start=(n == 1), stop=(n == N))
                    mm.then_inc(sq_used, 1)
            pe.wait_ge(rstd_ready, 1)
            for n in range(N):
                if n >= 2:
                    pe.wait_ge(norm_ready, n - 1)
                pe.matmul(rb[n % 2][:, :], m.sel[:, n, :], rstd[:, :], start=True, stop=True).then_inc(rb_ready, 1)

        @block.vector
        def _(dve):
            if dst == "Z":
                dve.memset(m.Z3[64:P, :, 0:1], 0.0)
            for n in range(N):
                dve.wait_ge(mean_ready, n + 1)
                dve.tensor_tensor(dev[:, n, :], src(n), meanp[n % 2][:, :], ALU.subtract).then_inc(dev_ready, 1)
            dve.wait_ge(sd_ready, 1)
            dve.reciprocal(rstd[:, :], sd[:, :]).then_inc(rstd_ready, 1)
            for n in range(N):
                dve.wait_ge(rb_ready, n + 1)
                dve.tensor_tensor(dev[:, n, :], dev[:, n, :], rb[n % 2][:, :], ALU.mult).then_inc(norm_ready, 1)
                dve.wait_ge(norm_ready, n + 1)
                if dst == "split":
                    dve.tensor_scalar(dev[:, n, :], dev[:, n, :], scale(n), shift(n), ALU.mult, ALU.add).then_inc(mod_ready, 1)
                else:
                    b, c = n // 2, CH * (n % 2)
                    for lo, o in ((0, 0), (64, 1)):
                        dve.tensor_scalar(m.Z3[lo:lo + 64, b, c + o:c + o + CH], dev[lo:lo + 64, n, :],
                                          scale(n)[lo:lo + 64], shift(n)[lo:lo + 64], ALU.mult, ALU.add)

        @block.scalar
        def _(act):
            for n in range(N):
                act.wait_ge(dev_ready, n + 1)
                if n >= 2:
                    act.wait_ge(sq_used, n - 1)
                act.activation(sq[:, n % 2, :], dev[:, n, :], ACT.Square).then_inc(sq_ready, 1)
            act.wait_ge(sq_used, N)
            act.activation(sd[:, :], varp[0:N, :], ACT.Sqrt, bias=m.eps[0:N, :]).then_inc(sd_ready, 1)
            if dst == "split":
                for n in range(N):
                    act.wait_ge(mod_ready, n + 1)
                    act.activation(m.HH[:, n, :], dev[:, n, :], ACT.Copy).then_inc(hi_ready, 1)

        @block.gpsimd
        def _(pool):
            if dst == "split":
                for n in range(N):
                    pool.wait_ge(hi_ready, n + 1)
                    pool.tensor_tensor(m.HL[:, n, :], dev[:, n, :], m.HH[:, n, :].bitcast(F32), ALU.subtract)


def add_attention(nc, m, i, scratch, dinv):
    ITERS = PAIRS // 2 * B
    PREP, SLOT = 10, 4
    with ExitStack() as ctx:
        sb = lambda n, s, d=F32: ctx.enter_context(nc.sbuf_tensor(n, s, d))
        ps = lambda n, s=(P, CH): ctx.enter_context(nc.psum_tensor(n, list(s), F32))
        sem = ctx.enter_context(semaphores(nc))

        qh = [sb(f"qh{h}", [P, S], F32R) for h in range(SLOT)]
        ql = [sb(f"ql{h}", [P, S], F32R) for h in range(SLOT)]
        kh = [sb(f"kh{h}", [P, S], F32R) for h in range(SLOT)]
        kl = [sb(f"kl{h}", [P, S], F32R) for h in range(SLOT)]
        v1 = [sb(f"v1{p}", [P, TILES, 3, DH]) for p in range(2)]
        wts = [sb(f"wts{p}", [P, 2, 4, P], F32R) for p in range(2)]
        wo = [sb(f"wo{p}", [P, P]) for p in range(2)]
        qf = sb("qf", [P, 2, CH])
        qt = sb("qt", [P, 2, CH])
        vt = sb("vt", [P, S])
        pt = sb("pt", [P, 3, CH])
        mxp = sb("mxp", [P, 2, NPC])
        mrow = sb("mrow", [TILES, 2, P], F32R)
        ou = [sb(f"ou{e}", [P, S]) for e in range(2)]
        den = sb("den", [P, 2, TILES])
        rcp = sb("rcp", [P, 2, TILES])
        rb = sb("rb", [P, S])
        ot = sb("ot", [P, S])
        qa = sb("qa", [P, S])
        tk32 = sb("tk32", [P, S])
        st = [ps(f"st{k}") for k in range(2)]
        sm = [ps(f"sm{k}") for k in range(2)]
        po = [ps(f"po{k}") for k in range(2)]
        g0, g1 = ps("g0"), ps("g1")

        tables_in, ready = sem("tables_in"), sem("ready")
        ready_t = sem("table_parts")
        w_in = [sem("wA_in"), sem("wB_in")]
        wo_in = [sem("woA_in"), sem("woB_in")]
        g0_ready = sem("g0_ready")
        g0_by_dve, g0_by_act = sem("g0_by_dve"), sem("g0_by_act")
        g1_ready, g1_read = sem("g1_ready"), sem("g1_read")
        qt_ready, qf_ready = sem("qt_ready"), sem("qf_ready")
        qsum_ready = sem("qsum_ready")
        qh_ready, ql_ready = sem("qh_ready"), sem("ql_ready")
        kh_ready, kl_ready = sem("kh_ready"), sem("kl_ready")
        sm_ready, mx_done = sem("sm_ready"), sem("mx_done")
        mx_ready, mrow_in = sem("mx_ready"), sem("mrow_in")
        st_ready, pt_ready, pv_done = sem("st_ready"), sem("pt_ready"), sem("pv_done")
        ou_ready = sem("ou_ready")
        den_in, rcp_ready, dinv_out, rb_in = sem("den_in"), sem("rcp_ready"), sem("dinv_out"), sem("rb_in")
        ot_ready = sem("ot_ready")

        PROJ = [("q", 0, 0), ("q", 0, 1), ("k", 0, 0), ("k", 0, 1), ("q", 1, 0), ("q", 1, 1),
                ("v", 0, 0), ("v", 0, 1), ("vt", 0, 0), ("vt", 0, 1)]
        BY_DVE = 6
        QH_LATE = 2
        MAX_AT = [0, 2, 4, 6, 7, 8, 9, 10, 11]
        MROW_AT, RCP_AT, OUT_AT = 9, 4, (3, 5)

        def pieces_at(s):
            ends = MAX_AT + [NPC] * NS
            return range(ends[s], ends[s + 1])

        def cols(c, j):
            return slice(_half(c, j), CH)

        block = ctx.enter_context(nc.Block())

        @block.sync
        def _(sp):
            def group(it):
                return (it >> 2) & 3 if isinstance(it, int) else sp.snap(it >> 2) & 3

            def load_w(p, u):
                u = bass.ds(u, 1)
                src = scratch.rearrange("(u s) p w -> s p u w", s=2)[p][:, u, :]
                sp.dma_start(wts[p][:, :, :, :].bitcast(F32).rearrange("p a c w -> p (a c w)"),
                             src.rearrange("p u w -> p (u w)")).then_inc(w_in[p], 16)

            def load_wo(p, u):
                u = bass.ds(u, 1)
                src = i["wo"].rearrange("(u s p) d -> s p u d", s=2, p=P)[p][:, u, :]
                sp.dma_start(wo[p][:, :], src.rearrange("p u d -> p (u d)")).then_inc(wo_in[p], 16)

            def reciprocals(n, e):
                row = 64 * (1 - e)
                sp.wait_ge(ou_ready, 2 * n + 4)
                sp.dma_start(den[:, e, :], ou[e][row:row + 1, :].rearrange("a (p t) -> a p t", t=TILES))\
                  .then_inc(den_in, 16)
                sp.wait_ge(rcp_ready, n + 2)
                sp.dma_start(dinv[e].rearrange("(p t) -> p t", t=TILES), rcp[:, e, :]).then_inc(dinv_out, 16)
                sp.wait_ge(dinv_out, 16 * (n + 1))
                sp.dma_start(rb[64 * e:64 * e + 64, :], dinv[e:e + 1].broadcast_to([64, S])).then_inc(rb_in, 16)

            def send_max(slot, par, use):
                sp.wait_ge(g1_read, use)
                sp.dma_start(qh[slot][96:97, :].bitcast(F32).rearrange("a (t w) -> a t w", t=TILES),
                             mrow[:, par, :].bitcast(F32)).then_inc(mrow_in, 16)

            load_w(0, 0)
            load_w(1, 0)
            sp.dma_start(qa[:, :], i["qa"]).then_inc(tables_in, 16)
            sp.dma_start(tk32[DH:DH + FREQS, :], i["tk"]).then_inc(tables_in, 16)
            load_wo(0, 0)
            load_wo(1, 0)
            send_max(0, 0, 1)
            with sp.Fori(0, ITERS) as it:
                for q in range(2):
                    g = 2 * it + q
                    u, now = group(it + 1), group(it + q)
                    sp.wait_ge(g0_ready, PREP * g + PREP)
                    load_w(q, u)
                    send_max((2 * q + 1) % SLOT, 1, 4 * g + 2)
                    reciprocals(2 * g, 0)
                    send_max((2 * q + 2) % SLOT, 0, 4 * g + 5)
                    load_wo(1 - q, now)
                    reciprocals(2 * g + 1, 1)
            for p in range(2):
                sp.wait_ge(w_in[p], 16 * (ITERS + 1))
                sp.wait_ge(wo_in[p], 16 * (ITERS + 1))

        @block.tensor
        def _(pe):
            def three(out, w_hi, w_lo, x_hi, x_lo, stop=True):
                pe.matmul(out, w_hi, x_hi, start=True, stop=False)
                pe.matmul(out, w_hi, x_lo, start=False, stop=False)
                return pe.matmul(out, w_lo, x_hi, start=False, stop=stop)

            def project(n, p, b, before, first=False):
                if n > BY_DVE:
                    pe.wait_ge(g0_by_act, 4 * before + n - BY_DVE)
                elif n in (3, 4):
                    pe.wait_ge(kl_ready, 4 * before + 2 * (n - 2))
                elif n > 0:
                    pe.wait_ge(g0_by_dve, 4 * before + (n if n < 3 else n - 2))
                elif not first:
                    pe.wait_ge(g0_by_act, 4 * before)
                what, e, c = PROJ[n]
                if what == "vt":
                    pe.wait_ge(g0_by_act, 4 * before + 2)
                    for t in range(4):
                        mm = pe.transpose(g0[:, P * t:P * t + P], vt[:, CH * c + P * t:CH * c + P * t + P], m.ident[:, :])
                else:
                    w = {"q": e, "k": 2, "v": 3}[what]
                    xh = m.HH[:, bass.ds(2 * b + c, 1), :].rearrange("p a w -> p (a w)")
                    xl = m.HL[:, bass.ds(2 * b + c, 1), :].rearrange("p a w -> p (a w)")
                    mm = three(g0[:, :], wts[p][:, 0, w, :], wts[p][:, 1, w, :], xh, xl)
                mm.then_inc(g0_ready, 1)

            def max_piece(p, slot, n, first=False):
                t, k0, w = PIECES[p]
                if not (first and p < 2):
                    pe.wait_ge(mx_done, NPC * n + p - 1)
                diag = k0 + w == P * (t + 1)
                out = sm[p % 2]
                mm = pe.matmul(out[:, 0:w], qh[slot][0:96, P * t:P * t + P], kh[slot][0:96, k0:k0 + w],
                               start=True, stop=not diag)
                if diag:
                    mm = pe.matmul(out[:, w - P:w], m.identb[:, :], m.masks[:, 0:P], start=False, stop=True)
                mm.then_inc(sm_ready, 1)

            def turn_max(n, par):
                pe.wait_ge(mx_ready, n + 1)
                pe.transpose(g1[0:TILES, 0:P], mxp[:, par, 0:TILES], m.ident[:, :]).then_inc(g1_ready, 1)

            def scores(s, slot, t):
                c, j = STEPS[s]
                k = slice(P * j, P * j + P)
                x = slice(CH * c + _half(c, j), CH * c + CH)
                w = CH - _half(c, j)
                out = st[s % 2]
                pe.matmul(out[:, 0:w], kh[slot][0:97, k], qh[slot][0:97, x], start=True, stop=False)
                pe.matmul(out[:, 0:w], kh[slot][0:96, k], ql[slot][0:96, x], start=False, stop=False)
                mm = pe.matmul(out[:, 0:w], kl[slot][0:96, k], qh[slot][0:96, x], start=False, stop=j < 4 * c)
                if j >= 4 * c:
                    mm = pe.matmul(out[:, 0:P], m.identb[:, :], m.masks[:, P:2 * P], start=False, stop=True)
                mm.then_inc(st_ready, 1)

            def outputs(s, q, e, t, k, g):
                c, j = STEPS[s]
                if j == 0:
                    pe.wait_ge(ou_ready, k + 1)
                    pe.wait_ge(g0_by_act, 4 * g + 4)
                pe.wait_ge(pt_ready, t + 2)
                v = v1[q][:, j, :, :].rearrange("p a d -> p (a d)")[:, 64 * e:64 * e + P]
                mm = pe.matmul(po[c][:, cols(c, j)], v, pt[:, s % 3, 0:CH - _half(c, j)],
                               start=(j == 0), stop=(j == 4 * c + 3))
                mm.then_inc(pv_done, 1)

            def product(c, p, g, use):
                pe.wait_ge(g1_read, use)
                if c == 0:
                    pe.wait_ge(ot_ready, 2 * g + 3)
                pe.matmul(g1[:, :], wo[p][:, :], ot[:, CH * c:CH * c + CH], start=True, stop=True).then_inc(g1_ready, 1)

            pe.wait_ge(ready, 3)
            pe.wait_ge(w_in[0], 16)
            for n in range(PREP):
                project(n, 0, 0, 0, first=True)
            pe.wait_ge(qh_ready, 4)
            pe.wait_ge(kh_ready, 4)
            for p in range(NPC):
                max_piece(p, 0, 0, first=True)
            turn_max(0, 0)
            pe.wait_ge(ql_ready, 4)
            pe.wait_ge(kl_ready, 4)
            pe.wait_ge(mrow_in, 16)
            scores(0, 0, 0)
            with pe.Fori(0, ITERS) as it:
                for q in range(2):
                    g = 2 * it + q
                    for e in range(2):
                        n = 2 * g + e
                        nxt = (2 * q + e + 1) % SLOT
                        for s in range(NS):
                            t = NS * n + s
                            pe.wait_ge(pt_ready, t + 1)
                            if s + 1 < NS:
                                scores(s + 1, 2 * q + e, t + 1)
                            else:
                                pe.wait_ge(mrow_in, 16 * n + 32)
                                if e == 1:
                                    pe.wait_ge(ql_ready, 4 * g + 8)
                                    pe.wait_ge(kl_ready, 4 * g + 8)
                                scores(0, nxt, t + 1)
                            for p in pieces_at(s):
                                if p == 0 and e == 1:
                                    pe.wait_ge(qh_ready, 4 * g + 6)
                                    pe.wait_ge(kh_ready, 4 * g + 8)
                                max_piece(p, nxt, n + 1)
                            if e == 0 and s < PREP:
                                if s == 0:
                                    pe.wait_ge(w_in[1 - q], 16 * it + 16 + 16 * q)
                                project(s, 1 - q, (it + q) & 3, g + 1)
                            if e == 1 and s in OUT_AT:
                                c = OUT_AT.index(s)
                                if c == 0:
                                    pe.wait_ge(wo_in[1 - q], 16 * it + 16)
                                product(c, 1 - q, g, 4 * g + 2 + c)
                            if s == MROW_AT:
                                pe.wait_ge(g1_read, 4 * g + (4 if e else 1))
                                turn_max(n + 1, 1 - e)
                            outputs(s, q, e, t, 2 * n + STEPS[s][0], g)
            pe.wait_ge(wo_in[1], 16 * ITERS + 16)
            for c in range(2):
                pe.wait_ge(g1_read, 4 * PAIRS * B + 1 + c)
                if c == 0:
                    pe.wait_ge(ot_ready, 2 * PAIRS * B + 3)
                pe.matmul(g1[:, :], wo[1][:, :], ot[:, CH * c:CH * c + CH], start=True, stop=True).then_inc(g1_ready, 1)

        @block.scalar
        def _(act):
            def project(n, p, before):
                what, e, c = PROJ[n]
                x = slice(CH * c, CH * c + CH)
                act.wait_ge(g0_ready, PREP * before + n + 1)
                if what == "k":
                    for h in range(2):
                        act.activation(kh[2 * p + h][0:DH, x], g0[DH * h:DH * h + DH, :], ACT.Copy, scale=QKV_C)\
                           .then_inc(kh_ready, 1)
                elif what == "v":
                    act.activation(vt[:, x], g0[:, :], ACT.Copy, scale=QKV_C).then_inc(g0_by_act, 1)
                elif what == "vt":
                    act.activation(v1[p][:, 4 * c:4 * c + 4, 0:3:2, :],
                                   g0[:, :].rearrange("p (t h d) -> p t h d", t=4, h=2), ACT.Copy).then_inc(g0_by_act, 1)

            def q_high(r, p, before):
                x = slice(CH * (r % 2), CH * (r % 2) + CH)
                act.wait_ge(qsum_ready, 4 * before + r + 1)
                act.activation(qh[2 * p + r // 2][0:96, x], qf[0:96, r % 2, :], ACT.Copy).then_inc(qh_ready, 1)

            def exp(s, t):
                c, j = STEPS[s]
                w = CH - _half(c, j)
                act.wait_ge(st_ready, t + 1)
                act.wait_ge(pv_done, t + 1)
                act.activation(pt[:, s % 3, 0:w], st[s % 2][:, 0:w], ACT.Exp).then_inc(pt_ready, 1)

            act.wait_ge(ready, 3)
            for n in range(PREP):
                if PROJ[n][0] != "q":
                    project(n, 0, 0)
                if n in (1, 5):
                    q_high(n // 4 * 2, 0, 0)
                    q_high(n // 4 * 2 + 1, 0, 0)
            exp(0, 0)
            with act.Fori(0, ITERS) as it:
                for q in range(2):
                    g = 2 * it + q
                    for e in range(2):
                        n = 2 * g + e
                        for s in range(NS):
                            exp((s + 1) % NS, NS * n + s + 1)
                            if e == 0:
                                if s < PREP and PROJ[s][0] != "q":
                                    project(s, 1 - q, g + 1)
                                late = s - QH_LATE
                                if 0 <= late < PREP and PROJ[late][0] == "q":
                                    q_high(PROJ[late][1] * 2 + PROJ[late][2], 1 - q, g + 1)

        @block.vector
        def _(dve):
            def project(n, p, u, before, first=False):
                what, e, c = PROJ[n]
                x = slice(CH * c, CH * c + CH)
                if what == "q":
                    r = 2 * e + c
                    dve.wait_ge(g0_ready, PREP * before + n + 1)
                    if not first or r >= 2:
                        dve.wait_ge(ql_ready, 4 * before + r - 1)
                        dve.wait_ge(qh_ready, 4 * before + r - 1)
                    h = bass.ds(4 * u + 2 * p + e, 1)
                    lo = slice(DH + FREQS, P)
                    dve.scalar_tensor_tensor(out=qt[DH:DH + FREQS, r % 2, :], in0=g0[lo, :], scalar=m.bias[lo, h],
                                             in1=qa[lo, x], op0=ALU.add, op1=ALU.mult).then_inc(qt_ready, 1)
                    dve.scalar_tensor_tensor(out=qf[0:96, r % 2, :], in0=g0[0:96, :], scalar=m.bias[0:96, h],
                                             in1=qa[0:96, x], op0=ALU.add, op1=ALU.mult).then_inc(g0_by_dve, 1)
                elif what == "k":
                    for h in range(2):
                        dve.wait_ge(kh_ready, 4 * before + 2 * c + h + 1)
                        ins = dve.scalar_tensor_tensor(
                            out=kl[2 * p + h][0:DH, x], in0=g0[DH * h:DH * h + DH, :], scalar=QKV_C,
                            in1=kh[2 * p + h][0:DH, x].bitcast(F32), op0=ALU.mult, op1=ALU.subtract)
                        ins.then_inc(kl_ready, 1)

            def max_piece(p, n, par):
                dve.wait_ge(sm_ready, NPC * n + p + 1)
                dve.tensor_reduce(mxp[:, par, p:p + 1], sm[p % 2][:, 0:PIECES[p][2]], AX.X, ALU.max).then_inc(mx_done, 1)

            def join_max(n, par):
                dve.wait_ge(mx_done, NPC * (n + 1))
                dve.tensor_tensor(mxp[:, par, 4:8], mxp[:, par, 4:8], mxp[:, par, 8:12], ALU.max).then_inc(mx_ready, 1)

            def max_rows(n, par, use):
                dve.wait_ge(g1_ready, use + 1)
                dve.tensor_scalar(mrow[:, par, :], g1[0:TILES, 0:P], -1.0, None, ALU.mult).then_inc(g1_read, 1)

            def chunk_out(n, e, c):
                dve.wait_ge(pv_done, NS * n + (4 if c == 0 else NS) + 3)
                dve.wait_ge(ot_ready, n + 2)
                dve.tensor_copy(ou[e][:, CH * c:CH * c + CH], po[c][:, :]).then_inc(ou_ready, 1)

            def reciprocal(n, e):
                dve.wait_ge(den_in, 16 * n + 32)
                dve.reciprocal(rcp[:, e, :], den[:, e, :]).then_inc(rcp_ready, 1)

            def accumulate(c, b, use):
                dve.wait_ge(g1_ready, use + 1)
                acc = m.ACC[:, bass.ds(S * b + CH * c, CH)]
                dve.scalar_tensor_tensor(out=acc, in0=g1[:, :], scalar=OUT_C, in1=acc, op0=ALU.mult, op1=ALU.add)\
                   .then_inc(g1_read, 1)

            dve.wait_ge(tables_in, 32)
            T = slice(DH, DH + FREQS)
            for h in range(SLOT):
                dve.tensor_copy(kh[h][T, :], tk32[T, :]).then_inc(ready_t, 1)
            dve.wait_ge(ready_t, SLOT)
            for h in range(SLOT):
                dve.tensor_tensor(kl[h][T, :], tk32[T, :], kh[h][T, :].bitcast(F32), ALU.subtract)
                dve.memset(kh[h][96:97, :].bitcast(F32), 1.0)
            for p in range(2):
                dve.memset(v1[p][:, :, 1, :], 1.0)
            dve.memset(m.ACC[:, :], 0.0)
            dve.memset(den[:, 1, :], 1.0).then_inc(ready, 1)
            dve.memset(ou[1][:, :], 0.0).then_inc(ready, 1)
            for n in range(BY_DVE):
                project(n, 0, 0, 0, first=True)
            for p in range(NPC):
                max_piece(p, 0, 0)
            join_max(0, 0)
            max_rows(0, 0, 0)
            with dve.Fori(0, ITERS) as it:
                for q in range(2):
                    g = 2 * it + q
                    u = ((it + q) >> 2) & 3
                    for e in range(2):
                        n = 2 * g + e
                        for s in range(NS):
                            for p in pieces_at(s):
                                max_piece(p, n + 1, 1 - e)
                                if p == NPC - 1:
                                    join_max(n + 1, 1 - e)
                            if e == 0 and s < BY_DVE:
                                project(s, 1 - q, u, g + 1)
                            if e == 1 and s in OUT_AT:
                                c = OUT_AT.index(s)
                                accumulate(c, (it + 3 + q) & 3, 4 * g + 2 + c)
                            if s == MROW_AT:
                                max_rows(n + 1, 1 - e, 4 * g + (4 if e else 1))
                            if s == RCP_AT:
                                reciprocal(n - 1, 1 - e)
                            c, j = STEPS[s]
                            if j == 4 * c + 3:
                                chunk_out(n, e, c)
            last = 2 * PAIRS * B - 1
            reciprocal(last, 1)
            for c in range(2):
                accumulate(c, 3, 4 * PAIRS * B + 1 + c)

        @block.gpsimd
        def _(pool):
            def q_low(r, p, before, first=False):
                x = slice(CH * (r % 2), CH * (r % 2) + CH)
                T = slice(DH, DH + FREQS)
                if r > 0 or not first:
                    pool.wait_ge(ql_ready, 4 * before + r)
                pool.wait_ge(g0_by_dve, 4 * before + r + 1)
                pool.wait_ge(qt_ready, 4 * before + r + 1)
                pool.tensor_tensor(qf[T, r % 2, :], qf[T, r % 2, :], qt[T, r % 2, :], ALU.add).then_inc(qsum_ready, 1)
                pool.wait_ge(qh_ready, 4 * before + r + 1)
                h = 2 * p + r // 2
                pool.tensor_tensor(ql[h][0:96, x], qf[0:96, r % 2, :], qh[h][0:96, x].bitcast(F32), ALU.subtract)\
                    .then_inc(ql_ready, 1)

            def normalise(n, e):
                rows = slice(64 * e, 64 * e + 64)
                pool.wait_ge(rb_in, 16 * n + 32)
                pool.tensor_tensor(ot[rows, :], ou[e][rows, :], rb[rows, :], ALU.mult).then_inc(ot_ready, 1)

            pool.memset(ot[:, :], 0.0)
            pool.sem_inc(pt_ready, 1)
            pool.sem_inc(pv_done, 3)
            pool.sem_inc(ou_ready, 2)
            pool.sem_inc(ot_ready, 2)
            pool.sem_inc(den_in, 16)
            pool.sem_inc(rb_in, 16)
            pool.memset(rb[:, :], 0.0).then_inc(ready, 1)
            pool.wait_ge(ready, 3)
            for r in range(4):
                q_low(r, 0, 0, first=True)
            with pool.Fori(0, ITERS) as it:
                for q in range(2):
                    g = 2 * it + q
                    for e in range(2):
                        n = 2 * g + e
                        if e == 0:
                            pool.wait_ge(ot_ready, n + 2)
                            for r in range(4):
                                q_low(r, 1 - q, g + 1)
                            pool.wait_ge(ql_ready, 4 * g + 8)
                        else:
                            pool.wait_ge(g1_ready, 4 * g + 4)
                        pool.wait_ge(ot_ready, n + 2)
                        normalise(n - 1, 1 - e)
            pool.wait_ge(ot_ready, 2 * PAIRS * B + 2)
            normalise(2 * PAIRS * B - 1, 1)


def add_residual_in(nc, m):
    with ExitStack() as ctx:
        gated = ctx.enter_context(semaphores(nc))("gated")
        block = ctx.enter_context(nc.Block())

        @block.vector
        def _(dve):
            for b in range(B):
                x = slice(S * b, S * b + S)
                dve.tensor_scalar(m.ACC[:, x], m.ACC[:, x], m.vecs[:, 0:1], m.mod[:, 2, b:b + 1], ALU.add, ALU.mult)\
                   .then_inc(gated, 1)
                dve.wait_ge(gated, b + 1)
                dve.tensor_tensor(m.X[:, x], m.X[:, x], m.ACC[:, x], ALU.add)


def add_local_attention(nc, m, i, layer):
    NT, X = B * TILES, 4
    NIT = NT // X
    KW = 192
    GH = 4
    with ExitStack() as ctx:
        sb = lambda n, s, d=F32: ctx.enter_context(nc.sbuf_tensor(f"{n}_l{layer}", s, d))
        ps = lambda n, s=(P, CH): ctx.enter_context(nc.psum_tensor(f"{n}_l{layer}", list(s), F32))
        sem = ctx.enter_context(semaphores(nc, f"_l{layer}"))
        w32 = sb("w32", [P, 3 * CH])
        wh = sb("wh", [P, 3 * CH], F32R)
        wl = sb("wl", [P, 3 * CH], F32R)
        wo = sb("lwo", [P, LH // 2, P])
        tab = sb("tab", [P, TILES, 2, 2, LD])
        scl = sb("scl", [P, 2, 2, LD])
        zt = sb("zt", [P, 2, 2, P], F32R)
        t1 = sb("t1", [P, 2, CH])
        t2 = sb("t2", [P, 2, CH])
        sq = sb("sq", [P, 2, CH])
        ss = sb("ss", [P, 2 * LH])
        nhalf = sb("nhalf", [P, 2 * LH])
        r = sb("r", [P, 2, 2 * LH])
        qT = sb("qT", [P, LH // 2, P])
        kT = sb("kT", [P, 2, LH // 2, KW])
        v = sb("v", [P, 4, CH])
        pb = sb("pb", [P, 2, GH, 2 * P])
        mx = sb("mx", [P, 2, GH])
        nm = sb("nm", [P, 2, GH])
        sums = sb("sums", [P, 2, GH])
        rs = sb("rs", [P, 2, GH])
        pT = sb("pT", [P, 2, CH])
        oT = sb("oT", [P, LH // 2, P])
        qk_ps = ps("qk_ps", (P, 2, CH))
        s_ps = ps("s_ps", (P, 2, CH))
        v_ps, ta_ps, tb_ps, o_ps = ps("v_ps"), ps("ta_ps"), ps("tb_ps"), ps("o_ps")

        loaded, tabs, w_split, ready = sem("loaded"), sem("tabs"), sem("w_split"), sem("lready")
        zt_hi, zt_ready = sem("zt_hi"), sem("zt_ready")
        qk_ready, qk_read, sq_ready, ss_ready, r_ready = (
            sem("qk_ready"), sem("qk_read"), sem("sq_ready"), sem("ss_ready"), sem("r_ready"))
        turned, rot_ready = sem("turned"), sem("rot_ready")
        v_ready, v_read = sem("v_ready"), sem("v_read")
        ta_ready, ta_read, tb_ready, tb_read, kT_ready, halo = (
            sem("ta_ready"), sem("ta_read"), sem("tb_ready"), sem("tb_read"), sem("kT_ready"), sem("halo"))
        s_ready, mx_done, nm_ready, exp_done, rs_ready, pn_ready = (
            sem("s_ready"), sem("lmx_done"), sem("nm_ready"), sem("exp_done"), sem("rs_ready"), sem("pn_ready"))
        o_ready, oT_ready, wo_ready, z_done = sem("o_ready"), sem("oT_ready"), sem("wo_ready"), sem("z_done")
        block = ctx.enter_context(nc.Block())

        def zoff(it, x):
            k = x // X
            turn = (it + (NIT + k)) & (NIT - 1) if k else it
            return (turn >> 1) * ZW + (turn & 1) * (X * P) + P * (x % X)

        def tile_in_batch(it, x):
            k = x // X
            turn = (it + (NIT + k)) & (NIT - 1) if k else it
            return (turn & 1) * X + x % X

        @block.sync
        def _(sp):
            sp.dma_start(w32[:, :], i["wqkv"][layer]).then_inc(loaded, 16)
            sp.dma_start(wo[:, :, :], i["lwo"][layer].rearrange("(q p) d -> p q d", p=P)).then_inc(loaded, 16)
            sp.dma_start(tab[:, :, :, :, :], i["rot"]).then_inc(loaded, 16)
            sp.dma_start(scl[:, :, :, :].rearrange("p a b d -> p (a b d)"),
                         i["qkscale"][layer:layer + 1].broadcast_to([P, 4 * LD])).then_inc(loaded, 16)

        @block.tensor
        def _(pe):
            def project(slot_ring):
                zh, zl = zt[:, slot_ring, 0, :], zt[:, slot_ring, 1, :]
                for n in range(3):
                    if n == 2:
                        yield
                    w = slice(CH * n, CH * n + CH)
                    out = qk_ps[:, n, :] if n < 2 else v_ps[:, :]
                    pe.matmul(out, zh, wh[:, w], start=True, stop=False)
                    pe.matmul(out, zh, wl[:, w], start=False, stop=False)
                    mm = pe.matmul(out, zl, wh[:, w], start=False, stop=True)
                    if n:
                        mm.then_inc(qk_ready if n == 1 else v_ready, 1)
                yield

            def scores(g, ring, mask):
                for e in range(2):
                    pe.matmul(s_ps[:, e, 0:2 * KW], m.identb[:, :], mask, start=True, stop=True)
                    for s in range(2):
                        rows = slice(LD * e, LD * e + LD)
                        mm = pe.matmul(s_ps[:, e, KW * s:KW * s + KW], qT[rows, 2 * g + s, :], kT[rows, ring, 2 * g + s, :],
                                       start=False, stop=True, skip_group_check=True)
                mm.then_inc(s_ready, 1)

            def turn_probs(g, s):
                bank, sm_ = (ta_ps, ta_ready) if s == 0 else (tb_ps, tb_ready)
                for e in range(2):
                    for a in range(2):
                        mm = pe.transpose(bank[:, P * (2 * e + a):P * (2 * e + a) + P],
                                          pb[:, g, 2 * s + e, P * a:P * a + P], m.ident[:, :])
                mm.then_inc(sm_, 1)

            def outputs(g, s, cur, prev):
                for e in range(2):
                    h = GH * g + 2 * s + e
                    d = slice(LD * h, LD * h + LD)
                    out = o_ps[LD * e:LD * e + LD, P * (2 * g + s):P * (2 * g + s) + P]
                    pe.matmul(out, v[:, prev, d], pT[:, s, 2 * P * e:2 * P * e + P], start=True, stop=False)
                    mm = pe.matmul(out, v[:, cur, d], pT[:, s, 2 * P * e + P:2 * P * e + 2 * P], start=False, stop=True)
                return mm

            def turn_qk():
                for n, (bank, sm_) in enumerate(((ta_ps, ta_ready), (tb_ps, tb_ready))):
                    for q in range(4):
                        mm = pe.transpose(bank[:, P * q:P * q + P], t1[:, n, P * q:P * q + P], m.ident[:, :])
                    mm.then_inc(sm_, 1)

            def finish(t, cur, prev):
                pe.wait_ge(pn_ready, 2 * t + 1)
                pe.wait_ge(ta_read, 3 * t + 1)
                turn_probs(1, 0)
                pe.wait_ge(kT_ready, t + 1)
                turn_probs(1, 1)
                pe.wait_ge(oT_ready, 2 * t + 1)
                pe.wait_ge(ta_read, 3 * t + 2)
                outputs(1, 0, cur, prev)
                pe.wait_ge(tb_read, 2 * t + 1)
                outputs(1, 1, cur, prev).then_inc(o_ready, 1)

            def product(t):
                pe.wait_ge(oT_ready, 2 * t + 2)
                pe.wait_ge(v_read, t + 2)
                for q in range(4):
                    mm = pe.matmul(v_ps[:, 0:P], wo[:, q, :], oT[:, q, :], start=(q == 0), stop=(q == 3))
                mm.then_inc(wo_ready, 1)

            pe.wait_ge(w_split, 2)
            pe.wait_ge(ready, 2)
            pe.wait_ge(zt_ready, 1)
            for _ in project(0):
                pass
            pe.wait_ge(rot_ready, 1)
            turn_qk()
            with pe.Fori(0, NIT) as it:
                for x in range(X):
                    t = it * X + x
                    mask = m.lmask[:, bass.ds(it & 1, 1), :].rearrange("p a w -> p (a w)") if x == 0 else m.lmask[:, 1, :]
                    pe.wait_ge(ta_read, 3 * t + 1)
                    pe.wait_ge(kT_ready, t + 1)
                    pe.wait_ge(halo, t + 1)
                    pe.wait_ge(exp_done, 2 * t + 1)
                    scores(0, x % 2, mask)
                    nxt = project((x + 1) % 2)
                    pe.wait_ge(zt_ready, t + 2)
                    pe.wait_ge(qk_read, t + 1)
                    pe.wait_ge(sq_ready, t + 1)
                    next(nxt)
                    pe.wait_ge(z_done, t + 1)
                    next(nxt)
                    finish(t, (x + 3) % 4, (x + 2) % 4)
                    pe.wait_ge(exp_done, 2 * t + 2)
                    scores(1, x % 2, mask)
                    product(t)
                    pe.wait_ge(pn_ready, 2 * t + 2)
                    pe.wait_ge(ta_read, 3 * t + 2)
                    turn_probs(0, 0)
                    pe.wait_ge(tb_read, 2 * t + 1)
                    turn_probs(0, 1)
                    pe.wait_ge(oT_ready, 2 * t + 2)
                    pe.wait_ge(ta_read, 3 * t + 3)
                    outputs(0, 0, x, (x + 3) % 4)
                    pe.wait_ge(tb_read, 2 * t + 2)
                    outputs(0, 1, x, (x + 3) % 4).then_inc(o_ready, 1)
                    pe.wait_ge(rot_ready, t + 2)
                    turn_qk()
            finish(NT, 3, 2)
            pe.wait_ge(oT_ready, 2 * NT + 2)
            pe.wait_ge(z_done, NT + 1)
            for q in range(4):
                mm = pe.matmul(v_ps[:, 0:P], wo[:, q, :], oT[:, q, :], start=(q == 0), stop=(q == 3))
            mm.then_inc(wo_ready, 1)

        @block.scalar
        def _(act):
            def exps(g, t, ring):
                act.wait_ge(nm_ready, 2 * t + g + 1)
                for e in range(2):
                    for s in range(2):
                        h = GH * g + 2 * s + e
                        ins = act.activation(pb[:, g, 2 * s + e, 64:2 * P], s_ps[:, e, KW * s:KW * s + KW], ACT.Exp,
                                             bias=nm[:, g, 2 * e + s:2 * e + s + 1], scale=r[:, ring, h:h + 1],
                                             accum_out=sums[:, g, 2 * s + e:2 * s + e + 1])
                ins.then_inc(exp_done, 1)

            def from_ta(dst, use):
                act.wait_ge(ta_ready, use)
                act.activation(dst, ta_ps[:, :], ACT.Copy).then_inc(ta_read, 1)

            def out_group(g, count):
                act.wait_ge(o_ready, count)
                act.activation(oT[:, 2 * g:2 * g + 2, :].rearrange("p q t -> p (q t)"),
                               o_ps[:, 2 * P * g:2 * P * g + 2 * P], ACT.Copy).then_inc(oT_ready, 1)

            def project(t1_, slot):
                act.wait_ge(qk_read, t1_)
                act.activation(sq[:, :, :], qk_ps[:, :, :], ACT.Square).then_inc(sq_ready, 1)

            def take_v(t1_, slot):
                act.wait_ge(v_ready, t1_)
                act.activation(v[:, slot, :], v_ps[:, :], ACT.Copy).then_inc(v_read, 1)

            def take_qk(use, t1_, ring):
                from_ta(qT[:, :, :].rearrange("p q t -> p (q t)"), use)
                act.wait_ge(tb_ready, use)
                act.activation(kT[:, ring, :, 64:KW], tb_ps[:, :].rearrange("p (q t) -> p q t", q=4), ACT.Copy)\
                   .then_inc(kT_ready, 1)

            act.wait_ge(ready, 2)
            project(1, 0)
            take_v(1, 0)
            take_qk(1, 1, 0)
            with act.Fori(0, NIT) as it:
                for x in range(X):
                    t = it * X + x
                    exps(0, t, x % 2)
                    act.wait_ge(ss_ready, t + 1)
                    project(t + 2, None)
                    from_ta(pT[:, 0, :], 3 * t + 2)
                    take_v(t + 2, (x + 1) % 4)
                    out_group(1, 2 * t + 1)
                    exps(1, t, x % 2)
                    from_ta(pT[:, 0, :], 3 * t + 3)
                    act.wait_ge(wo_ready, t + 1)
                    out_group(0, 2 * t + 2)
                    take_qk(3 * t + 4, t + 2, (x + 1) % 2)
            from_ta(pT[:, 0, :], 3 * NT + 2)
            out_group(1, 2 * NT + 1)

        @block.vector
        def _(dve):
            def split_tile(off, ring, count):
                z = m.Z[:, bass.ds(off, P)] if not isinstance(off, int) else m.Z[:, off:off + P]
                dve.tensor_copy(zt[:, ring, 0, :], z).then_inc(zt_hi, 1)
                dve.wait_ge(zt_hi, count)
                dve.tensor_tensor(zt[:, ring, 1, :], z, zt[:, ring, 0, :].bitcast(F32), ALU.subtract).then_inc(zt_ready, 1)

            def table(a, T, d):
                w = d.stop - d.start
                if isinstance(T, int):
                    src = tab[:, T:T + 1, a, :, d]
                else:
                    src = tab[:, bass.ds(T, 1), a, :, d]
                return src.rearrange("p o b d -> p (o b) d").unsqueeze(2).broadcast_to([P, 2, LH, w])

            def rotate_a(T, count):
                heads = qk_ps[:, :, :].rearrange("p n (h d) -> p n h d", d=LD)
                a = t1[:, :, :].rearrange("p n (h d) -> p n h d", d=LD)
                dve.wait_ge(qk_ready, count)
                dve.tensor_tensor(a, heads, table(0, T, slice(0, LD)), ALU.mult).then_inc(turned, 1)

            def rotate_b(T, count):
                heads = qk_ps[:, :, :].rearrange("p n (h d) -> p n h d", d=LD)
                b = t2[:, :, :].rearrange("p n (h d) -> p n h d", d=LD)
                lo, hi = slice(0, LD // 2), slice(LD // 2, LD)
                dve.tensor_tensor(b[:, :, :, lo], heads[:, :, :, hi], table(1, T, lo), ALU.mult)
                dve.tensor_tensor(b[:, :, :, hi], heads[:, :, :, lo], table(1, T, hi), ALU.mult).then_inc(qk_read, 1)

            def squares(count):
                dve.wait_ge(sq_ready, count)
                dve.tensor_reduce(ss[:, :], sq[:, :, :].rearrange("p n (h d) -> p (n h) d", d=LD), AX.X, ALU.add)\
                   .then_inc(turned, 1)
                dve.wait_ge(turned, 3 * count - 1)
                dve.tensor_scalar(ss[:, :], ss[:, :], 1e-24, None, ALU.max).then_inc(ss_ready, 1)

            def rotate_c(count):
                dve.wait_ge(qk_read, count)
                dve.tensor_tensor(t1[:, :, :], t1[:, :, :], t2[:, :, :], ALU.add).then_inc(turned, 1)

            def normalise_k(ring, count):
                dve.wait_ge(turned, 3 * count)
                dve.wait_ge(r_ready, count)
                k = t1[:, 1, :].rearrange("p (h d) -> p h d", d=LD)
                dve.tensor_tensor(k, k, r[:, ring, LH:2 * LH].unsqueeze(2).broadcast_to([P, LH, LD]), ALU.mult)\
                   .then_inc(rot_ready, 1)

            def take_halo(ring, count):
                dve.wait_ge(kT_ready, count)
                dve.tensor_copy(kT[:, 1 - ring, :, 0:64], kT[:, ring, :, P:KW]).then_inc(halo, 1)

            def maxima(g, t, ring):
                dve.wait_ge(s_ready, 2 * t + g + 1)
                dve.tensor_reduce(mx[:, g, :].rearrange("p (e s) -> p e s", e=2),
                                  s_ps[:, :, 0:2 * KW].rearrange("p e (s w) -> p e s w", s=2), AX.X, ALU.max).then_inc(mx_done, 1)
                dve.wait_ge(mx_done, 2 * t + g + 1)
                rq = r[:, ring, GH * g:GH * g + GH].rearrange("p (s e) -> p e s", e=2)
                dve.scalar_tensor_tensor(out=nm[:, g, :].rearrange("p (e s) -> p e s", e=2),
                                         in0=mx[:, g, :].rearrange("p (e s) -> p e s", e=2), scalar=-1.0, in1=rq,
                                         op0=ALU.mult, op1=ALU.mult).then_inc(nm_ready, 1)

            def reciprocal(g, count):
                dve.wait_ge(exp_done, count)
                dve.reciprocal(rs[:, g, :], sums[:, g, :]).then_inc(rs_ready, 1)

            def from_tb(use):
                dve.wait_ge(tb_ready, use)
                dve.tensor_copy(pT[:, 1, :], tb_ps[:, :]).then_inc(tb_read, 1)

            def add_to_z(off, t):
                dve.wait_ge(wo_ready, t + 1)
                for rows, o in ((slice(0, 64), 0), (slice(64, P), 1)):
                    z = m.Z[rows, bass.ds(off + o, P)] if not isinstance(off, int) else m.Z[rows, off + o:off + o + P]
                    ins = dve.tensor_tensor(z, z, v_ps[rows, 0:P], ALU.add)
                ins.then_inc(z_done, 1)

            dve.wait_ge(loaded, 64)
            dve.tensor_copy(wh[:, :], w32[:, :]).then_inc(w_split, 1)
            dve.wait_ge(w_split, 1)
            dve.tensor_tensor(wl[:, :], w32[:, :], wh[:, :].bitcast(F32), ALU.subtract).then_inc(w_split, 1)
            dve.memset(pb[:, :, :, 0:P], 0.0)
            dve.memset(pb[:, :, :, P:2 * P], 0.0)
            dve.memset(oT[:, :, :], 0.0)
            dve.memset(v[:, 2:4, :], 0.0)
            dve.memset(kT[:, 0, :, 0:64], 0.0)
            dve.memset(sums[:, 1, :], 1.0)
            for a in range(2):
                tt = tab[:, :, a, :, :]
                dve.tensor_tensor(tt, tt, scl[:, a, :, :].unsqueeze(1).broadcast_to([P, TILES, 2, LD]), ALU.mult)\
                   .then_inc(tabs, 1)
            dve.memset(nhalf[:, :], -0.5).then_inc(ready, 1)
            split_tile(0, 0, 1)
            split_tile(P, 1, 2)
            dve.wait_ge(tabs, 2)
            rotate_a(0, 1)
            rotate_b(0, 1)
            squares(1)
            rotate_c(1)
            normalise_k(0, 1)
            take_halo(0, 1)
            with dve.Fori(0, NIT) as it:
                for x in range(X):
                    t = it * X + x
                    reciprocal(1, 2 * t + 1)
                    maxima(0, t, x % 2)
                    T = tile_in_batch(it, x + 1)
                    dve.wait_ge(ta_ready, 3 * t + 1)
                    rotate_a(T, t + 2)
                    from_tb(3 * t + 2)
                    rotate_b(T, t + 2)
                    dve.wait_ge(r_ready, t + 1)
                    squares(t + 2)
                    reciprocal(0, 2 * t + 2)
                    rotate_c(t + 2)
                    maxima(1, t, x % 2)
                    add_to_z(zoff(it, x - 1), t)
                    from_tb(3 * t + 3)
                    split_tile(zoff(it, x + 2), x % 2, t + 3)
                    normalise_k((x + 1) % 2, t + 2)
                    take_halo((x + 1) % 2, t + 2)
            reciprocal(1, 2 * NT + 1)
            from_tb(3 * NT + 2)
            add_to_z((B - 1) * ZW + (TILES - 1) * P, NT)

        @block.gpsimd
        def _(pool):
            def norms(ring, count):
                pool.wait_ge(ss_ready, count)
                pool.tensor_tensor(r[:, ring, :], ss[:, :], nhalf[:, :], ALU.pow).then_inc(r_ready, 1)

            def normalise(g, count):
                pool.wait_ge(rs_ready, count)
                p = pb[:, g, :, 64:2 * P]
                pool.tensor_tensor(p, p, rs[:, g, :].unsqueeze(2).broadcast_to([P, GH, KW]), ALU.mult).then_inc(pn_ready, 1)

            pool.sem_inc(exp_done, 1)
            pool.sem_inc(oT_ready, 1)
            pool.sem_inc(z_done, 1)
            pool.sem_inc(ready, 1)
            pool.wait_ge(ready, 2)
            norms(0, 1)
            with pool.Fori(0, NIT) as it:
                for x in range(X):
                    t = it * X + x
                    pool.wait_ge(r_ready, t + 1)
                    normalise(1, 2 * t + 1)
                    pool.wait_ge(pn_ready, 2 * t + 1)
                    norms((x + 1) % 2, t + 2)
                    pool.wait_ge(r_ready, t + 2)
                    normalise(0, 2 * t + 2)
                    pool.wait_ge(pn_ready, 2 * t + 2)
            normalise(1, 2 * NT + 1)


def add_mlp(nc, m, i, layer):
    with ExitStack() as ctx:
        sb = lambda n, s, d=F32: ctx.enter_context(nc.sbuf_tensor(f"{n}_m{layer}", s, d))
        ps = lambda n: ctx.enter_context(nc.psum_tensor(f"{n}_m{layer}", [P, CH], F32))
        sem = ctx.enter_context(semaphores(nc, f"_m{layer}"))
        w32 = sb("mw32", [P, 2 * HID])
        wh = sb("mwh", [P, 2 * HID], F32R)
        wl = sb("mwl", [P, 2 * HID], F32R)
        w2 = sb("w2", [P, NHID, D])
        gl = sb("gl", [P, NHID, CH])
        u = sb("u", [P, 2, NHID, CH])
        bank = [ps(f"b{k}") for k in range(2 * NHID)]
        y_ps = [ps(f"y{k}") for k in range(2)]
        loaded, w_split = sem("mloaded"), sem("mw_split")
        g_ready, a_ready, gelu_done, u_ready, y_ready, z_done = (
            sem("g_ready"), sem("a_ready"), sem("gelu_done"), sem("u_ready"), sem("y_ready"), sem("mz_done"))
        ms = [min(P, HID - P * j) for j in range(NHID)]
        block = ctx.enter_context(nc.Block())

        @block.sync
        def _(sp):
            sp.dma_start(w32[:, :], i["w1"][layer]).then_inc(loaded, 16)
            full = HID // P
            sp.dma_start(w2[:, 0:full, :], i["w2"][layer, 0:P * full].rearrange("(q p) d -> p q d", p=P)).then_inc(loaded, 16)
            sp.dma_start(w2[0:ms[-1], full, :], i["w2"][layer, P * full:HID]).then_inc(loaded, 16)

        @block.tensor
        def _(pe):
            def hidden(n, half, b, first):
                xh = m.HH[:, bass.ds(2 * b + half, 1), :].rearrange("p a w -> p (a w)")
                xl = m.HL[:, bass.ds(2 * b + half, 1), :].rearrange("p a w -> p (a w)")
                for j in range(NHID):
                    for k, sm_ in ((1, g_ready), (0, a_ready)):
                        w = slice(HID * k + P * j, HID * k + P * j + ms[j])
                        out = bank[2 * j + k][0:ms[j], :]
                        if not first:
                            pe.wait_ge(u_ready, NHID * n + j + 1 - NHID)
                        pe.matmul(out, wh[:, w], xh, start=True, stop=False)
                        pe.matmul(out, wh[:, w], xl, start=False, stop=False)
                        pe.matmul(out, wl[:, w], xh, start=False, stop=True).then_inc(sm_, 1)

            def down(n, half):
                pe.wait_ge(z_done, 2 * n + 2)
                for j in range(NHID):
                    pe.wait_ge(u_ready, NHID * n + j + 1)
                    mm = pe.matmul(y_ps[half][:, :], w2[0:ms[j], j, :], u[0:ms[j], half, j, :], start=(j == 0), stop=(j == NHID - 1))
                mm.then_inc(y_ready, 1)

            pe.wait_ge(loaded, 48)
            pe.wait_ge(w_split, 2)
            hidden(0, 0, 0, True)
            with pe.Fori(0, B) as b:
                hidden(2 * b + 1, 1, b, False)
                down(2 * b, 0)
                hidden(2 * b + 2, 0, (b + 1) & (B - 1), False)
                down(2 * b + 1, 1)

        @block.scalar
        def _(act):
            def gelus(n, first):
                for j in range(NHID):
                    act.wait_ge(g_ready, NHID * n + j + 1)
                    if not first:
                        act.wait_ge(u_ready, NHID * n + j + 1 - NHID)
                    act.activation(gl[0:ms[j], j, :], bank[2 * j + 1][0:ms[j], :], ACT.Gelu,
                                   bias=m.b1[0:ms[j], layer, 1, j:j + 1]).then_inc(gelu_done, 1)
            gelus(0, True)
            with act.Fori(0, B) as b:
                gelus(2 * b + 1, False)
                gelus(2 * b + 2, False)

        @block.vector
        def _(dve):
            def gate(n, half):
                for j in range(NHID):
                    dve.wait_ge(gelu_done, NHID * n + j + 1)
                    dve.wait_ge(a_ready, NHID * n + j + 1)
                    dve.scalar_tensor_tensor(out=u[0:ms[j], half, j, :], in0=bank[2 * j][0:ms[j], :],
                                             scalar=m.b1[0:ms[j], layer, 0, j:j + 1], in1=gl[0:ms[j], j, :],
                                             op0=ALU.add, op1=ALU.mult).then_inc(u_ready, 1)

            def add_to_z(n, half, b):
                dve.wait_ge(y_ready, n + 1)
                for lo, o in ((0, 0), (64, 1)):
                    z = m.Z[lo:lo + 64, bass.ds(ZW * b + CH * half + o, CH)]
                    dve.scalar_tensor_tensor(out=z, in0=y_ps[half][lo:lo + 64, :], scalar=m.vecs[lo:lo + 64, 3 + 3 * layer:4 + 3 * layer],
                                             in1=z, op0=ALU.add, op1=ALU.add).then_inc(z_done, 1)

            dve.wait_ge(loaded, 48)
            dve.tensor_copy(wh[:, :], w32[:, :]).then_inc(w_split, 1)
            dve.wait_ge(w_split, 1)
            dve.tensor_tensor(wl[:, :], w32[:, :], wh[:, :].bitcast(F32), ALU.subtract).then_inc(w_split, 1)
            dve.sem_inc(z_done, 2)
            gate(0, 0)
            with dve.Fori(0, B) as b:
                gate(2 * b + 1, 1)
                add_to_z(2 * b, 0, b)
                dve.wait_ge(y_ready, 2 * b + 1)
                gate(2 * b + 2, 0)
                add_to_z(2 * b + 1, 1, b)


def add_output(nc, m, out):
    with ExitStack() as ctx:
        sem = ctx.enter_context(semaphores(nc))
        summed, stored = sem("o_summed"), sem("o_stored")
        block = ctx.enter_context(nc.Block())

        @block.vector
        def _(dve):
            for b in range(B):
                for rows, o in ((slice(0, 64), 0), (slice(64, P), 1)):
                    x = m.X[rows, S * b:S * b + S]
                    dve.scalar_tensor_tensor(out=x, in0=m.Z[rows, ZW * b + o:ZW * b + o + S], scalar=m.mod[rows, 5, b:b + 1],
                                             in1=x, op0=ALU.mult, op1=ALU.add).then_inc(summed, 1)

        @block.sync
        def _(sp):
            for b in range(B):
                sp.wait_ge(summed, 2 * b + 2)
                sp.dma_start(out[:, S * b:S * b + S], m.X[:, S * b:S * b + S]).then_inc(stored, 16)
            sp.wait_ge(stored, 16 * B)


def host_constants():
    f = np.float32
    ident = np.eye(P, dtype=f)
    mean = np.full((P, P), 1.0 / D, f)
    N = B * S // CH
    oneh = np.zeros((P, N, N), f)
    sel = np.zeros((N, N, P), f)
    for n in range(N):
        oneh[:, n, n] = 1.0 / D
        sel[n, n, :] = 1.0
    a = np.arange(P)
    nat = np.where(a[None, :] > a[:, None], BIG, 0.0)
    tr = nat.T
    key = np.arange(192)[None, :] - 64
    loc = np.where((key > a[:, None]) | (key < a[:, None] - WIN), BIG, 0.0)
    loc0 = np.where(key < 0, BIG, loc)
    masks = np.concatenate([nat, tr, loc0, loc], 1).astype(f)
    w = 1250.0 ** (-(np.arange(FREQS) // 2 * 2) / FREQS)
    ang = w[:, None] * np.arange(S)[None, :]
    even = (np.arange(FREQS) % 2 == 0)[:, None]
    tk = np.where(even, np.cos(ang), np.sin(ang)).astype(f)
    qa = np.zeros((P, S))
    qa[0:DH] = QKV_C / 8
    qa[DH:DH + FREQS] = QKV_C / 32 * np.sin(ang)
    qa[DH + FREQS:] = QKV_C / 32 * np.where(even, np.cos(ang), -np.cos(ang))
    hidx = np.arange(0, LD, 2, dtype=f)
    inv = (f(1.0) / np.power(f(10000.0), hidx / f(LD))).astype(f)
    tok = np.arange(S, dtype=f)
    fr = tok[:, None] * inv[None, :]
    fr = np.concatenate([fr, fr], 1)
    base = ((hidx + f(0.4 * LD)) / f(1.4 * LD)).astype(f)
    power = ((tok - S // 2) / f(WIN // 2)).astype(f)
    sc = np.power(base[None, :], power[:, None]).astype(f)
    sc = np.concatenate([sc, sc], 1)
    sign = np.where(np.arange(LD) < LD // 2, -1.0, 1.0).astype(f)
    cos, sin = np.cos(fr), np.sin(fr) * sign
    rot = np.stack([np.stack([cos * sc * 8, cos / sc]), np.stack([sin * sc * 8, sin / sc])])
    rot = rot.reshape(2, 2, TILES, P, LD).transpose(3, 2, 0, 1, 4).astype(f)
    return {"rot": rot, "ident": ident, "mean": mean, "oneh": oneh, "sel": sel, "masks": masks, "tk": tk, "qa": qa.astype(f)}


def build(nc, i, scratch, dinv, out):
    with ExitStack() as ctx:
        sb = lambda n, s, d=F32: ctx.enter_context(nc.sbuf_tensor(n, s, d))
        m = Mem()
        m.X = sb("X", [P, B * S])
        m.ident = sb("ident", [P, P])
        m.identb = sb("identb", [P, P], BF16)
        m.masks = sb("masks", [P, 2 * P + 2 * 192], BF16)
        m.mean = sb("mean", [P, P])
        m.oneh = sb("oneh", [P, 8, 8])
        m.sel = sb("sel", [8, 8, P])
        m.bias = sb("bias", [P, H])
        m.mod = sb("mod", [P, 6, B])
        m.vecs = sb("vecs", [P, 8])
        m.b1 = sb("b1", [P, DEPTH, 2, NHID])
        m.eps = m.vecs[:, 7:8]
        m.lmask = sb("lmask", [P, 2, 2 * 192], BF16)
        add_mod_and_weights(nc, m, i, scratch)
        with ExitStack() as att:
            m.HH = att.enter_context(nc.sbuf_tensor("HH", [P, 8, CH], F32R))
            m.HL = att.enter_context(nc.sbuf_tensor("HL", [P, 8, CH], F32R))
            add_layernorm(nc, m, "ln1", lambda n: m.X[:, CH * n:CH * n + CH],
                          lambda n: m.mod[:, 1, n // 2:n // 2 + 1], lambda n: m.mod[:, 0, n // 2:n // 2 + 1], "split")
            m.ACC = att.enter_context(nc.sbuf_tensor("ACC", [P, B * S], F32))
            add_attention(nc, m, i, scratch, dinv)
            add_residual_in(nc, m)
        with ExitStack() as ffn:
            m.Z = ffn.enter_context(nc.sbuf_tensor("Z", [P, (B + 1) * ZW], F32))
            m.Z3 = m.Z[:, 0:B * ZW].rearrange("p (b w) -> p b w", b=B)
            one = lambda k: (lambda n: m.vecs[:, k:k + 1])
            add_layernorm(nc, m, "ln2", lambda n: m.X[:, CH * n:CH * n + CH],
                          lambda n: m.mod[:, 4, n // 2:n // 2 + 1], lambda n: m.mod[:, 3, n // 2:n // 2 + 1], "Z")
            for layer in range(DEPTH):
                add_local_attention(nc, m, i, layer)
                with ExitStack() as mlp:
                    m.HH = mlp.enter_context(nc.sbuf_tensor(f"HH{layer}", [P, 8, CH], F32R))
                    m.HL = mlp.enter_context(nc.sbuf_tensor(f"HL{layer}", [P, 8, CH], F32R))
                    add_layernorm(nc, m, f"ln3{layer}",
                                  lambda n: m.Z[:, ZW * (n // 2) + CH * (n % 2):ZW * (n // 2) + CH * (n % 2) + CH],
                                  one(1 + 3 * layer), one(2 + 3 * layer), "split")
                    add_mlp(nc, m, i, layer)
            add_output(nc, m, out)


def kernel(**inputs):
    import numpy as _np
    import concourse.bacc as _bacc
    from concourse import mybir as _mybir
    from concourse.bass_utils import run_bass_kernel_spmd as _run

    v = {k.replace("L0_", ""): _np.asarray(a) for k, a in inputs.items()}
    f = _np.float32
    qkv, pos = v["attn_qkv"], v["attn_positional"]
    swap = _np.arange(FREQS) ^ 1
    posT = _np.concatenate([pos.transpose(2, 1, 0), pos[swap].transpose(2, 1, 0)], 2)
    vecs = _np.zeros((P, 8), f)
    vecs[:, 0] = v["attn_out_bias"]
    for l in range(DEPTH):
        vecs[:, 1 + 3 * l] = v["ffn_ln_g"][l]
        vecs[:, 2 + 3 * l] = v["ffn_ln_b"][l]
        vecs[:, 3 + 3 * l] = v["ffn_b2"][l]
    vecs[:, 7] = 1e-5
    b1 = _np.zeros((DEPTH, 2, NHID * P), f)
    b1[:, :, :HID] = v["ffn_b1"].reshape(DEPTH, 2, HID)
    half = (_np.arange(LD) + LD // 2) % LD
    qs = _np.stack([v["ffn_q_scale"], v["ffn_k_scale"]], 1)
    qks = _np.stack([qs, qs[:, :, half]], 1).reshape(DEPTH, 4 * LD)
    data = {
        "xT": v["attn_input"].transpose(2, 0, 1).reshape(D, B * S),
        "qkv": qkv, "wqT": qkv[:, 0].transpose(2, 1, 0), "posT": posT, "biasT": v["attn_q_bias"].T,
        "cT": v["c"].T, "wmod": v["wmod"], "vecs": vecs,
        "b1": b1.reshape(DEPTH, 2, NHID, P).transpose(3, 0, 1, 2),
        "wo": v["attn_out_kernel"], "wqkv": v["ffn_wqkv"], "lwo": v["ffn_wo"], "w1": v["ffn_w1"], "w2": v["ffn_w2"],
        "qkscale": qks,
    } | host_constants()
    nc = _bacc.Bacc("TRN2", target_bir_lowering=False, num_devices=1)
    arrays, aps = {}, {}
    for name, a in data.items():
        a = _np.ascontiguousarray(a)
        arrays[f"in_{name}_dram"] = a
        aps[name] = nc.dram_tensor(f"in_{name}_dram", a.shape, _mybir.dt.from_np(a.dtype), kind="ExternalInput").ap()
    scratch = nc.dram_tensor("split_weights", (PAIRS, P, 2 * 4 * P), F32, kind="Internal").ap()
    dinv = nc.dram_tensor("denominators", (2, S), F32, kind="Internal").ap()
    out = nc.dram_tensor("out_0_dram", (P, B * S), F32, kind="ExternalOutput").ap()
    build(nc, aps, scratch, dinv, out)
    r = _run(nc, [arrays], core_ids=[0])
    got = r.results[0]["out_0_dram"]
    return _np.ascontiguousarray(got.reshape(D, B, S).transpose(1, 2, 0))
```

```python
import numpy as np
import concourse.bass as bass
from concourse import mybir
from contextlib import ExitStack, contextmanager

F32 = mybir.dt.float32
F32R = mybir.dt.float32r
BF16 = mybir.dt.bfloat16
ALU = mybir.AluOpType
ACT = mybir.ActivationFunctionType
AX = mybir.AxisListType

P = 128
B, S, D = 4, 1024, 128
H, DH, FREQS = 16, 64, 32
PAIRS = H // 2
TILES = S // P
CH = 512
DEPTH = 2
LH, LD = 8, 64
WIN = 64
HID = int(D * 4 * 2 / 3)
NHID = -(-HID // P)
BIG = -1e30
QKV_C = (3.0 * D * DH * H) ** -0.25
OUT_C = (H * DH * D) ** -0.25
ZW = S + 4

STEPS = [(c, j) for c in range(S // CH) for j in range(4 * (c + 1))]
PIECES = [(i, 0, min(P * (i + 1), CH)) for i in range(TILES)] + [(i, CH, P * (i + 1) - CH) for i in range(4, TILES)]
NS, NPC = len(STEPS), len(PIECES)


def _half(c, j):
    return max(0, P * j - CH * c)


@contextmanager
def semaphores(nc, suffix=""):
    held = []

    def sem(name):
        held.append(nc.alloc_semaphore(name=name + suffix))
        return held[-1]
    yield sem
    nc.clear_and_free_semaphores(held)
    nc.all_engine_barrier()


class Mem:
    pass


def add_mod_and_weights(nc, m, i, scratch):
    with ExitStack() as ctx:
        sb = lambda n, s, d=F32: ctx.enter_context(nc.sbuf_tensor(n, s, d))
        ps = lambda n, s: ctx.enter_context(nc.psum_tensor(n, s, F32))
        sem = ctx.enter_context(semaphores(nc))
        w3 = sb("w3", [P, 3, H * DH])
        wqT = sb("wqT", [DH, H, P])
        posT = sb("posT", [DH, H, 2 * FREQS])
        biasT = sb("biasT", [P, H])
        cT = sb("cT", [P, B])
        sT = sb("sT", [P, B])
        wmod = sb("wmod", [P, 6 * D])
        wc = sb("wc", [P, PAIRS, 4, P])
        whl = sb("whl", [P, PAIRS, 2, 4 * P], F32R)
        sg = sb("sg", [P, 2, B])
        ab = sb("ab", [P, 2, B])
        masks = sb("masks32", [P, 2 * P + 2 * 192])
        comp = [ps(f"comp{k}", [P, CH]) for k in range(2)]
        modp = ps("modp", [P, CH])
        biasp = ps("biasp", [P, CH])
        loaded, consts, weights_out = sem("loaded"), sem("consts_in"), sem("weights_out")
        silu_done, mod_ready, comp_ready, pos_bias = sem("silu_done"), sem("mod_ready"), sem("comp_ready"), sem("pos_bias")
        chain, wc_ready, lo_ready = sem("chain"), sem("wc_ready"), sem("lo_ready")
        block = ctx.enter_context(nc.Block())
        NC = 8

        @block.sync
        def _(sp):
            sp.dma_start(w3[:, :, :], i["qkv"].rearrange("x a n h -> x a (n h)")).then_inc(loaded, 16)
            sp.dma_start(wqT[:, :, :], i["wqT"]).then_inc(loaded, 16)
            sp.dma_start(posT[:, :, :], i["posT"]).then_inc(loaded, 16)
            sp.dma_start(biasT[0:DH, :], i["biasT"]).then_inc(loaded, 16)
            sp.dma_start(cT[:, :], i["cT"]).then_inc(loaded, 16)
            sp.dma_start(wmod[:, :], i["wmod"]).then_inc(loaded, 16)
            sp.dma_start(m.ident[:, :], i["ident"]).then_inc(consts, 16)
            sp.dma_start(m.mean[:, :], i["mean"]).then_inc(consts, 16)
            sp.dma_start(m.oneh[:, :, :], i["oneh"]).then_inc(consts, 16)
            sp.dma_start(m.sel[:, :, :], i["sel"]).then_inc(consts, 16)
            sp.dma_start(masks[:, :], i["masks"]).then_inc(consts, 16)
            sp.dma_start(m.vecs[:, :], i["vecs"]).then_inc(consts, 16)
            sp.dma_start(m.b1[:, :, :, :], i["b1"]).then_inc(consts, 16)
            sp.dma_start(m.X[:, :], i["xT"]).then_inc(consts, 16)
            sp.wait_ge(consts, 16 * NC)
            sp.wait_ge(wc_ready, 5)
            sp.wait_ge(lo_ready, 1)
            sp.dma_start(scratch.rearrange("q p w -> p q w"),
                         whl[:, :, :, :].bitcast(F32).rearrange("p q a w -> p q (a w)")).then_inc(weights_out, 16)
            sp.wait_ge(weights_out, 16)

        @block.scalar
        def _(act):
            act.wait_ge(loaded, 96)
            act.activation(sT[:, :], cT[:, :], ACT.Silu).then_inc(silu_done, 1)

        @block.tensor
        def _(pe):
            pe.wait_ge(loaded, 96)
            for h in range(H):
                mm = pe.matmul(comp[h // 8][:, 64 * (h % 8):64 * (h % 8) + 64], wqT[:, h, :], posT[:, h, :],
                               start=(h % 8 == 0), stop=True, skip_group_check=True)
            mm.then_inc(comp_ready, 1)
            for h in range(H):
                mm = pe.matmul(biasp[64:128, h:1 + h], posT[:, h, :], biasT[0:DH, h:h + 1],
                               start=(h == 0), stop=True, skip_group_check=True)
            mm.then_inc(pos_bias, 1)
            pe.wait_ge(silu_done, 1)
            for k in range(6):
                mm = pe.matmul(modp[:, B * k:B * k + B], wmod[:, P * k:P * k + P], sT[:, :],
                               start=(k == 0), stop=True, skip_group_check=True)
            mm.then_inc(mod_ready, 1)

        @block.vector
        def _(dve):
            dve.wait_ge(loaded, 96)
            src = w3[:, :, :].rearrange("p a (q n) -> p a q n", n=P)
            q2 = w3[:, 0, :].rearrange("p (q e d) -> p q e d", e=2, d=DH)
            dve.tensor_copy(wc[:, :, 0:2, 0:DH], q2).then_inc(wc_ready, 1)
            dve.tensor_copy(wc[:, :, 2, :], src[:, 1]).then_inc(wc_ready, 1)
            dve.tensor_copy(wc[:, :, 3, :], src[:, 2]).then_inc(wc_ready, 1)
            dve.wait_ge(comp_ready, 1)
            for k in range(2):
                last = dve.tensor_copy(wc[:, 4 * k:4 * k + 4, 0:2, DH:P],
                                       comp[k][:, :].rearrange("p (q e d) -> p q e d", e=2, d=DH))
            last.then_inc(wc_ready, 1)
            dve.wait_ge(wc_ready, 4)
            dve.tensor_copy(whl[:, :, 0, :], wc[:, :, :, :].rearrange("p q a w -> p q (a w)")).then_inc(wc_ready, 1)
            dve.wait_ge(wc_ready, 5)
            dve.tensor_tensor(whl[:, :, 1, :], wc[:, :, :, :].rearrange("p q a w -> p q (a w)"),
                              whl[:, :, 0, :].bitcast(F32), ALU.subtract).then_inc(lo_ready, 1)
            dve.tensor_scalar(m.bias[0:DH, :], biasT[0:DH, :], 1.0 / QKV_C, None, ALU.mult)
            dve.wait_ge(pos_bias, 1)
            dve.tensor_scalar(m.bias[DH:P, :], biasp[DH:P, 0:H], 1.0 / QKV_C, None, ALU.mult)
            dve.wait_ge(consts, 16 * NC)
            dve.tensor_copy(m.identb[:, :], m.ident[:, :])
            dve.tensor_copy(m.masks[:, :], masks[:, :])
            for k in range(2):
                for e in range(2):
                    dve.tensor_copy(m.lmask[:, k, 192 * e:192 * e + 192], masks[:, 2 * P + 192 * k:2 * P + 192 * k + 192])
            dve.wait_ge(mod_ready, 1)
            dve.tensor_copy(m.mod[:, :, :], modp[:, 0:6 * B].rearrange("p (k b) -> p k b", b=B)).then_inc(chain, 1)
            dve.wait_ge(chain, 1)
            mod2 = m.mod[:, :, :].rearrange("p (a t) b -> p a t b", t=3)
            dve.tensor_scalar(mod2[:, :, 1, :], mod2[:, :, 1, :], 1.0, None, ALU.add)
            dve.tensor_scalar(sg[:, :, :], mod2[:, :, 2, :], 0.0, 2.0, ALU.is_ge, ALU.mult).then_inc(chain, 1)
            dve.scalar_tensor_tensor(out=ab[:, :, :], in0=mod2[:, :, 2, :], scalar=-1.0, in1=mod2[:, :, 2, :],
                                     op0=ALU.mult, op1=ALU.max).then_inc(chain, 1)
            dve.wait_ge(chain, 3)
            dve.tensor_scalar(sg[:, :, :], sg[:, :, :], -1.0, None, ALU.add).then_inc(chain, 1)
            dve.tensor_scalar(ab[:, :, :], ab[:, :, :], 0.25, None, ALU.max).then_inc(chain, 1)
            dve.wait_ge(chain, 5)
            dve.tensor_tensor(mod2[:, :, 2, :], ab[:, :, :], sg[:, :, :], ALU.mult)


def add_layernorm(nc, m, name, src, scale, shift, dst):
    N = B * S // CH
    with ExitStack() as ctx:
        sb = lambda n, s, d=F32: ctx.enter_context(nc.sbuf_tensor(f"{name}_{n}", s, d))
        ps = lambda n, s: ctx.enter_context(nc.psum_tensor(f"{name}_{n}", s, F32))
        sem = ctx.enter_context(semaphores(nc, f"_{name}"))
        dev = sb("dev", [P, N, CH])
        sq = sb("sq", [P, 2, CH])
        sd = sb("sd", [N, CH])
        rstd = sb("rstd", [N, CH])
        meanp = [ps(f"meanp{k}", [P, CH]) for k in range(2)]
        varp = ps("varp", [P, CH])
        rb = [ps(f"rb{k}", [P, CH]) for k in range(2)]
        mean_ready, dev_ready, sq_ready, sq_used, var_ready = (
            sem("mean_ready"), sem("dev_ready"), sem("sq_ready"), sem("sq_used"), sem("var_ready"))
        sd_ready, rstd_ready, rb_ready, norm_ready, mod_ready, hi_ready = (
            sem("sd_ready"), sem("rstd_ready"), sem("rb_ready"), sem("norm_ready"), sem("mod_ready"), sem("hi_ready"))
        block = ctx.enter_context(nc.Block())

        @block.tensor
        def _(pe):
            for n in range(N + 1):
                if n < N:
                    if n >= 2:
                        pe.wait_ge(dev_ready, n - 1)
                    pe.matmul(meanp[n % 2][:, :], m.mean[:, :], src(n), start=True, stop=True).then_inc(mean_ready, 1)
                if n >= 1:
                    pe.wait_ge(sq_ready, n)
                    mm = pe.matmul(varp[0:N, :], m.oneh[:, n - 1, :], sq[:, (n - 1) % 2, :],
                                   start=(n == 1), stop=(n == N))
                    mm.then_inc(sq_used, 1)
            pe.wait_ge(rstd_ready, 1)
            for n in range(N):
                if n >= 2:
                    pe.wait_ge(norm_ready, n - 1)
                pe.matmul(rb[n % 2][:, :], m.sel[:, n, :], rstd[:, :], start=True, stop=True).then_inc(rb_ready, 1)

        @block.vector
        def _(dve):
            if dst == "Z":
                dve.memset(m.Z3[64:P, :, 0:1], 0.0)
            for n in range(N):
                dve.wait_ge(mean_ready, n + 1)
                dve.tensor_tensor(dev[:, n, :], src(n), meanp[n % 2][:, :], ALU.subtract).then_inc(dev_ready, 1)
            dve.wait_ge(sd_ready, 1)
            dve.reciprocal(rstd[:, :], sd[:, :]).then_inc(rstd_ready, 1)
            for n in range(N):
                dve.wait_ge(rb_ready, n + 1)
                dve.tensor_tensor(dev[:, n, :], dev[:, n, :], rb[n % 2][:, :], ALU.mult).then_inc(norm_ready, 1)
                dve.wait_ge(norm_ready, n + 1)
                if dst == "split":
                    dve.tensor_scalar(dev[:, n, :], dev[:, n, :], scale(n), shift(n), ALU.mult, ALU.add).then_inc(mod_ready, 1)
                else:
                    b, c = n // 2, CH * (n % 2)
                    for lo, o in ((0, 0), (64, 1)):
                        dve.tensor_scalar(m.Z3[lo:lo + 64, b, c + o:c + o + CH], dev[lo:lo + 64, n, :],
                                          scale(n)[lo:lo + 64], shift(n)[lo:lo + 64], ALU.mult, ALU.add)

        @block.scalar
        def _(act):
            for n in range(N):
                act.wait_ge(dev_ready, n + 1)
                if n >= 2:
                    act.wait_ge(sq_used, n - 1)
                act.activation(sq[:, n % 2, :], dev[:, n, :], ACT.Square).then_inc(sq_ready, 1)
            act.wait_ge(sq_used, N)
            act.activation(sd[:, :], varp[0:N, :], ACT.Sqrt, bias=m.eps[0:N, :]).then_inc(sd_ready, 1)
            if dst == "split":
                for n in range(N):
                    act.wait_ge(mod_ready, n + 1)
                    act.activation(m.HH[:, n, :], dev[:, n, :], ACT.Copy).then_inc(hi_ready, 1)

        @block.gpsimd
        def _(pool):
            if dst == "split":
                for n in range(N):
                    pool.wait_ge(hi_ready, n + 1)
                    pool.tensor_tensor(m.HL[:, n, :], dev[:, n, :], m.HH[:, n, :].bitcast(F32), ALU.subtract)


def add_attention(nc, m, i, scratch, dinv):
    ITERS = PAIRS // 2 * B
    PREP, SLOT = 10, 4
    with ExitStack() as ctx:
        sb = lambda n, s, d=F32: ctx.enter_context(nc.sbuf_tensor(n, s, d))
        ps = lambda n, s=(P, CH): ctx.enter_context(nc.psum_tensor(n, list(s), F32))
        sem = ctx.enter_context(semaphores(nc))

        qh = [sb(f"qh{h}", [P, S], F32R) for h in range(SLOT)]
        ql = [sb(f"ql{h}", [P, S], F32R) for h in range(SLOT)]
        kh = [sb(f"kh{h}", [P, S], F32R) for h in range(SLOT)]
        kl = [sb(f"kl{h}", [P, S], F32R) for h in range(SLOT)]
        vh = [sb(f"vh{p}", [P, TILES, 3, DH], F32R) for p in range(2)]
        vl = [sb(f"vl{p}", [P, TILES, 3, DH], F32R) for p in range(2)]
        wts = [sb(f"wts{p}", [P, 2, 4, P], F32R) for p in range(2)]
        wo = [sb(f"wo{p}", [P, P]) for p in range(2)]
        qf = sb("qf", [P, 2, CH])
        qt = sb("qt", [P, 2, CH])
        vt = sb("vt", [P, S])
        p32 = sb("p32", [P, 3, CH])
        ph = sb("ph", [P, 3, CH], F32R)
        pl = sb("pl", [P, 3, CH], F32R)
        mxp = sb("mxp", [P, 2, NPC])
        mrow = sb("mrow", [TILES, 2, P], F32R)
        ou = [sb(f"ou{e}", [P, S]) for e in range(2)]
        den = sb("den", [P, 2, TILES])
        rcp = sb("rcp", [P, 2, TILES])
        rb = sb("rb", [P, S])
        ot = sb("ot", [P, S])
        qa = sb("qa", [P, S])
        tk32 = ou[0]
        gate, gate_bias = sb("gate", [P, B]), sb("gate_bias", [P, B])
        st = [ps(f"st{k}") for k in range(2)]
        sm = [ps(f"sm{k}") for k in range(2)]
        po = [ps(f"po{k}") for k in range(2)]
        g0, g1 = ps("g0"), ps("g1")

        tables_in, ready = sem("tables_in"), sem("ready")
        ready_t = sem("table_parts")
        w_in = [sem("wA_in"), sem("wB_in")]
        wo_in = [sem("woA_in"), sem("woB_in")]
        g0_ready = sem("g0_ready")
        g0_by_dve, g0_by_act = sem("g0_by_dve"), sem("g0_by_act")
        g1_ready, g1_read = sem("g1_ready"), sem("g1_read")
        qt_ready, qf_ready = sem("qt_ready"), sem("qf_ready")
        qsum_ready = sem("qsum_ready")
        qh_ready, ql_ready = sem("qh_ready"), sem("ql_ready")
        kh_ready, kl_ready = sem("kh_ready"), sem("kl_ready")
        sm_ready, mx_done = sem("sm_ready"), sem("mx_done")
        mx_ready, mrow_in = sem("mx_ready"), sem("mrow_in")
        st_ready, pt_ready, pv_done = sem("st_ready"), sem("pt_ready"), sem("pv_done")
        pl_by_dve, pl_by_pool = sem("pl_by_dve"), sem("pl_by_pool")
        vh_ready, vl_ready = sem("vh_ready"), sem("vl_ready")
        ou_ready = sem("ou_ready")
        den_in, rcp_ready, dinv_out, rb_in = sem("den_in"), sem("rcp_ready"), sem("dinv_out"), sem("rb_in")
        ot_ready = sem("ot_ready")

        PROJ = [("q", 0, 0), ("q", 0, 1), ("k", 0, 0), ("k", 0, 1), ("q", 1, 0), ("q", 1, 1),
                ("v", 0, 0), ("v", 0, 1), ("vt", 0, 0), ("vt", 0, 1)]
        PROJ_AT = [(0, 1), (0, 3), (0, 7), (0, 9), (0, 11), (1, 1), (1, 3), (1, 5), (1, 7), (1, 10)]
        QH_AT = [(0, 3), (0, 5), (1, 3), (1, 5)]
        BY_POOL = [0, 8]
        BY_DVE = [s for s in range(NS) if s not in BY_POOL]
        MAX_AT = [0, 0, 1, 1, 2, 3, 4, 4, 6, 6, 7, 7]
        MROW_AT, RCP_AT, OUT_AT = 8, 3, (2, 6)

        def pieces_at(s):
            return [p for p in range(NPC) if MAX_AT[p] == s]

        SUM_AT, NORM_AT = (2, 3), 9

        def low_parts(n, s):
            if s in BY_POOL:
                return pl_by_pool, len(BY_POOL) * n + BY_POOL.index(s) + 1
            return pl_by_dve, len(BY_DVE) * n + BY_DVE.index(s) + 4

        def at(places, e, s):
            return [n for n in range(len(places)) if places[n] == (e, s)]

        def cols(c, j):
            return slice(_half(c, j), CH)

        block = ctx.enter_context(nc.Block())

        @block.sync
        def _(sp):
            def group(it):
                return (it >> 2) & 3 if isinstance(it, int) else sp.snap(it >> 2) & 3

            def load_w(p, u):
                u = bass.ds(u, 1)
                src = scratch.rearrange("(u s) p w -> s p u w", s=2)[p][:, u, :]
                sp.dma_start(wts[p][:, :, :, :].bitcast(F32).rearrange("p a c w -> p (a c w)"),
                             src.rearrange("p u w -> p (u w)")).then_inc(w_in[p], 16)

            def load_wo(p, u):
                u = bass.ds(u, 1)
                src = i["wo"].rearrange("(u s p) d -> s p u d", s=2, p=P)[p][:, u, :]
                sp.dma_start(wo[p][:, :], src.rearrange("p u d -> p (u d)")).then_inc(wo_in[p], 16)

            def reciprocals(n, e):
                row = 64 * (1 - e)
                sp.wait_ge(ou_ready, 2 * n + 4)
                sp.dma_start(den[:, e, :], ou[e][row:row + 1, :].rearrange("a (p t) -> a p t", t=TILES))\
                  .then_inc(den_in, 16)
                sp.wait_ge(rcp_ready, n + 2)
                sp.dma_start(dinv[e].rearrange("(p t) -> p t", t=TILES), rcp[:, e, :]).then_inc(dinv_out, 16)
                sp.wait_ge(dinv_out, 16 * (n + 1))
                sp.dma_start(rb[64 * e:64 * e + 64, :], dinv[e:e + 1].broadcast_to([64, S])).then_inc(rb_in, 16)

            def send_max(slot, par, use):
                sp.wait_ge(g1_read, use)
                sp.dma_start(qh[slot][96:97, :].bitcast(F32).rearrange("a (t w) -> a t w", t=TILES),
                             mrow[:, par, :].bitcast(F32)).then_inc(mrow_in, 16)

            load_w(0, 0)
            load_w(1, 0)
            sp.dma_start(qa[:, :], i["qa"]).then_inc(tables_in, 16)
            sp.dma_start(tk32[DH:DH + FREQS, :], i["tk"]).then_inc(tables_in, 16)
            load_wo(0, 0)
            load_wo(1, 0)
            send_max(0, 0, 1)
            with sp.Fori(0, ITERS) as it:
                for q in range(2):
                    g = 2 * it + q
                    u, now = group(it + 1), group(it + q)
                    sp.wait_ge(g0_ready, PREP * g + PREP)
                    load_w(q, u)
                    send_max((2 * q + 1) % SLOT, 1, 4 * g + 2)
                    reciprocals(2 * g, 0)
                    send_max((2 * q + 2) % SLOT, 0, 4 * g + 5)
                    load_wo(1 - q, now)
                    reciprocals(2 * g + 1, 1)
            for p in range(2):
                sp.wait_ge(w_in[p], 16 * (ITERS + 1))
                sp.wait_ge(wo_in[p], 16 * (ITERS + 1))

        @block.tensor
        def _(pe):
            def three(out, w_hi, w_lo, x_hi, x_lo, stop=True):
                pe.matmul(out, w_hi, x_hi, start=True, stop=False)
                pe.matmul(out, w_hi, x_lo, start=False, stop=False)
                return pe.matmul(out, w_lo, x_hi, start=False, stop=stop)

            def project(n, p, b, before, first=False):
                if n in (1, 2, 5, 6):
                    pe.wait_ge(g0_by_dve, 4 * before + (n if n < 3 else n - 2))
                elif n in (3, 4):
                    pe.wait_ge(kl_ready, 4 * before + 2 * (n - 2))
                elif n in (7, 8):
                    pe.wait_ge(g0_by_act, 2 * before + n - 6)
                elif n == 9:
                    pe.wait_ge(vl_ready, 2 * before + 1)
                elif not first:
                    pe.wait_ge(vl_ready, 2 * before)
                what, e, c = PROJ[n]
                if what == "vt":
                    for t in range(4):
                        mm = pe.transpose(g0[:, P * t:P * t + P], vt[:, CH * c + P * t:CH * c + P * t + P], m.ident[:, :])
                else:
                    w = {"q": e, "k": 2, "v": 3}[what]
                    xh = m.HH[:, bass.ds(2 * b + c, 1), :].rearrange("p a w -> p (a w)")
                    xl = m.HL[:, bass.ds(2 * b + c, 1), :].rearrange("p a w -> p (a w)")
                    mm = three(g0[:, :], wts[p][:, 0, w, :], wts[p][:, 1, w, :], xh, xl)
                mm.then_inc(g0_ready, 1)

            def max_piece(p, slot, n, first=False):
                t, k0, w = PIECES[p]
                if not (first and p < 2):
                    pe.wait_ge(mx_done, NPC * n + p - 1)
                diag = k0 + w == P * (t + 1)
                out = sm[p % 2]
                mm = pe.matmul(out[:, 0:w], qh[slot][0:96, P * t:P * t + P], kh[slot][0:96, k0:k0 + w],
                               start=True, stop=not diag)
                if diag:
                    mm = pe.matmul(out[:, w - P:w], m.identb[:, :], m.masks[:, 0:P], start=False, stop=True)
                mm.then_inc(sm_ready, 1)

            def turn_max(n, par):
                pe.wait_ge(mx_ready, n + 1)
                pe.transpose(g1[0:TILES, 0:P], mxp[:, par, 0:TILES], m.ident[:, :]).then_inc(g1_ready, 1)

            def scores(s, slot, t):
                c, j = STEPS[s]
                k = slice(P * j, P * j + P)
                x = slice(CH * c + _half(c, j), CH * c + CH)
                w = CH - _half(c, j)
                out = st[s % 2]
                pe.matmul(out[:, 0:w], kh[slot][0:97, k], qh[slot][0:97, x], start=True, stop=False)
                pe.matmul(out[:, 0:w], kh[slot][0:96, k], ql[slot][0:96, x], start=False, stop=False)
                mm = pe.matmul(out[:, 0:w], kl[slot][0:96, k], qh[slot][0:96, x], start=False, stop=j < 4 * c)
                if j >= 4 * c:
                    mm = pe.matmul(out[:, 0:P], m.identb[:, :], m.masks[:, P:2 * P], start=False, stop=True)
                mm.then_inc(st_ready, 1)

            def outputs(s, n, q, e, k, g):
                c, j = STEPS[s]
                if j == 0:
                    pe.wait_ge(ou_ready, k + 1)
                    pe.wait_ge(vl_ready, 2 * g + 2)
                hi, lo = (v[q][:, j, :, :].rearrange("p a d -> p (a d)")[:, 64 * e:64 * e + P] for v in (vh, vl))
                w = CH - _half(c, j)
                out = po[c][:, cols(c, j)]
                pe.matmul(out, hi, ph[:, s % 3, 0:w], start=(j == 0), stop=False)
                pe.matmul(out, lo, ph[:, s % 3, 0:w], start=False, stop=False)
                pe.wait_ge(*low_parts(n, s))
                pe.matmul(out, hi, pl[:, s % 3, 0:w], start=False, stop=(j == 4 * c + 3)).then_inc(pv_done, 1)

            def product(c, p, g, use):
                pe.wait_ge(g1_read, use)
                if c == 0:
                    pe.wait_ge(ot_ready, 2 * g + 3)
                pe.matmul(g1[:, :], wo[p][:, :], ot[:, CH * c:CH * c + CH], start=True, stop=True).then_inc(g1_ready, 1)

            pe.wait_ge(ready, 3)
            pe.wait_ge(w_in[0], 16)
            for n in range(PREP):
                project(n, 0, 0, 0, first=True)
            pe.wait_ge(qh_ready, 4)
            pe.wait_ge(kh_ready, 4)
            for p in range(NPC):
                max_piece(p, 0, 0, first=True)
            turn_max(0, 0)
            pe.wait_ge(ql_ready, 4)
            pe.wait_ge(kl_ready, 4)
            pe.wait_ge(mrow_in, 16)
            scores(0, 0, 0)
            pe.matmul(po[1][:, :], vl[1][:, TILES - 1, 0:2, :].rearrange("p a d -> p (a d)"), ph[:, (NS - 1) % 3, :], start=True, stop=False)
            with pe.Fori(0, ITERS) as it:
                for q in range(2):
                    g = 2 * it + q
                    for e in range(2):
                        n = 2 * g + e
                        nxt = (2 * q + e + 1) % SLOT
                        for s in range(NS):
                            t = NS * n + s
                            pe.wait_ge(pt_ready, t + 1)
                            if s + 1 < NS:
                                scores(s + 1, 2 * q + e, t + 1)
                            else:
                                pe.wait_ge(mrow_in, 16 * n + 32)
                                if e == 1:
                                    pe.wait_ge(ql_ready, 4 * g + 8)
                                    pe.wait_ge(kl_ready, 4 * g + 8)
                                scores(0, nxt, t + 1)
                            now = pieces_at(s)
                            for p in now:
                                if p == 0 and e == 1:
                                    pe.wait_ge(qh_ready, 4 * g + 6)
                                    pe.wait_ge(kh_ready, 4 * g + 8)
                                max_piece(p, nxt, n + 1)
                            for k in at(PROJ_AT, e, s):
                                if k == 0:
                                    pe.wait_ge(w_in[1 - q], 16 * it + 16 + 16 * q)
                                project(k, 1 - q, (it + q) & 3, g + 1)
                            if e == 1 and s in OUT_AT:
                                c = OUT_AT.index(s)
                                if c == 0:
                                    pe.wait_ge(wo_in[1 - q], 16 * it + 16)
                                product(c, 1 - q, g, 4 * g + 2 + c)
                            if s == MROW_AT:
                                pe.wait_ge(g1_read, 4 * g + (4 if e else 1))
                                turn_max(n + 1, 1 - e)
                            if s > 0:
                                outputs(s - 1, n, q, e, 2 * n + STEPS[s - 1][0], g)
                            else:
                                outputs(NS - 1, n - 1, q if e else 1 - q, 1 - e, None, None)
                            for p in []:
                                max_piece(p, nxt, n + 1)
            pe.wait_ge(pt_ready, 2 * NS * PAIRS * B + 1)
            outputs(NS - 1, 2 * PAIRS * B - 1, 1, 1, None, None)
            pe.wait_ge(wo_in[1], 16 * ITERS + 16)
            for c in range(2):
                pe.wait_ge(g1_read, 4 * PAIRS * B + 1 + c)
                if c == 0:
                    pe.wait_ge(ot_ready, 2 * PAIRS * B + 3)
                pe.matmul(g1[:, :], wo[1][:, :], ot[:, CH * c:CH * c + CH], start=True, stop=True).then_inc(g1_ready, 1)

        @block.scalar
        def _(act):
            def project(n, p, before):
                what, e, c = PROJ[n]
                x = slice(CH * c, CH * c + CH)
                act.wait_ge(g0_ready, PREP * before + n + 1)
                if what == "k":
                    for h in range(2):
                        act.activation(kh[2 * p + h][0:DH, x], g0[DH * h:DH * h + DH, :], ACT.Copy, scale=QKV_C)\
                           .then_inc(kh_ready, 1)
                elif what == "v":
                    act.activation(vt[:, x], g0[:, :], ACT.Copy, scale=QKV_C).then_inc(g0_by_act, 1)
                elif what == "vt":
                    act.activation(vh[p][:, 4 * c:4 * c + 4, 0:3:2, :],
                                   g0[:, :].rearrange("p (t h d) -> p t h d", t=4, h=2), ACT.Copy).then_inc(vh_ready, 1)

            def q_high(r, p, before):
                x = slice(CH * (r % 2), CH * (r % 2) + CH)
                act.wait_ge(qsum_ready, 4 * before + r + 1)
                act.activation(qh[2 * p + r // 2][0:96, x], qf[0:96, r % 2, :], ACT.Copy).then_inc(qh_ready, 1)

            def exp(s, n):
                c, j = STEPS[s]
                t = NS * n + s
                w = CH - _half(c, j)
                act.wait_ge(st_ready, t + 1)
                act.wait_ge(*(low_parts(n, s - 3) if s >= 3 else low_parts(n - 1, s - 3 + NS)))
                act.activation(p32[:, s % 3, 0:w], st[s % 2][:, 0:w], ACT.Exp)
                act.wait_ge(pv_done, t + 1)
                act.activation(ph[:, s % 3, 0:w], st[s % 2][:, 0:w], ACT.Exp).then_inc(pt_ready, 1)

            def chunk_out(n, e, c):
                act.wait_ge(pv_done, NS * n + (4 if c == 0 else NS) + 3)
                act.wait_ge(ot_ready, n + 2)
                act.activation(ou[e][:, CH * c:CH * c + CH], po[c][:, :], ACT.Copy).then_inc(ou_ready, 1)

            act.wait_ge(ready, 3)
            for n in range(PREP):
                if PROJ[n][0] != "q":
                    project(n, 0, 0)
                if n in (1, 5):
                    q_high(n // 4 * 2, 0, 0)
                    q_high(n // 4 * 2 + 1, 0, 0)
            exp(0, 0)
            with act.Fori(0, ITERS) as it:
                for q in range(2):
                    g = 2 * it + q
                    for e in range(2):
                        n = 2 * g + e
                        for s in range(NS):
                            exp((s + 1) % NS, n + (s + 1) // NS)
                            for k in at(PROJ_AT, e, s):
                                if PROJ[k][0] != "q":
                                    project(k, 1 - q, g + 1)
                            for r in at(QH_AT, e, s):
                                q_high(r, 1 - q, g + 1)
                            if s == 0:
                                chunk_out(n - 1, 1 - e, 1)
                            if s == 4:
                                chunk_out(n, e, 0)
            chunk_out(2 * PAIRS * B - 1, 1, 1)

        @block.vector
        def _(dve):
            def project(n, p, u, before, first=False):
                what, e, c = PROJ[n]
                x = slice(CH * c, CH * c + CH)
                if what == "q":
                    r = 2 * e + c
                    dve.wait_ge(g0_ready, PREP * before + n + 1)
                    if not first or r >= 2:
                        dve.wait_ge(ql_ready, 4 * before + r - 1)
                        dve.wait_ge(qh_ready, 4 * before + r - 1)
                    h = bass.ds(4 * u + 2 * p + e, 1)
                    lo = slice(DH + FREQS, P)
                    dve.scalar_tensor_tensor(out=qt[DH:DH + FREQS, r % 2, :], in0=g0[lo, :], scalar=m.bias[lo, h],
                                             in1=qa[lo, x], op0=ALU.add, op1=ALU.mult).then_inc(qt_ready, 1)
                    dve.scalar_tensor_tensor(out=qf[0:96, r % 2, :], in0=g0[0:96, :], scalar=m.bias[0:96, h],
                                             in1=qa[0:96, x], op0=ALU.add, op1=ALU.mult).then_inc(g0_by_dve, 1)
                elif what == "k":
                    for h in range(2):
                        dve.wait_ge(kh_ready, 4 * before + 2 * c + h + 1)
                        ins = dve.scalar_tensor_tensor(
                            out=kl[2 * p + h][0:DH, x], in0=g0[DH * h:DH * h + DH, :], scalar=QKV_C,
                            in1=kh[2 * p + h][0:DH, x].bitcast(F32), op0=ALU.mult, op1=ALU.subtract)
                        ins.then_inc(kl_ready, 1)
                elif what == "vt":
                    dve.wait_ge(vh_ready, 2 * before + c + 1)
                    part = slice(4 * c, 4 * c + 4)
                    dve.tensor_tensor(vl[p][:, part, 0:3:2, :], g0[:, :].rearrange("p (t h d) -> p t h d", t=4, h=2),
                                      vh[p][:, part, 0:3:2, :].bitcast(F32), ALU.subtract).then_inc(vl_ready, 1)

            def max_piece(p, n, par):
                dve.wait_ge(sm_ready, NPC * n + p + 1)
                dve.tensor_reduce(mxp[:, par, p:p + 1], sm[p % 2][:, 0:PIECES[p][2]], AX.X, ALU.max).then_inc(mx_done, 1)

            def join_max(n, par):
                dve.wait_ge(mx_done, NPC * (n + 1))
                dve.tensor_tensor(mxp[:, par, 4:8], mxp[:, par, 4:8], mxp[:, par, 8:12], ALU.max).then_inc(mx_ready, 1)

            def max_rows(n, par, use):
                dve.wait_ge(g1_ready, use + 1)
                dve.tensor_scalar(mrow[:, par, :], g1[0:TILES, 0:P], -1.0, None, ALU.mult).then_inc(g1_read, 1)

            def low_part(s, t):
                w = CH - _half(*STEPS[s])
                dve.wait_ge(pt_ready, t + 2)
                dve.wait_ge(pv_done, t + 1)
                dve.tensor_tensor(pl[:, s % 3, 0:w], p32[:, s % 3, 0:w], ph[:, s % 3, 0:w].bitcast(F32), ALU.subtract)\
                   .then_inc(pl_by_dve, 1)

            def reciprocal(n, e):
                dve.wait_ge(den_in, 16 * n + 32)
                dve.reciprocal(rcp[:, e, :], den[:, e, :]).then_inc(rcp_ready, 1)

            def accumulate(c, b, use):
                dve.wait_ge(g1_ready, use + 1)
                x = m.X[:, bass.ds(S * b + CH * c, CH)]
                dve.scalar_tensor_tensor(out=x, in0=g1[:, :], scalar=gate[:, bass.ds(b, 1)], in1=x, op0=ALU.mult, op1=ALU.add)\
                   .then_inc(g1_read, 1)

            dve.wait_ge(tables_in, 32)
            T = slice(DH, DH + FREQS)
            for h in range(SLOT):
                dve.tensor_copy(kh[h][T, :], tk32[T, :]).then_inc(ready_t, 1)
            dve.wait_ge(ready_t, SLOT)
            for h in range(SLOT):
                dve.tensor_tensor(kl[h][T, :], tk32[T, :], kh[h][T, :].bitcast(F32), ALU.subtract)
                dve.memset(kh[h][96:97, :].bitcast(F32), 1.0)
            for p in range(2):
                dve.memset(vh[p][:, :, 1, :].bitcast(F32), 1.0)
                dve.memset(vl[p][:, :, 1, :].bitcast(F32), 0.0)
            dve.memset(vh[1][:, TILES - 1, 0:3:2, :].bitcast(F32), 0.0)
            dve.memset(vl[1][:, TILES - 1, 0:3:2, :].bitcast(F32), 0.0)
            dve.memset(ph[:, (NS - 1) % 3, :].bitcast(F32), 0.0)
            dve.memset(pl[:, (NS - 1) % 3, :].bitcast(F32), 0.0)
            dve.tensor_scalar(gate_bias[:, :], m.mod[:, 2, :], m.vecs[:, 0:1], None, ALU.mult).then_inc(ready_t, 1)
            dve.tensor_scalar(gate[:, :], m.mod[:, 2, :], OUT_C, None, ALU.mult)
            dve.wait_ge(ready_t, SLOT + 1)
            for b in range(B):
                x = m.X[:, S * b:S * b + S]
                dve.tensor_scalar(x, x, gate_bias[:, b:b + 1], None, ALU.add)
            dve.memset(den[:, 1, :], 1.0).then_inc(ready, 1)
            dve.memset(ou[1][:, :], 0.0).then_inc(ready, 1)
            for n in range(PREP):
                project(n, 0, 0, 0, first=True)
            for p in range(NPC):
                max_piece(p, 0, 0)
            join_max(0, 0)
            max_rows(0, 0, 0)
            with dve.Fori(0, ITERS) as it:
                for q in range(2):
                    g = 2 * it + q
                    u = ((it + q) >> 2) & 3
                    for e in range(2):
                        n = 2 * g + e
                        for s in range(NS):
                            if s in BY_DVE:
                                low_part(s, NS * n + s)
                            for p in pieces_at(s):
                                max_piece(p, n + 1, 1 - e)
                                if p == NPC - 1:
                                    join_max(n + 1, 1 - e)
                            for k in at(PROJ_AT, e, s):
                                project(k, 1 - q, u, g + 1)
                            if e == 1 and s in OUT_AT:
                                c = OUT_AT.index(s)
                                accumulate(c, (it + 3 + q) & 3, 4 * g + 2 + c)
                            if s == MROW_AT:
                                max_rows(n + 1, 1 - e, 4 * g + (4 if e else 1))
                            if s == RCP_AT:
                                reciprocal(n - 1, 1 - e)
            last = 2 * PAIRS * B - 1
            reciprocal(last, 1)
            for c in range(2):
                accumulate(c, 3, 4 * PAIRS * B + 1 + c)

        @block.gpsimd
        def _(pool):
            def low_part(s, n, before):
                t = NS * n + s
                w = CH - _half(*STEPS[s])
                if before:
                    pool.wait_ge(*before)
                pool.wait_ge(pt_ready, t + 2)
                pool.wait_ge(pv_done, t + 1)
                pool.tensor_tensor(pl[:, s % 3, 0:w], p32[:, s % 3, 0:w], ph[:, s % 3, 0:w].bitcast(F32), ALU.subtract)\
                    .then_inc(pl_by_pool, 1)

            def position_sum(r, projected, before):
                T = slice(DH, DH + FREQS)
                if before:
                    pool.wait_ge(*before)
                pool.wait_ge(g0_by_dve, 4 * projected + r + 1)
                pool.wait_ge(qt_ready, 4 * projected + r + 1)
                pool.tensor_tensor(qf[T, r % 2, :], qf[T, r % 2, :], qt[T, r % 2, :], ALU.add).then_inc(qsum_ready, 1)

            def q_low(r, p, projected):
                x = slice(CH * (r % 2), CH * (r % 2) + CH)
                pool.wait_ge(qh_ready, 4 * projected + r + 1)
                h = 2 * p + r // 2
                pool.tensor_tensor(ql[h][0:96, x], qf[0:96, r % 2, :], qh[h][0:96, x].bitcast(F32), ALU.subtract)\
                    .then_inc(ql_ready, 1)

            def normalise(n, e, before):
                rows = slice(64 * e, 64 * e + 64)
                pool.wait_ge(*before)
                pool.wait_ge(rb_in, 16 * n + 32)
                pool.tensor_tensor(ot[rows, :], ou[e][rows, :], rb[rows, :], ALU.mult).then_inc(ot_ready, 1)

            pool.memset(ot[:, :], 0.0)
            pool.sem_inc(pt_ready, 1)
            pool.sem_inc(pv_done, 2)
            pool.sem_inc(pl_by_dve, 3)
            pool.sem_inc(ou_ready, 1)
            pool.sem_inc(ot_ready, 2)
            pool.sem_inc(den_in, 16)
            pool.sem_inc(rb_in, 16)
            pool.memset(rb[:, :], 0.0).then_inc(ready, 1)
            pool.wait_ge(ready, 3)
            for r in range(4):
                position_sum(r, 0, (ql_ready, r) if r else None)
                q_low(r, 0, 0)
            pool.wait_ge(ql_ready, 4)
            with pool.Fori(0, ITERS) as it:
                for q in range(2):
                    g = 2 * it + q
                    for e in range(2):
                        n = 2 * g + e
                        r = 2 * e
                        before = (ot_ready, n + 2)
                        for s in range(NS):
                            if s in BY_POOL:
                                low_part(s, n, before)
                                before = low_parts(n, s)
                            if s in SUM_AT:
                                k = SUM_AT.index(s)
                                position_sum(r + k, g + 1, before)
                                q_low(r + k, 1 - q, g + 1)
                                before = (ql_ready, 4 * (g + 1) + r + k + 1)
                            if s == NORM_AT:
                                if e == 1:
                                    pool.wait_ge(g1_ready, 4 * g + 4)
                                normalise(n - 1, 1 - e, before)
                                before = (ot_ready, n + 3)
            last = 2 * PAIRS * B - 1
            normalise(last, 1, (ot_ready, last + 2))


def add_local_attention(nc, m, i, layer):
    NT, X = B * TILES, 4
    NIT = NT // X
    KW = 192
    GH = 4
    with ExitStack() as ctx:
        sb = lambda n, s, d=F32: ctx.enter_context(nc.sbuf_tensor(f"{n}_l{layer}", s, d))
        ps = lambda n, s=(P, CH): ctx.enter_context(nc.psum_tensor(f"{n}_l{layer}", list(s), F32))
        sem = ctx.enter_context(semaphores(nc, f"_l{layer}"))
        w32 = sb("w32", [P, 3 * CH])
        wh = sb("wh", [P, 3 * CH], F32R)
        wl = sb("wl", [P, 3 * CH], F32R)
        wo = sb("lwo", [P, LH // 2, P])
        tab = sb("tab", [P, TILES, 2, 2, LD])
        scl = sb("scl", [P, 2, 2, LD])
        zt = sb("zt", [P, 2, 2, P], F32R)
        qk = sb("qk", [P, 2, 2, CH])
        t1 = sb("t1", [P, 2, CH])
        t2 = sb("t2", [P, 2, CH])
        sq = sb("sq", [P, 2, CH])
        ss = sb("ss", [P, 2 * LH])
        nhalf = sb("nhalf", [P, 2 * LH])
        r = sb("r", [P, X, 2 * LH])
        qT = sb("qT", [P, LH // 2, P])
        kT = sb("kT", [P, 2, LH // 2, KW])
        v = sb("v", [P, 4, CH])
        pb = sb("pb", [P, 2, GH, 2 * P])
        mx = sb("mx", [P, 2, GH])
        nm = sb("nm", [P, 2, GH])
        sums = sb("sums", [P, 2, GH])
        rs = sb("rs", [P, 2, GH])
        pT = sb("pT", [P, 2, CH])
        oT = sb("oT", [P, LH // 2, P])
        qk_ps = ps("qk_ps", (P, 2, CH))
        s_ps = ps("s_ps", (P, 2, CH))
        v_ps, ta_ps, tb_ps, o_ps = ps("v_ps"), ps("ta_ps"), ps("tb_ps"), ps("o_ps")

        loaded, tabs, w_split, ready = sem("loaded"), sem("tabs"), sem("w_split"), sem("lready")
        zt_hi, zt_ready = sem("zt_hi"), sem("zt_ready")
        qk_ready, qk_copied, sq_ready, summed, ss_ready, r_ready = (
            sem("qk_ready"), sem("qk_copied"), sem("sq_ready"), sem("summed"), sem("ss_ready"), sem("r_ready"))
        cos_done, sin_done, turned, rot_ready = sem("cos_done"), sem("sin_done"), sem("turned"), sem("rot_ready")
        v_ready, v_read = sem("v_ready"), sem("v_read")
        ta_ready, ta_read, tb_ready, tb_read, kT_ready, halo = (
            sem("ta_ready"), sem("ta_read"), sem("tb_ready"), sem("tb_read"), sem("kT_ready"), sem("halo"))
        t0_read = sem("t0_read")
        s_ready, mx_done, nm_ready, exp_done, rs_ready, pn_ready = (
            sem("s_ready"), sem("lmx_done"), sem("nm_ready"), sem("exp_done"), sem("rs_ready"), sem("pn_ready"))
        o_ready, oT_ready, wo_ready, z_done = sem("o_ready"), sem("oT_ready"), sem("wo_ready"), sem("z_done")
        block = ctx.enter_context(nc.Block())

        def zoff(it, x):
            k = x // X
            turn = (it + (NIT + k)) & (NIT - 1) if k else it
            return (turn >> 1) * ZW + (turn & 1) * (X * P) + P * (x % X)

        def tile_in_batch(it, x):
            k = x // X
            turn = (it + (NIT + k)) & (NIT - 1) if k else it
            return (turn & 1) * X + x % X

        def table(a, T, d):
            w = d.stop - d.start
            if isinstance(T, int):
                src = tab[:, T:T + 1, a, :, d]
            else:
                src = tab[:, bass.ds(T, 1), a, :, d]
            return src.rearrange("p o b d -> p (o b) d").unsqueeze(2).broadcast_to([P, 2, LH, w])

        @block.sync
        def _(sp):
            sp.dma_start(w32[:, :], i["wqkv"][layer]).then_inc(loaded, 16)
            sp.dma_start(wo[:, :, :], i["lwo"][layer].rearrange("(q p) d -> p q d", p=P)).then_inc(loaded, 16)
            sp.dma_start(tab[:, :, :, :, :], i["rot"]).then_inc(loaded, 16)
            sp.dma_start(scl[:, :, :, :].rearrange("p a b d -> p (a b d)"),
                         i["qkscale"][layer:layer + 1].broadcast_to([P, 4 * LD])).then_inc(loaded, 16)

        @block.tensor
        def _(pe):
            def project(slot_ring):
                zh, zl = zt[:, slot_ring, 0, :], zt[:, slot_ring, 1, :]
                for n in range(3):
                    if n == 2:
                        yield
                    w = slice(CH * n, CH * n + CH)
                    out = qk_ps[:, n, :] if n < 2 else v_ps[:, :]
                    pe.matmul(out, zh, wh[:, w], start=True, stop=False)
                    pe.matmul(out, zh, wl[:, w], start=False, stop=False)
                    mm = pe.matmul(out, zl, wh[:, w], start=False, stop=True)
                    if n:
                        mm.then_inc(qk_ready if n == 1 else v_ready, 1)
                yield

            def scores(g, ring, mask):
                for e in range(2):
                    pe.matmul(s_ps[:, e, 0:2 * KW], m.identb[:, :], mask, start=True, stop=True)
                    for s in range(2):
                        rows = slice(LD * e, LD * e + LD)
                        mm = pe.matmul(s_ps[:, e, KW * s:KW * s + KW], qT[rows, 2 * g + s, :], kT[rows, ring, 2 * g + s, :],
                                       start=False, stop=True, skip_group_check=True)
                mm.then_inc(s_ready, 1)

            def turn_probs(g, s):
                bank, sm_ = (ta_ps, ta_ready) if s == 0 else (tb_ps, tb_ready)
                for e in range(2):
                    for a in range(2):
                        mm = pe.transpose(bank[:, P * (2 * e + a):P * (2 * e + a) + P],
                                          pb[:, g, 2 * s + e, P * a:P * a + P], m.ident[:, :])
                mm.then_inc(sm_, 1)

            def outputs(g, s, cur, prev):
                for e in range(2):
                    h = GH * g + 2 * s + e
                    d = slice(LD * h, LD * h + LD)
                    out = o_ps[LD * e:LD * e + LD, P * (2 * g + s):P * (2 * g + s) + P]
                    pe.matmul(out, v[:, prev, d], pT[:, s, 2 * P * e:2 * P * e + P], start=True, stop=False)
                    mm = pe.matmul(out, v[:, cur, d], pT[:, s, 2 * P * e + P:2 * P * e + 2 * P], start=False, stop=True)
                return mm

            def turn_qk():
                for n, (bank, sm_) in enumerate(((ta_ps, ta_ready), (tb_ps, tb_ready))):
                    for q in range(4):
                        mm = pe.transpose(bank[:, P * q:P * q + P], t1[:, n, P * q:P * q + P], m.ident[:, :])
                    mm.then_inc(sm_, 1)

            def first_outputs(t, cur, prev):
                pe.wait_ge(oT_ready, t + 1)
                pe.wait_ge(t0_read, t + 1)
                outputs(0, 0, cur, prev)
                pe.wait_ge(tb_read, 2 * t + 1)
                outputs(0, 1, cur, prev)

            def finish_probs(t):
                pe.wait_ge(pn_ready, 2 * t + 1)
                pe.wait_ge(t0_read, t + 1)
                turn_probs(1, 0)
                pe.wait_ge(tb_read, 2 * t + 1)
                turn_probs(1, 1)

            def finish_outputs(t, cur, prev):
                pe.wait_ge(ta_read, 2 * t + 2)
                outputs(1, 0, cur, prev)
                pe.wait_ge(tb_read, 2 * t + 2)
                outputs(1, 1, cur, prev).then_inc(o_ready, 1)

            def product(t, last=False):
                pe.wait_ge(oT_ready, t + 2)
                if last:
                    pe.wait_ge(z_done, t + 1)
                else:
                    pe.wait_ge(v_read, t + 3)
                for q in range(4):
                    mm = pe.matmul(v_ps[:, 0:P], wo[:, q, :], oT[:, q, :], start=(q == 0), stop=(q == 3))
                mm.then_inc(wo_ready, 1)

            pe.wait_ge(w_split, 2)
            pe.wait_ge(ready, 2)
            for k in range(2):
                pe.wait_ge(zt_ready, k + 1)
                if k == 1:
                    pe.wait_ge(qk_copied, 1)
                    pe.wait_ge(v_read, 1)
                for _ in project(k):
                    pass
            pe.wait_ge(rot_ready, 1)
            turn_qk()
            with pe.Fori(0, NIT) as it:
                for x in range(X):
                    t = it * X + x
                    mask = m.lmask[:, bass.ds(it & 1, 1), :].rearrange("p a w -> p (a w)") if x == 0 else m.lmask[:, 1, :]
                    pe.wait_ge(ta_read, 2 * t + 1)
                    pe.wait_ge(kT_ready, t + 1)
                    pe.wait_ge(halo, t + 1)
                    pe.wait_ge(exp_done, 2 * t + 1)
                    scores(0, x % 2, mask)
                    first_outputs(t, (x + 3) % 4, (x + 2) % 4)
                    finish_probs(t)
                    nxt = project(x % 2)
                    pe.wait_ge(zt_ready, t + 3)
                    pe.wait_ge(qk_copied, t + 2)
                    next(nxt)
                    pe.wait_ge(v_read, t + 2)
                    pe.wait_ge(z_done, t + 1)
                    next(nxt)
                    finish_outputs(t, (x + 3) % 4, (x + 2) % 4)
                    pe.wait_ge(exp_done, 2 * t + 2)
                    scores(1, x % 2, mask)
                    product(t)
                    pe.wait_ge(rot_ready, t + 2)
                    pe.wait_ge(ta_read, 2 * t + 2)
                    pe.wait_ge(tb_read, 2 * t + 2)
                    turn_qk()
                    pe.wait_ge(pn_ready, 2 * t + 2)
                    pe.wait_ge(ta_read, 2 * t + 3)
                    turn_probs(0, 0)
                    pe.wait_ge(kT_ready, t + 2)
                    turn_probs(0, 1)
            first_outputs(NT, 3, 2)
            finish_probs(NT)
            finish_outputs(NT, 3, 2)
            product(NT, last=True)

        @block.scalar
        def _(act):
            def exps(g, t, ring):
                act.wait_ge(nm_ready, 2 * t + g + 1)
                for e in range(2):
                    for s in range(2):
                        h = GH * g + 2 * s + e
                        ins = act.activation(pb[:, g, 2 * s + e, 64:2 * P], s_ps[:, e, KW * s:KW * s + KW], ACT.Exp,
                                             bias=nm[:, g, 2 * e + s:2 * e + s + 1], scale=r[:, ring, h:h + 1],
                                             accum_out=sums[:, g, 2 * s + e:2 * s + e + 1])
                ins.then_inc(exp_done, 1)

            def from_ta(dst, use):
                act.wait_ge(ta_ready, use)
                act.activation(dst, ta_ps[:, :], ACT.Copy).then_inc(ta_read, 1)

            def take_out(t):
                act.wait_ge(o_ready, t + 1)
                act.wait_ge(wo_ready, t + 1)
                act.activation(oT[:, :, :].rearrange("p q t -> p (q t)"), o_ps[:, :], ACT.Copy).then_inc(oT_ready, 1)

            def copy_qk(count, ring):
                act.wait_ge(qk_ready, count)
                act.activation(qk[:, ring, :, :], qk_ps[:, :, :], ACT.Copy).then_inc(qk_copied, 1)

            def square(count, ring):
                act.wait_ge(qk_copied, count)
                act.activation(sq[:, :, :], qk[:, ring, :, :], ACT.Square).then_inc(sq_ready, 1)

            def take_v(t1_, slot):
                act.wait_ge(v_ready, t1_)
                act.activation(v[:, slot, :], v_ps[:, :], ACT.Copy).then_inc(v_read, 1)

            def take_qk(use, t1_, ring):
                from_ta(qT[:, :, :].rearrange("p q t -> p (q t)"), use)
                act.wait_ge(tb_ready, use)
                act.activation(kT[:, ring, :, 64:KW], tb_ps[:, :].rearrange("p (q t) -> p q t", q=4), ACT.Copy)\
                   .then_inc(kT_ready, 1)

            act.wait_ge(ready, 2)
            copy_qk(1, 0)
            take_v(1, 0)
            square(1, 0)
            copy_qk(2, 1)
            take_v(2, 1)
            act.wait_ge(ss_ready, 1)
            square(2, 1)
            take_qk(1, 1, 0)
            with act.Fori(0, NIT) as it:
                for x in range(X):
                    t = it * X + x
                    from_ta(pT[:, 0, :], 3 * t + 2)
                    exps(0, t, x)
                    act.wait_ge(rot_ready, t + 1)
                    copy_qk(t + 3, x % 2)
                    take_out(t)
                    take_v(t + 3, (x + 2) % 4)
                    act.wait_ge(ss_ready, t + 2)
                    square(t + 3, x % 2)
                    take_qk(3 * t + 3, t + 2, (x + 1) % 2)
                    exps(1, t, x)
            from_ta(pT[:, 0, :], 3 * NT + 2)
            take_out(NT)

        @block.vector
        def _(dve):
            def split_tile(off, ring, count):
                z = m.Z[:, bass.ds(off, P)] if not isinstance(off, int) else m.Z[:, off:off + P]
                dve.tensor_copy(zt[:, ring, 0, :], z).then_inc(zt_hi, 1)
                dve.wait_ge(zt_hi, count)
                dve.tensor_tensor(zt[:, ring, 1, :], z, zt[:, ring, 0, :].bitcast(F32), ALU.subtract).then_inc(zt_ready, 1)

            def turn_cos(T, count, ring):
                dve.wait_ge(qk_copied, count)
                dve.tensor_tensor(t1[:, :, :].rearrange("p n (h d) -> p n h d", d=LD),
                                  qk[:, ring, :, :].rearrange("p n (h d) -> p n h d", d=LD),
                                  table(0, T, slice(0, LD)), ALU.mult).then_inc(cos_done, 1)

            def squares(count):
                dve.wait_ge(sq_ready, count)
                dve.tensor_reduce(ss[:, :], sq[:, :, :].rearrange("p n (h d) -> p (n h) d", d=LD), AX.X, ALU.add)\
                   .then_inc(summed, 1)
                dve.wait_ge(summed, count)
                dve.tensor_scalar(ss[:, :], ss[:, :], 1e-24, None, ALU.max).then_inc(ss_ready, 1)

            def turn(count):
                dve.wait_ge(cos_done, count)
                dve.wait_ge(sin_done, count)
                dve.tensor_tensor(t1[:, :, :], t1[:, :, :], t2[:, :, :], ALU.add).then_inc(turned, 1)

            def normalise_k(ring, count):
                dve.wait_ge(turned, count)
                dve.wait_ge(r_ready, count)
                k = t1[:, 1, :].rearrange("p (h d) -> p h d", d=LD)
                dve.tensor_tensor(k, k, r[:, ring, LH:2 * LH].unsqueeze(2).broadcast_to([P, LH, LD]), ALU.mult)\
                   .then_inc(rot_ready, 1)

            def take_halo(ring, count):
                dve.wait_ge(kT_ready, count)
                dve.tensor_copy(kT[:, 1 - ring, :, 0:64], kT[:, ring, :, P:KW]).then_inc(halo, 1)

            def maxima(g, t, ring):
                dve.wait_ge(s_ready, 2 * t + g + 1)
                dve.tensor_reduce(mx[:, g, :].rearrange("p (e s) -> p e s", e=2),
                                  s_ps[:, :, 0:2 * KW].rearrange("p e (s w) -> p e s w", s=2), AX.X, ALU.max).then_inc(mx_done, 1)
                dve.wait_ge(mx_done, 2 * t + g + 1)
                rq = r[:, ring, GH * g:GH * g + GH].rearrange("p (s e) -> p e s", e=2)
                dve.scalar_tensor_tensor(out=nm[:, g, :].rearrange("p (e s) -> p e s", e=2),
                                         in0=mx[:, g, :].rearrange("p (e s) -> p e s", e=2), scalar=-1.0, in1=rq,
                                         op0=ALU.mult, op1=ALU.mult).then_inc(nm_ready, 1)

            def reciprocal(g, count):
                dve.wait_ge(exp_done, count)
                dve.reciprocal(rs[:, g, :], sums[:, g, :]).then_inc(rs_ready, 1)

            def from_tb(use):
                dve.wait_ge(tb_ready, use)
                dve.tensor_copy(pT[:, 1, :], tb_ps[:, :]).then_inc(tb_read, 1)

            def add_to_z(off, t):
                dve.wait_ge(wo_ready, t + 2)
                for rows, o in ((slice(0, 64), 0), (slice(64, P), 1)):
                    z = m.Z[rows, bass.ds(off + o, P)] if not isinstance(off, int) else m.Z[rows, off + o:off + o + P]
                    ins = dve.tensor_tensor(z, z, v_ps[rows, 0:P], ALU.add)
                ins.then_inc(z_done, 1)

            dve.wait_ge(loaded, 64)
            dve.tensor_copy(wh[:, :], w32[:, :]).then_inc(w_split, 1)
            dve.wait_ge(w_split, 1)
            dve.tensor_tensor(wl[:, :], w32[:, :], wh[:, :].bitcast(F32), ALU.subtract).then_inc(w_split, 1)
            dve.memset(pb[:, :, :, 0:P], 0.0)
            dve.memset(pb[:, :, :, P:2 * P], 0.0)
            dve.memset(pT[:, :, :], 0.0)
            dve.memset(v[:, 2:4, :], 0.0)
            dve.memset(kT[:, 0, :, 0:64], 0.0)
            dve.memset(sums[:, 1, :], 1.0)
            for a in range(2):
                tt = tab[:, :, a, :, :]
                dve.tensor_tensor(tt, tt, scl[:, a, :, :].unsqueeze(1).broadcast_to([P, TILES, 2, LD]), ALU.mult)\
                   .then_inc(tabs, 1)
            dve.memset(nhalf[:, :], -0.5).then_inc(ready, 1)
            split_tile(0, 0, 1)
            split_tile(P, 1, 2)
            dve.wait_ge(tabs, 2)
            turn_cos(0, 1, 0)
            squares(1)
            dve.wait_ge(v_ready, 1)
            split_tile(2 * P, 0, 3)
            turn(1)
            normalise_k(0, 1)
            dve.wait_ge(r_ready, 1)
            squares(2)
            take_halo(0, 1)
            with dve.Fori(0, NIT) as it:
                for x in range(X):
                    t = it * X + x
                    reciprocal(1, 2 * t + 1)
                    dve.wait_ge(ta_ready, 3 * t + 1)
                    dve.wait_ge(tb_ready, 3 * t + 1)
                    turn_cos(tile_in_batch(it, x + 1), t + 2, (x + 1) % 2)
                    maxima(0, t, x)
                    from_tb(3 * t + 2)
                    turn(t + 2)
                    normalise_k((x + 1) % X, t + 2)
                    reciprocal(0, 2 * t + 2)
                    maxima(1, t, x)
                    dve.wait_ge(r_ready, t + 2)
                    squares(t + 3)
                    add_to_z(zoff(it, x - 1), t)
                    split_tile(zoff(it, x + 3), (x + 1) % 2, t + 4)
                    take_halo((x + 1) % 2, t + 2)
                    dve.wait_ge(ta_ready, 3 * t + 4)
                    dve.tensor_copy(pT[:, 0, :], ta_ps[:, :]).then_inc(t0_read, 1)
                    from_tb(3 * t + 4)
            reciprocal(1, 2 * NT + 1)
            from_tb(3 * NT + 2)
            add_to_z((B - 1) * ZW + (TILES - 1) * P, NT)

        @block.gpsimd
        def _(pool):
            def norms(ring, count):
                pool.wait_ge(ss_ready, count)
                pool.tensor_tensor(r[:, ring, :], ss[:, :], nhalf[:, :], ALU.pow).then_inc(r_ready, 1)

            def normalise(g, count):
                pool.wait_ge(rs_ready, count)
                p = pb[:, g, :, 64:2 * P]
                pool.tensor_tensor(p, p, rs[:, g, :].unsqueeze(2).broadcast_to([P, GH, KW]), ALU.mult).then_inc(pn_ready, 1)

            def turn_sin(T, ring):
                q = qk[:, ring, :, :].rearrange("p n (h d) -> p n h d", d=LD)
                o = t2[:, :, :].rearrange("p n (h d) -> p n h d", d=LD)
                lo, hi = slice(0, LD // 2), slice(LD // 2, LD)
                pool.tensor_tensor(o[:, :, :, lo], q[:, :, :, hi], table(1, T, lo), ALU.mult)
                pool.tensor_tensor(o[:, :, :, hi], q[:, :, :, lo], table(1, T, hi), ALU.mult).then_inc(sin_done, 1)

            pool.sem_inc(exp_done, 1)
            pool.sem_inc(oT_ready, 1)
            pool.sem_inc(z_done, 1)
            pool.sem_inc(tb_read, 1)
            pool.sem_inc(t0_read, 1)
            pool.sem_inc(wo_ready, 1)
            pool.sem_inc(ready, 1)
            pool.wait_ge(ready, 2)
            pool.wait_ge(tabs, 2)
            pool.wait_ge(qk_copied, 1)
            turn_sin(0, 0)
            norms(0, 1)
            norms(1, 2)
            with pool.Fori(0, NIT) as it:
                for x in range(X):
                    t = it * X + x
                    pool.wait_ge(r_ready, t + 2)
                    normalise(1, 2 * t + 1)
                    turn_sin(tile_in_batch(it, x + 1), (x + 1) % 2)
                    pool.wait_ge(sin_done, t + 2)
                    normalise(0, 2 * t + 2)
                    pool.wait_ge(pn_ready, 2 * t + 2)
                    norms((x + 2) % X, t + 3)
            normalise(1, 2 * NT + 1)


def add_mlp(nc, m, i, layer):
    with ExitStack() as ctx:
        sb = lambda n, s, d=F32: ctx.enter_context(nc.sbuf_tensor(f"{n}_m{layer}", s, d))
        ps = lambda n: ctx.enter_context(nc.psum_tensor(f"{n}_m{layer}", [P, CH], F32))
        sem = ctx.enter_context(semaphores(nc, f"_m{layer}"))
        w32 = sb("mw32", [P, 2 * HID])
        wh = sb("mwh", [P, 2 * HID], F32R)
        wl = sb("mwl", [P, 2 * HID], F32R)
        w2 = sb("w2", [P, NHID, D])
        gl = sb("gl", [P, NHID, CH])
        u = sb("u", [P, 2, NHID, CH])
        bank = [ps(f"b{k}") for k in range(2 * NHID)]
        y_ps = [ps(f"y{k}") for k in range(2)]
        loaded, w_split = sem("mloaded"), sem("mw_split")
        g_ready, a_ready, gelu_done, u_ready, y_ready, z_done = (
            sem("g_ready"), sem("a_ready"), sem("gelu_done"), sem("u_ready"), sem("y_ready"), sem("mz_done"))
        ms = [min(P, HID - P * j) for j in range(NHID)]
        block = ctx.enter_context(nc.Block())

        @block.sync
        def _(sp):
            sp.dma_start(w32[:, :], i["w1"][layer]).then_inc(loaded, 16)
            full = HID // P
            sp.dma_start(w2[:, 0:full, :], i["w2"][layer, 0:P * full].rearrange("(q p) d -> p q d", p=P)).then_inc(loaded, 16)
            sp.dma_start(w2[0:ms[-1], full, :], i["w2"][layer, P * full:HID]).then_inc(loaded, 16)

        @block.tensor
        def _(pe):
            def hidden(n, half, b, first):
                xh = m.HH[:, bass.ds(2 * b + half, 1), :].rearrange("p a w -> p (a w)")
                xl = m.HL[:, bass.ds(2 * b + half, 1), :].rearrange("p a w -> p (a w)")
                for j in range(NHID):
                    for k, sm_ in ((1, g_ready), (0, a_ready)):
                        w = slice(HID * k + P * j, HID * k + P * j + ms[j])
                        out = bank[2 * j + k][0:ms[j], :]
                        if not first:
                            pe.wait_ge(u_ready, NHID * n + j + 1 - NHID)
                        pe.matmul(out, wh[:, w], xh, start=True, stop=False)
                        pe.matmul(out, wh[:, w], xl, start=False, stop=False)
                        pe.matmul(out, wl[:, w], xh, start=False, stop=True).then_inc(sm_, 1)

            def down(n, half):
                pe.wait_ge(z_done, 2 * n + 2)
                for j in range(NHID):
                    pe.wait_ge(u_ready, NHID * n + j + 1)
                    mm = pe.matmul(y_ps[half][:, :], w2[0:ms[j], j, :], u[0:ms[j], half, j, :], start=(j == 0), stop=(j == NHID - 1))
                mm.then_inc(y_ready, 1)

            pe.wait_ge(loaded, 48)
            pe.wait_ge(w_split, 2)
            hidden(0, 0, 0, True)
            with pe.Fori(0, B) as b:
                hidden(2 * b + 1, 1, b, False)
                down(2 * b, 0)
                hidden(2 * b + 2, 0, (b + 1) & (B - 1), False)
                down(2 * b + 1, 1)

        @block.scalar
        def _(act):
            def gelus(n, first):
                for j in range(NHID):
                    act.wait_ge(g_ready, NHID * n + j + 1)
                    if not first:
                        act.wait_ge(u_ready, NHID * n + j + 1 - NHID)
                    act.activation(gl[0:ms[j], j, :], bank[2 * j + 1][0:ms[j], :], ACT.Gelu,
                                   bias=m.b1[0:ms[j], layer, 1, j:j + 1]).then_inc(gelu_done, 1)
            gelus(0, True)
            with act.Fori(0, B) as b:
                gelus(2 * b + 1, False)
                gelus(2 * b + 2, False)

        @block.vector
        def _(dve):
            def gate(n, half):
                for j in range(NHID):
                    dve.wait_ge(gelu_done, NHID * n + j + 1)
                    dve.wait_ge(a_ready, NHID * n + j + 1)
                    dve.scalar_tensor_tensor(out=u[0:ms[j], half, j, :], in0=bank[2 * j][0:ms[j], :],
                                             scalar=m.b1[0:ms[j], layer, 0, j:j + 1], in1=gl[0:ms[j], j, :],
                                             op0=ALU.add, op1=ALU.mult).then_inc(u_ready, 1)

            def add_to_z(n, half, b):
                dve.wait_ge(y_ready, n + 1)
                for lo, o in ((0, 0), (64, 1)):
                    z = m.Z[lo:lo + 64, bass.ds(ZW * b + CH * half + o, CH)]
                    dve.scalar_tensor_tensor(out=z, in0=y_ps[half][lo:lo + 64, :], scalar=m.vecs[lo:lo + 64, 3 + 3 * layer:4 + 3 * layer],
                                             in1=z, op0=ALU.add, op1=ALU.add).then_inc(z_done, 1)

            dve.wait_ge(loaded, 48)
            dve.tensor_copy(wh[:, :], w32[:, :]).then_inc(w_split, 1)
            dve.wait_ge(w_split, 1)
            dve.tensor_tensor(wl[:, :], w32[:, :], wh[:, :].bitcast(F32), ALU.subtract).then_inc(w_split, 1)
            dve.sem_inc(z_done, 2)
            gate(0, 0)
            with dve.Fori(0, B) as b:
                gate(2 * b + 1, 1)
                add_to_z(2 * b, 0, b)
                dve.wait_ge(y_ready, 2 * b + 1)
                gate(2 * b + 2, 0)
                add_to_z(2 * b + 1, 1, b)


def add_output(nc, m, out):
    with ExitStack() as ctx:
        sem = ctx.enter_context(semaphores(nc))
        summed, stored = sem("o_summed"), sem("o_stored")
        block = ctx.enter_context(nc.Block())

        @block.vector
        def _(dve):
            for b in range(B):
                for rows, o in ((slice(0, 64), 0), (slice(64, P), 1)):
                    x = m.X[rows, S * b:S * b + S]
                    dve.scalar_tensor_tensor(out=x, in0=m.Z[rows, ZW * b + o:ZW * b + o + S], scalar=m.mod[rows, 5, b:b + 1],
                                             in1=x, op0=ALU.mult, op1=ALU.add).then_inc(summed, 1)

        @block.sync
        def _(sp):
            for b in range(B):
                sp.wait_ge(summed, 2 * b + 2)
                sp.dma_start(out[:, S * b:S * b + S], m.X[:, S * b:S * b + S]).then_inc(stored, 16)
            sp.wait_ge(stored, 16 * B)


def host_constants():
    f = np.float32
    ident = np.eye(P, dtype=f)
    mean = np.full((P, P), 1.0 / D, f)
    N = B * S // CH
    oneh = np.zeros((P, N, N), f)
    sel = np.zeros((N, N, P), f)
    for n in range(N):
        oneh[:, n, n] = 1.0 / D
        sel[n, n, :] = 1.0
    a = np.arange(P)
    nat = np.where(a[None, :] > a[:, None], BIG, 0.0)
    tr = nat.T
    key = np.arange(192)[None, :] - 64
    loc = np.where((key > a[:, None]) | (key < a[:, None] - WIN), BIG, 0.0)
    loc0 = np.where(key < 0, BIG, loc)
    masks = np.concatenate([nat, tr, loc0, loc], 1).astype(f)
    w = 1250.0 ** (-(np.arange(FREQS) // 2 * 2) / FREQS)
    ang = w[:, None] * np.arange(S)[None, :]
    even = (np.arange(FREQS) % 2 == 0)[:, None]
    tk = np.where(even, np.cos(ang), np.sin(ang)).astype(f)
    qa = np.zeros((P, S))
    qa[0:DH] = QKV_C / 8
    qa[DH:DH + FREQS] = QKV_C / 32 * np.sin(ang)
    qa[DH + FREQS:] = QKV_C / 32 * np.where(even, np.cos(ang), -np.cos(ang))
    hidx = np.arange(0, LD, 2, dtype=f)
    inv = (f(1.0) / np.power(f(10000.0), hidx / f(LD))).astype(f)
    tok = np.arange(S, dtype=f)
    fr = tok[:, None] * inv[None, :]
    fr = np.concatenate([fr, fr], 1)
    base = ((hidx + f(0.4 * LD)) / f(1.4 * LD)).astype(f)
    power = ((tok - S // 2) / f(WIN // 2)).astype(f)
    sc = np.power(base[None, :], power[:, None]).astype(f)
    sc = np.concatenate([sc, sc], 1)
    sign = np.where(np.arange(LD) < LD // 2, -1.0, 1.0).astype(f)
    cos, sin = np.cos(fr), np.sin(fr) * sign
    rot = np.stack([np.stack([cos * sc * 8, cos / sc]), np.stack([sin * sc * 8, sin / sc])])
    rot = rot.reshape(2, 2, TILES, P, LD).transpose(3, 2, 0, 1, 4).astype(f)
    return {"rot": rot, "ident": ident, "mean": mean, "oneh": oneh, "sel": sel, "masks": masks, "tk": tk, "qa": qa.astype(f)}


def build(nc, i, scratch, dinv, out):
    with ExitStack() as ctx:
        sb = lambda n, s, d=F32: ctx.enter_context(nc.sbuf_tensor(n, s, d))
        m = Mem()
        m.X = sb("X", [P, B * S])
        m.ident = sb("ident", [P, P])
        m.identb = sb("identb", [P, P], BF16)
        m.masks = sb("masks", [P, 2 * P + 2 * 192], BF16)
        m.mean = sb("mean", [P, P])
        m.oneh = sb("oneh", [P, 8, 8])
        m.sel = sb("sel", [8, 8, P])
        m.bias = sb("bias", [P, H])
        m.mod = sb("mod", [P, 6, B])
        m.vecs = sb("vecs", [P, 8])
        m.b1 = sb("b1", [P, DEPTH, 2, NHID])
        m.eps = m.vecs[:, 7:8]
        m.lmask = sb("lmask", [P, 2, 2 * 192], BF16)
        add_mod_and_weights(nc, m, i, scratch)
        with ExitStack() as att:
            m.HH = att.enter_context(nc.sbuf_tensor("HH", [P, 8, CH], F32R))
            m.HL = att.enter_context(nc.sbuf_tensor("HL", [P, 8, CH], F32R))
            add_layernorm(nc, m, "ln1", lambda n: m.X[:, CH * n:CH * n + CH],
                          lambda n: m.mod[:, 1, n // 2:n // 2 + 1], lambda n: m.mod[:, 0, n // 2:n // 2 + 1], "split")
            add_attention(nc, m, i, scratch, dinv)
        with ExitStack() as ffn:
            m.Z = ffn.enter_context(nc.sbuf_tensor("Z", [P, (B + 1) * ZW], F32))
            m.Z3 = m.Z[:, 0:B * ZW].rearrange("p (b w) -> p b w", b=B)
            one = lambda k: (lambda n: m.vecs[:, k:k + 1])
            add_layernorm(nc, m, "ln2", lambda n: m.X[:, CH * n:CH * n + CH],
                          lambda n: m.mod[:, 4, n // 2:n // 2 + 1], lambda n: m.mod[:, 3, n // 2:n // 2 + 1], "Z")
            for layer in range(DEPTH):
                add_local_attention(nc, m, i, layer)
                with ExitStack() as mlp:
                    m.HH = mlp.enter_context(nc.sbuf_tensor(f"HH{layer}", [P, 8, CH], F32R))
                    m.HL = mlp.enter_context(nc.sbuf_tensor(f"HL{layer}", [P, 8, CH], F32R))
                    add_layernorm(nc, m, f"ln3{layer}",
                                  lambda n: m.Z[:, ZW * (n // 2) + CH * (n % 2):ZW * (n // 2) + CH * (n % 2) + CH],
                                  one(1 + 3 * layer), one(2 + 3 * layer), "split")
                    add_mlp(nc, m, i, layer)
            add_output(nc, m, out)


def kernel(**inputs):
    import numpy as _np
    import concourse.bacc as _bacc
    from concourse import mybir as _mybir
    from concourse.bass_utils import run_bass_kernel_spmd as _run

    v = {k.replace("L0_", ""): _np.asarray(a) for k, a in inputs.items()}
    f = _np.float32
    qkv, pos = v["attn_qkv"], v["attn_positional"]
    swap = _np.arange(FREQS) ^ 1
    posT = _np.concatenate([pos.transpose(2, 1, 0), pos[swap].transpose(2, 1, 0)], 2)
    vecs = _np.zeros((P, 8), f)
    vecs[:, 0] = v["attn_out_bias"]
    for l in range(DEPTH):
        vecs[:, 1 + 3 * l] = v["ffn_ln_g"][l]
        vecs[:, 2 + 3 * l] = v["ffn_ln_b"][l]
        vecs[:, 3 + 3 * l] = v["ffn_b2"][l]
    vecs[:, 7] = 1e-5
    b1 = _np.zeros((DEPTH, 2, NHID * P), f)
    b1[:, :, :HID] = v["ffn_b1"].reshape(DEPTH, 2, HID)
    half = (_np.arange(LD) + LD // 2) % LD
    qs = _np.stack([v["ffn_q_scale"], v["ffn_k_scale"]], 1)
    qks = _np.stack([qs, qs[:, :, half]], 1).reshape(DEPTH, 4 * LD)
    data = {
        "xT": v["attn_input"].transpose(2, 0, 1).reshape(D, B * S),
        "qkv": qkv, "wqT": qkv[:, 0].transpose(2, 1, 0), "posT": posT, "biasT": v["attn_q_bias"].T,
        "cT": v["c"].T, "wmod": v["wmod"], "vecs": vecs,
        "b1": b1.reshape(DEPTH, 2, NHID, P).transpose(3, 0, 1, 2),
        "wo": v["attn_out_kernel"], "wqkv": v["ffn_wqkv"], "lwo": v["ffn_wo"], "w1": v["ffn_w1"], "w2": v["ffn_w2"],
        "qkscale": qks,
    } | host_constants()
    nc = _bacc.Bacc("TRN2", target_bir_lowering=False, num_devices=1)
    arrays, aps = {}, {}
    for name, a in data.items():
        a = _np.ascontiguousarray(a)
        arrays[f"in_{name}_dram"] = a
        aps[name] = nc.dram_tensor(f"in_{name}_dram", a.shape, _mybir.dt.from_np(a.dtype), kind="ExternalInput").ap()
    scratch = nc.dram_tensor("split_weights", (PAIRS, P, 2 * 4 * P), F32, kind="Internal").ap()
    dinv = nc.dram_tensor("denominators", (2, S), F32, kind="Internal").ap()
    out = nc.dram_tensor("out_0_dram", (P, B * S), F32, kind="ExternalOutput").ap()
    build(nc, aps, scratch, dinv, out)
    r = _run(nc, [arrays], core_ids=[0])
    got = r.results[0]["out_0_dram"]
    return _np.ascontiguousarray(got.reshape(D, B, S).transpose(1, 2, 0))
```

```python
import numpy as np
import concourse.bass as bass
from concourse import mybir
from contextlib import ExitStack, contextmanager

F32 = mybir.dt.float32
F32R = mybir.dt.float32r
BF16 = mybir.dt.bfloat16
ALU = mybir.AluOpType
ACT = mybir.ActivationFunctionType
AX = mybir.AxisListType

P = 128
B, S, D = 4, 1024, 128
H, DH, FREQS = 16, 64, 32
PAIRS = H // 2
TILES = S // P
CH = 512
DEPTH = 2
LH, LD = 8, 64
WIN = 64
HID = int(D * 4 * 2 / 3)
NHID = -(-HID // P)
BIG = -1e30
QKV_C = (3.0 * D * DH * H) ** -0.25
OUT_C = (H * DH * D) ** -0.25
ZW = S + 4

STEPS = [(c, j) for c in range(S // CH) for j in range(4 * (c + 1))]
PIECES = [(i, 0, min(P * (i + 1), CH)) for i in range(TILES)] + [(i, CH, P * (i + 1) - CH) for i in range(4, TILES)]
NS, NPC = len(STEPS), len(PIECES)


def _half(c, j):
    return max(0, P * j - CH * c)


@contextmanager
def semaphores(nc, suffix=""):
    held = []

    def sem(name):
        held.append(nc.alloc_semaphore(name=name + suffix))
        return held[-1]
    yield sem
    nc.clear_and_free_semaphores(held)
    nc.all_engine_barrier()


class Mem:
    pass


def add_mod_and_weights(nc, m, i, scratch):
    with ExitStack() as ctx:
        sb = lambda n, s, d=F32: ctx.enter_context(nc.sbuf_tensor(n, s, d))
        ps = lambda n, s: ctx.enter_context(nc.psum_tensor(n, s, F32))
        sem = ctx.enter_context(semaphores(nc))
        w3 = sb("w3", [P, 3, H * DH])
        wqT = sb("wqT", [DH, H, P])
        posT = sb("posT", [DH, H, 2 * FREQS])
        biasT = sb("biasT", [P, H])
        cT = sb("cT", [P, B])
        sT = sb("sT", [P, B])
        wmod = sb("wmod", [P, 6 * D])
        wc = sb("wc", [P, PAIRS, 4, P])
        whl = sb("whl", [P, PAIRS, 2, 4 * P], F32R)
        sg = sb("sg", [P, 2, B])
        ab = sb("ab", [P, 2, B])
        sel32 = sb("sel32", [8, 8, P])
        masks = sb("masks32", [P, 2 * P + 2 * 192])
        comp = [ps(f"comp{k}", [P, CH]) for k in range(2)]
        modp = ps("modp", [P, CH])
        biasp = ps("biasp", [P, CH])
        loaded, consts, weights_out = sem("loaded"), sem("consts_in"), sem("weights_out")
        silu_done, mod_ready, comp_ready, pos_bias = sem("silu_done"), sem("mod_ready"), sem("comp_ready"), sem("pos_bias")
        chain, wc_ready, lo_ready = sem("chain"), sem("wc_ready"), sem("lo_ready")
        block = ctx.enter_context(nc.Block())
        NC = 8

        @block.sync
        def _(sp):
            sp.dma_start(w3[:, :, :], i["qkv"].rearrange("x a n h -> x a (n h)")).then_inc(loaded, 16)
            sp.dma_start(wqT[:, :, :], i["wqT"]).then_inc(loaded, 16)
            sp.dma_start(posT[:, :, :], i["posT"]).then_inc(loaded, 16)
            sp.dma_start(biasT[0:DH, :], i["biasT"]).then_inc(loaded, 16)
            sp.dma_start(cT[:, :], i["cT"]).then_inc(loaded, 16)
            sp.dma_start(wmod[:, :], i["wmod"]).then_inc(loaded, 16)
            sp.dma_start(m.ident[:, :], i["ident"]).then_inc(consts, 16)
            sp.dma_start(m.mean[:, :], i["mean"]).then_inc(consts, 16)
            sp.dma_start(m.oneh[:, :, :], i["oneh"]).then_inc(consts, 16)
            sp.dma_start(sel32[:, :, :], i["sel"]).then_inc(consts, 16)
            sp.dma_start(masks[:, :], i["masks"]).then_inc(consts, 16)
            sp.dma_start(m.vecs[:, :], i["vecs"]).then_inc(consts, 16)
            sp.dma_start(m.b1[:, :, :, :], i["b1"]).then_inc(consts, 16)
            sp.dma_start(m.X[:, :], i["xT"]).then_inc(consts, 16)
            sp.wait_ge(consts, 16 * NC)
            parts = scratch.rearrange("q p (a w) -> a p q w", a=2)
            sp.wait_ge(wc_ready, 5)
            sp.dma_start(parts[0], whl[:, :, 0, :].bitcast(F32)).then_inc(weights_out, 16)
            sp.wait_ge(lo_ready, 1)
            sp.dma_start(parts[1], whl[:, :, 1, :].bitcast(F32)).then_inc(weights_out, 16)
            sp.wait_ge(weights_out, 32)

        @block.scalar
        def _(act):
            act.wait_ge(loaded, 96)
            act.activation(sT[:, :], cT[:, :], ACT.Silu).then_inc(silu_done, 1)

        @block.tensor
        def _(pe):
            pe.wait_ge(loaded, 96)
            for h in range(H):
                mm = pe.matmul(comp[h // 8][:, 64 * (h % 8):64 * (h % 8) + 64], wqT[:, h, :], posT[:, h, :],
                               start=(h % 8 == 0), stop=True, skip_group_check=True)
            mm.then_inc(comp_ready, 1)
            for h in range(H):
                mm = pe.matmul(biasp[64:128, h:1 + h], posT[:, h, :], biasT[0:DH, h:h + 1],
                               start=(h == 0), stop=True, skip_group_check=True)
            mm.then_inc(pos_bias, 1)
            pe.wait_ge(silu_done, 1)
            for k in range(6):
                mm = pe.matmul(modp[:, B * k:B * k + B], wmod[:, P * k:P * k + P], sT[:, :],
                               start=(k == 0), stop=True, skip_group_check=True)
            mm.then_inc(mod_ready, 1)

        @block.vector
        def _(dve):
            dve.wait_ge(loaded, 96)
            src = w3[:, :, :].rearrange("p a (q n) -> p a q n", n=P)
            q2 = w3[:, 0, :].rearrange("p (q e d) -> p q e d", e=2, d=DH)
            dve.tensor_copy(wc[:, :, 0:2, 0:DH], q2).then_inc(wc_ready, 1)
            dve.tensor_copy(wc[:, :, 2, :], src[:, 1]).then_inc(wc_ready, 1)
            dve.tensor_copy(wc[:, :, 3, :], src[:, 2]).then_inc(wc_ready, 1)
            dve.wait_ge(comp_ready, 1)
            for k in range(2):
                last = dve.tensor_copy(wc[:, 4 * k:4 * k + 4, 0:2, DH:P],
                                       comp[k][:, :].rearrange("p (q e d) -> p q e d", e=2, d=DH))
            last.then_inc(wc_ready, 1)
            dve.wait_ge(wc_ready, 4)
            dve.tensor_copy(whl[:, :, 0, :], wc[:, :, :, :].rearrange("p q a w -> p q (a w)")).then_inc(wc_ready, 1)
            dve.wait_ge(wc_ready, 5)
            dve.tensor_tensor(whl[:, :, 1, :], wc[:, :, :, :].rearrange("p q a w -> p q (a w)"),
                              whl[:, :, 0, :].bitcast(F32), ALU.subtract).then_inc(lo_ready, 1)
            dve.tensor_scalar(m.bias[0:DH, :], biasT[0:DH, :], 1.0 / QKV_C, None, ALU.mult)
            dve.wait_ge(pos_bias, 1)
            dve.tensor_scalar(m.bias[DH:P, :], biasp[DH:P, 0:H], 1.0 / QKV_C, None, ALU.mult)
            dve.wait_ge(consts, 16 * NC)
            dve.tensor_copy(m.identb[:, :], m.ident[:, :])
            dve.tensor_copy(m.sel[:, :, :], sel32[:, :, :])
            dve.tensor_copy(m.masks[:, :], masks[:, :])
            for k in range(2):
                for e in range(2):
                    dve.tensor_copy(m.lmask[:, k, 192 * e:192 * e + 192], masks[:, 2 * P + 192 * k:2 * P + 192 * k + 192])
            dve.wait_ge(mod_ready, 1)
            dve.tensor_copy(m.mod[:, :, :], modp[:, 0:6 * B].rearrange("p (k b) -> p k b", b=B)).then_inc(chain, 1)
            dve.wait_ge(chain, 1)
            mod2 = m.mod[:, :, :].rearrange("p (a t) b -> p a t b", t=3)
            dve.tensor_scalar(mod2[:, :, 1, :], mod2[:, :, 1, :], 1.0, None, ALU.add)
            dve.tensor_scalar(sg[:, :, :], mod2[:, :, 2, :], 0.0, 2.0, ALU.is_ge, ALU.mult).then_inc(chain, 1)
            dve.scalar_tensor_tensor(out=ab[:, :, :], in0=mod2[:, :, 2, :], scalar=-1.0, in1=mod2[:, :, 2, :],
                                     op0=ALU.mult, op1=ALU.max).then_inc(chain, 1)
            dve.wait_ge(chain, 3)
            dve.tensor_scalar(sg[:, :, :], sg[:, :, :], -1.0, None, ALU.add).then_inc(chain, 1)
            dve.tensor_scalar(ab[:, :, :], ab[:, :, :], 0.25, None, ALU.max).then_inc(chain, 1)
            dve.wait_ge(chain, 5)
            dve.tensor_tensor(mod2[:, :, 2, :], ab[:, :, :], sg[:, :, :], ALU.mult)


def add_layernorm(nc, m, name, src, scale, shift, dst, meanwhile=None):
    N = B * S // CH
    LOW_BY_DVE = (3, N - 1)
    with ExitStack() as ctx:
        sb = lambda n, s, d=F32: ctx.enter_context(nc.sbuf_tensor(f"{name}_{n}", s, d))
        ps = lambda n, s: ctx.enter_context(nc.psum_tensor(f"{name}_{n}", s, F32))
        sem = ctx.enter_context(semaphores(nc, f"_{name}"))
        dev = sb("dev", [P, N, CH])
        sq = sb("sq", [P, 2, CH])
        sd = sb("sd", [N, CH])
        rstd = sb("rstd", [N, CH])
        rstd_h, rstd_l = sb("rstd_h", [N, CH], F32R), sb("rstd_l", [N, CH], F32R)
        meanp = [ps(f"meanp{k}", [P, CH]) for k in range(2)]
        varp = ps("varp", [P, CH])
        rb = [ps(f"rb{k}", [P, CH]) for k in range(2)]
        mean_ready, dev_ready, sq_ready, sq_used, var_ready = (
            sem("mean_ready"), sem("dev_ready"), sem("sq_ready"), sem("sq_used"), sem("var_ready"))
        sd_ready, rstd_ready, rb_ready, norm_ready, mod_ready, hi_ready = (
            sem("sd_ready"), sem("rstd_ready"), sem("rb_ready"), sem("norm_ready"), sem("mod_ready"), sem("hi_ready"))
        block = ctx.enter_context(nc.Block())

        if meanwhile:
            meanwhile = meanwhile(nc, ctx, sem)

            @block.sync
            def _(sp):
                meanwhile["sync"](sp)

        @block.tensor
        def _(pe):
            for n in range(N + 1):
                if n < N:
                    if n >= 2:
                        pe.wait_ge(dev_ready, n - 1)
                    pe.matmul(meanp[n % 2][:, :], m.mean[:, :], src(n), start=True, stop=True).then_inc(mean_ready, 1)
                if n >= 1:
                    pe.wait_ge(sq_ready, n)
                    mm = pe.matmul(varp[0:N, :], m.oneh[:, n - 1, :], sq[:, (n - 1) % 2, :],
                                   start=(n == 1), stop=(n == N))
                    mm.then_inc(sq_used, 1)
            pe.wait_ge(rstd_ready, 3)
            for n in range(N):
                if n >= 2:
                    pe.wait_ge(norm_ready, n - 1)
                pe.matmul(rb[n % 2][:, :], m.sel[:, n, :], rstd_h[:, :], start=True, stop=False)
                pe.matmul(rb[n % 2][:, :], m.sel[:, n, :], rstd_l[:, :], start=False, stop=True).then_inc(rb_ready, 1)

        @block.vector
        def _(dve):
            if dst == "Z":
                dve.memset(m.Z3[64:P, :, 0:1], 0.0)
            for n in range(N):
                dve.wait_ge(mean_ready, n + 1)
                dve.tensor_tensor(dev[:, n, :], src(n), meanp[n % 2][:, :], ALU.subtract).then_inc(dev_ready, 1)
            dve.wait_ge(sd_ready, 1)
            dve.reciprocal(rstd[:, :], sd[:, :]).then_inc(rstd_ready, 1)
            dve.wait_ge(rstd_ready, 1)
            dve.tensor_copy(rstd_h[:, :], rstd[:, :]).then_inc(rstd_ready, 1)
            dve.wait_ge(rstd_ready, 2)
            dve.tensor_tensor(rstd_l[:, :], rstd[:, :], rstd_h[:, :].bitcast(F32), ALU.subtract).then_inc(rstd_ready, 1)
            for n in range(N):
                dve.wait_ge(rb_ready, n + 1)
                dve.tensor_tensor(dev[:, n, :], dev[:, n, :], rb[n % 2][:, :], ALU.mult).then_inc(norm_ready, 1)
                dve.wait_ge(norm_ready, n + 1)
                if dst == "split":
                    dve.tensor_scalar(dev[:, n, :], dev[:, n, :], scale(n), shift(n), ALU.mult, ALU.add).then_inc(mod_ready, 1)
                    if n - 1 in LOW_BY_DVE or n in LOW_BY_DVE and n == N - 1:
                        k = n if n == N - 1 else n - 1
                        dve.wait_ge(hi_ready, k + 1)
                        dve.tensor_tensor(m.HL[:, k, :], dev[:, k, :], m.HH[:, k, :].bitcast(F32), ALU.subtract)
                else:
                    b, c = n // 2, CH * (n % 2)
                    for lo, o in ((0, 0), (64, 1)):
                        dve.tensor_scalar(m.Z3[lo:lo + 64, b, c + o:c + o + CH], dev[lo:lo + 64, n, :],
                                          scale(n)[lo:lo + 64], shift(n)[lo:lo + 64], ALU.mult, ALU.add)
            if meanwhile:
                meanwhile["vector"](dve)

        @block.scalar
        def _(act):
            for n in range(N):
                act.wait_ge(dev_ready, n + 1)
                if n >= 2:
                    act.wait_ge(sq_used, n - 1)
                act.activation(sq[:, n % 2, :], dev[:, n, :], ACT.Square).then_inc(sq_ready, 1)
                if meanwhile:
                    meanwhile["between"](act, n)
            act.wait_ge(sq_used, N)
            act.activation(sd[:, :], varp[0:N, :], ACT.Sqrt, bias=m.eps[0:N, :]).then_inc(sd_ready, 1)
            if meanwhile:
                meanwhile["scalar"](act)
            if dst == "split":
                for n in range(N):
                    act.wait_ge(mod_ready, n + 1)
                    act.activation(m.HH[:, n, :], dev[:, n, :], ACT.Copy).then_inc(hi_ready, 1)

        @block.gpsimd
        def _(pool):
            if meanwhile:
                meanwhile["gpsimd"](pool)
            if dst == "split":
                for n in range(N):
                    if n in LOW_BY_DVE:
                        continue
                    pool.wait_ge(hi_ready, n + 1)
                    pool.tensor_tensor(m.HL[:, n, :], dev[:, n, :], m.HH[:, n, :].bitcast(F32), ALU.subtract)


class AttentionMemory:
    pass


SLOT = 4


def allocate_attention(nc, ctx):
    sb = lambda n, s, d=F32: ctx.enter_context(nc.sbuf_tensor(n, s, d))
    a = AttentionMemory()
    a.kh = [sb(f"kh{h}", [P, S], F32R) for h in range(SLOT)]
    a.kl = [sb(f"kl{h}", [P, S], F32R) for h in range(SLOT)]
    a.vh = [sb(f"vh{p}", [P, TILES, 3, DH], F32R) for p in range(2)]
    a.vl = [sb(f"vl{p}", [P, TILES, 3, DH], F32R) for p in range(2)]
    a.ph = sb("ph", [P, 3, CH], F32R)
    a.pl = sb("pl", [P, 3, CH], F32R)
    a.ou = [sb(f"ou{e}", [P, S]) for e in range(2)]
    a.den = sb("den", [P, 2, TILES])
    a.rb = sb("rb", [P, S])
    a.ot = sb("ot", [P, S])
    a.qa = sb("qa", [P, S])
    a.gate = sb("gate", [P, B])
    a.gate_bias = sb("gate_bias", [P, B])
    return a


def prepare_attention(m, i):
    a = m.att

    def work(nc, ctx, sem):
        tables_in, high, settled, gates = sem("tables_in"), sem("position_high"), sem("settled"), sem("gates")
        T = slice(DH, DH + FREQS)
        tk = a.ou[0]

        def sync(sp):
            sp.dma_start(tk[T, :], i["tk"]).then_inc(tables_in, 16)
            sp.dma_start(a.qa[:, :], i["qa"]).then_inc(tables_in, 16)

        def between(act, n):
            h = n - 2
            if h == 0:
                act.wait_ge(tables_in, 32)
            if 0 <= h < SLOT:
                act.activation(a.kh[h][T, :], tk[T, :], ACT.Copy).then_inc(high, 1)

        def gpsimd(pool):
            for h in range(SLOT):
                ones = pool.memset(a.kh[h][96:97, :].bitcast(F32), 1.0)
            ones.then_inc(settled, 1)
            pool.wait_ge(settled, 1)
            for p in range(2):
                pool.memset(a.vh[p][:, :, 1, :].bitcast(F32), 1.0)
                pool.memset(a.vl[p][:, :, 1, :].bitcast(F32), 0.0)
            for v in (a.vh[1], a.vl[1]):
                pool.memset(v[:, TILES - 1, 0:3:2, :].bitcast(F32), 0.0)
            pool.memset(a.ph[:, (NS - 1) % 3, :].bitcast(F32), 0.0)
            pool.memset(a.pl[:, (NS - 1) % 3, :].bitcast(F32), 0.0)
            pool.memset(a.ot[:, :], 0.0)
            pool.memset(a.rb[:, :], 0.0)
            pool.memset(a.ou[1][:, :], 0.0)
            pool.memset(a.den[:, 1, :], 1.0).then_inc(settled, 1)
            pool.wait_ge(settled, 2)
            pool.wait_ge(tables_in, 32)
            pool.wait_ge(high, SLOT)
            for h in range(SLOT):
                low = pool.tensor_tensor(a.kl[h][T, :], tk[T, :], a.kh[h][T, :].bitcast(F32), ALU.subtract)
            low.then_inc(settled, 1)
            pool.wait_ge(settled, 3)

        def vector(dve):
            dve.tensor_scalar(a.gate_bias[:, :], m.mod[:, 2, :], m.vecs[:, 0:1], None, ALU.mult).then_inc(gates, 1)
            dve.tensor_scalar(a.gate[:, :], m.mod[:, 2, :], OUT_C, None, ALU.mult)
            dve.wait_ge(gates, 1)
            for b in range(B):
                x = m.X[:, S * b:S * b + S]
                dve.tensor_scalar(x, x, a.gate_bias[:, b:b + 1], None, ALU.add)

        return {"sync": sync, "between": between, "scalar": lambda act: None, "vector": vector, "gpsimd": gpsimd}
    return work


def add_attention(nc, m, i, scratch, dinv):
    ITERS = PAIRS // 2 * B
    PREP = 10
    with ExitStack() as ctx:
        sb = lambda n, s, d=F32: ctx.enter_context(nc.sbuf_tensor(n, s, d))
        ps = lambda n, s=(P, CH): ctx.enter_context(nc.psum_tensor(n, list(s), F32))
        sem = ctx.enter_context(semaphores(nc))

        a = m.att
        kh, kl, vh, vl, ph, pl, ou, den, rb, ot, qa, gate = (
            a.kh, a.kl, a.vh, a.vl, a.ph, a.pl, a.ou, a.den, a.rb, a.ot, a.qa, a.gate)
        qh = [sb(f"qh{h}", [P, S], F32R) for h in range(SLOT)]
        ql = [sb(f"ql{h}", [P, S], F32R) for h in range(SLOT)]
        wts = [sb(f"wts{p}", [P, 2, 4, P], F32R) for p in range(2)]
        wo = [sb(f"wo{p}", [P, P]) for p in range(2)]
        qf = sb("qf", [P, 2, CH])
        qt = sb("qt", [P, 2, CH])
        vt = sb("vt", [P, S])
        p32 = sb("p32", [P, 3, CH])
        mxp = sb("mxp", [P, 2, NPC])
        mrow = sb("mrow", [TILES, 2, P], F32R)
        rcp = sb("rcp", [P, 2, TILES])
        st = [ps(f"st{k}") for k in range(2)]
        sm = [ps(f"sm{k}") for k in range(2)]
        po = [ps(f"po{k}") for k in range(2)]
        g0, g1 = ps("g0"), ps("g1")

        w_in = [sem("wA_in"), sem("wB_in")]
        wo_in = [sem("woA_in"), sem("woB_in")]
        g0_ready = sem("g0_ready")
        g0_by_dve, g0_by_act = sem("g0_by_dve"), sem("g0_by_act")
        g1_ready, g1_read = sem("g1_ready"), sem("g1_read")
        qt_ready = sem("qt_ready")
        qsum_ready = sem("qsum_ready")
        qh_ready, ql_ready = sem("qh_ready"), sem("ql_ready")
        kh_ready, kl_ready = sem("kh_ready"), sem("kl_ready")
        sm_ready, mx_done = sem("sm_ready"), sem("mx_done")
        mx_ready, mrow_in = sem("mx_ready"), sem("mrow_in")
        st_ready, pt_ready, pv_done = sem("st_ready"), sem("pt_ready"), sem("pv_done")
        pl_by_dve, pl_by_pool = sem("pl_by_dve"), sem("pl_by_pool")
        vh_ready, vl_ready = sem("vh_ready"), sem("vl_ready")
        ou_ready = sem("ou_ready")
        den_in, rcp_ready, dinv_out, rb_in = sem("den_in"), sem("rcp_ready"), sem("dinv_out"), sem("rb_in")
        ot_ready = sem("ot_ready")

        PROJ = [("q", 0, 0), ("q", 0, 1), ("k", 0, 0), ("k", 0, 1), ("q", 1, 0), ("q", 1, 1),
                ("v", 0, 0), ("v", 0, 1), ("vt", 0, 0), ("vt", 0, 1)]
        PROJ_AT = [(0, 1), (0, 3), (0, 7), (0, 9), (0, 11), (1, 1), (1, 3), (1, 5), (1, 7), (1, 10)]
        QH_AT = [(0, 3), (0, 5), (1, 3), (1, 5)]
        BY_POOL = [0, 2, 7, 8]
        BY_DVE = [s for s in range(NS) if s not in BY_POOL]
        MAX_AT = [0, 0, 1, 1, 2, 3, 4, 4, 6, 6, 7, 7]
        MROW_AT, RCP_AT, OUT_AT = 8, 4, (4, 6)

        def pieces_at(s):
            return [p for p in range(NPC) if MAX_AT[p] == s]

        SUM_AT, NORM_AT = (2, 3), 9

        def low_parts(n, s):
            if s in BY_POOL:
                return pl_by_pool, len(BY_POOL) * n + BY_POOL.index(s) + 1
            return pl_by_dve, len(BY_DVE) * n + BY_DVE.index(s) + 4

        def at(places, e, s):
            return [n for n in range(len(places)) if places[n] == (e, s)]

        def cols(c, j):
            return slice(_half(c, j), CH)

        block = ctx.enter_context(nc.Block())

        @block.sync
        def _(sp):
            def group(it):
                return (it >> 2) & 3 if isinstance(it, int) else sp.snap(it >> 2) & 3

            def load_w(p, u):
                u = bass.ds(u, 1)
                src = scratch.rearrange("(u s) p w -> s p u w", s=2)[p][:, u, :]
                sp.dma_start(wts[p][:, :, :, :].bitcast(F32).rearrange("p a c w -> p (a c w)"),
                             src.rearrange("p u w -> p (u w)")).then_inc(w_in[p], 16)

            def load_wo(p, u):
                u = bass.ds(u, 1)
                src = i["wo"].rearrange("(u s p) d -> s p u d", s=2, p=P)[p][:, u, :]
                sp.dma_start(wo[p][:, :], src.rearrange("p u d -> p (u d)")).then_inc(wo_in[p], 16)

            def reciprocals(n, e):
                row = 64 * (1 - e)
                sp.wait_ge(ou_ready, 2 * n + 4)
                sp.dma_start(den[:, e, :], ou[e][row:row + 1, :].rearrange("a (p t) -> a p t", t=TILES))\
                  .then_inc(den_in, 16)
                sp.wait_ge(rcp_ready, n + 2)
                sp.dma_start(dinv[e].rearrange("(p t) -> p t", t=TILES), rcp[:, e, :]).then_inc(dinv_out, 16)
                sp.wait_ge(dinv_out, 16 * (n + 1))
                sp.dma_start(rb[64 * e:64 * e + 64, :], dinv[e:e + 1].broadcast_to([64, S])).then_inc(rb_in, 16)

            def send_max(slot, par, use):
                sp.wait_ge(g1_read, use)
                sp.dma_start(qh[slot][96:97, :].bitcast(F32).rearrange("a (t w) -> a t w", t=TILES),
                             mrow[:, par, :].bitcast(F32)).then_inc(mrow_in, 16)

            load_w(0, 0)
            load_w(1, 0)
            load_wo(0, 0)
            load_wo(1, 0)
            send_max(0, 0, 1)
            with sp.Fori(0, ITERS) as it:
                for q in range(2):
                    g = 2 * it + q
                    u, now = group(it + 1), group(it + q)
                    sp.wait_ge(g0_ready, PREP * g + PREP)
                    load_w(q, u)
                    send_max((2 * q + 1) % SLOT, 1, 4 * g + 2)
                    reciprocals(2 * g, 0)
                    send_max((2 * q + 2) % SLOT, 0, 4 * g + 5)
                    load_wo(1 - q, now)
                    reciprocals(2 * g + 1, 1)
            for p in range(2):
                sp.wait_ge(w_in[p], 16 * (ITERS + 1))
                sp.wait_ge(wo_in[p], 16 * (ITERS + 1))

        @block.tensor
        def _(pe):
            def three(out, w_hi, w_lo, x_hi, x_lo, stop=True):
                pe.matmul(out, w_hi, x_hi, start=True, stop=False)
                pe.matmul(out, w_hi, x_lo, start=False, stop=False)
                return pe.matmul(out, w_lo, x_hi, start=False, stop=stop)

            def project(n, p, b, before, first=False):
                if n in (1, 2, 5, 6):
                    pe.wait_ge(g0_by_dve, 4 * before + (n if n < 3 else n - 2))
                elif n in (3, 4):
                    pe.wait_ge(kl_ready, 4 * before + 2 * (n - 2))
                elif n in (7, 8):
                    pe.wait_ge(g0_by_act, 2 * before + n - 6)
                elif n == 9:
                    pe.wait_ge(vl_ready, 2 * before + 1)
                elif not first:
                    pe.wait_ge(vl_ready, 2 * before)
                what, e, c = PROJ[n]
                if what == "vt":
                    for t in range(4):
                        mm = pe.transpose(g0[:, P * t:P * t + P], vt[:, CH * c + P * t:CH * c + P * t + P], m.ident[:, :])
                else:
                    w = {"q": e, "k": 2, "v": 3}[what]
                    xh = m.HH[:, bass.ds(2 * b + c, 1), :].rearrange("p a w -> p (a w)")
                    xl = m.HL[:, bass.ds(2 * b + c, 1), :].rearrange("p a w -> p (a w)")
                    mm = three(g0[:, :], wts[p][:, 0, w, :], wts[p][:, 1, w, :], xh, xl)
                mm.then_inc(g0_ready, 1)

            def max_piece(p, slot, n, first=False):
                t, k0, w = PIECES[p]
                if not (first and p < 2):
                    pe.wait_ge(mx_done, NPC * n + p - 1)
                diag = k0 + w == P * (t + 1)
                out = sm[p % 2]
                mm = pe.matmul(out[:, 0:w], qh[slot][0:96, P * t:P * t + P], kh[slot][0:96, k0:k0 + w],
                               start=True, stop=not diag)
                if diag:
                    mm = pe.matmul(out[:, w - P:w], m.identb[:, :], m.masks[:, 0:P], start=False, stop=True)
                mm.then_inc(sm_ready, 1)

            def turn_max(n, par):
                pe.wait_ge(mx_ready, n + 1)
                pe.transpose(g1[0:TILES, 0:P], mxp[:, par, 0:TILES], m.ident[:, :]).then_inc(g1_ready, 1)

            def scores(s, slot, t):
                c, j = STEPS[s]
                k = slice(P * j, P * j + P)
                x = slice(CH * c + _half(c, j), CH * c + CH)
                w = CH - _half(c, j)
                out = st[s % 2]
                pe.matmul(out[:, 0:w], kh[slot][0:97, k], qh[slot][0:97, x], start=True, stop=False)
                pe.matmul(out[:, 0:w], kh[slot][0:96, k], ql[slot][0:96, x], start=False, stop=False)
                mm = pe.matmul(out[:, 0:w], kl[slot][0:96, k], qh[slot][0:96, x], start=False, stop=j < 4 * c)
                if j >= 4 * c:
                    mm = pe.matmul(out[:, 0:P], m.identb[:, :], m.masks[:, P:2 * P], start=False, stop=True)
                mm.then_inc(st_ready, 1)

            def outputs(s, n, q, e, k, g):
                c, j = STEPS[s]
                if j == 0:
                    pe.wait_ge(ou_ready, k + 1)
                    pe.wait_ge(vl_ready, 2 * g + 2)
                hi, lo = (v[q][:, j, :, :].rearrange("p a d -> p (a d)")[:, 64 * e:64 * e + P] for v in (vh, vl))
                w = CH - _half(c, j)
                out = po[c][:, cols(c, j)]
                pe.matmul(out, hi, ph[:, s % 3, 0:w], start=(j == 0), stop=False)
                pe.matmul(out, lo, ph[:, s % 3, 0:w], start=False, stop=False)
                pe.wait_ge(*low_parts(n, s))
                pe.matmul(out, hi, pl[:, s % 3, 0:w], start=False, stop=(j == 4 * c + 3)).then_inc(pv_done, 1)

            def product(c, p, g, use):
                pe.wait_ge(g1_read, use)
                if c == 0:
                    pe.wait_ge(ot_ready, 2 * g + 3)
                pe.matmul(g1[:, :], wo[p][:, :], ot[:, CH * c:CH * c + CH], start=True, stop=True).then_inc(g1_ready, 1)

            pe.wait_ge(w_in[0], 16)
            for n in range(PREP):
                project(n, 0, 0, 0, first=True)
            pe.wait_ge(qh_ready, 4)
            pe.wait_ge(kh_ready, 4)
            for p in range(NPC):
                max_piece(p, 0, 0, first=True)
            turn_max(0, 0)
            pe.wait_ge(ql_ready, 4)
            pe.wait_ge(kl_ready, 4)
            pe.wait_ge(mrow_in, 16)
            scores(0, 0, 0)
            pe.matmul(po[1][:, :], vl[1][:, TILES - 1, 0:2, :].rearrange("p a d -> p (a d)"), ph[:, (NS - 1) % 3, :], start=True, stop=False)
            with pe.Fori(0, ITERS) as it:
                for q in range(2):
                    g = 2 * it + q
                    for e in range(2):
                        n = 2 * g + e
                        nxt = (2 * q + e + 1) % SLOT
                        for s in range(NS):
                            t = NS * n + s
                            pe.wait_ge(pt_ready, t + 1)
                            if s + 1 < NS:
                                scores(s + 1, 2 * q + e, t + 1)
                            else:
                                pe.wait_ge(mrow_in, 16 * n + 32)
                                if e == 1:
                                    pe.wait_ge(ql_ready, 4 * g + 8)
                                    pe.wait_ge(kl_ready, 4 * g + 8)
                                scores(0, nxt, t + 1)
                            for p in pieces_at(s):
                                if p == 0 and e == 1:
                                    pe.wait_ge(qh_ready, 4 * g + 6)
                                    pe.wait_ge(kh_ready, 4 * g + 8)
                                max_piece(p, nxt, n + 1)
                            for k in at(PROJ_AT, e, s):
                                if k == 0:
                                    pe.wait_ge(w_in[1 - q], 16 * it + 16 + 16 * q)
                                project(k, 1 - q, (it + q) & 3, g + 1)
                            if e == 1 and s in OUT_AT:
                                c = OUT_AT.index(s)
                                if c == 0:
                                    pe.wait_ge(wo_in[1 - q], 16 * it + 16)
                                product(c, 1 - q, g, 4 * g + 2 + c)
                            if s == MROW_AT:
                                pe.wait_ge(g1_read, 4 * g + (4 if e else 1))
                                turn_max(n + 1, 1 - e)
                            if s > 0:
                                outputs(s - 1, n, q, e, 2 * n + STEPS[s - 1][0], g)
                            else:
                                outputs(NS - 1, n - 1, q if e else 1 - q, 1 - e, None, None)
            pe.wait_ge(pt_ready, 2 * NS * PAIRS * B + 1)
            outputs(NS - 1, 2 * PAIRS * B - 1, 1, 1, None, None)
            pe.wait_ge(wo_in[1], 16 * ITERS + 16)
            for c in range(2):
                pe.wait_ge(g1_read, 4 * PAIRS * B + 1 + c)
                if c == 0:
                    pe.wait_ge(ot_ready, 2 * PAIRS * B + 3)
                pe.matmul(g1[:, :], wo[1][:, :], ot[:, CH * c:CH * c + CH], start=True, stop=True).then_inc(g1_ready, 1)

        @block.scalar
        def _(act):
            def project(n, p, before):
                what, e, c = PROJ[n]
                x = slice(CH * c, CH * c + CH)
                act.wait_ge(g0_ready, PREP * before + n + 1)
                if what == "k":
                    for h in range(2):
                        act.activation(kh[2 * p + h][0:DH, x], g0[DH * h:DH * h + DH, :], ACT.Copy, scale=QKV_C)\
                           .then_inc(kh_ready, 1)
                elif what == "v":
                    act.activation(vt[:, x], g0[:, :], ACT.Copy, scale=QKV_C).then_inc(g0_by_act, 1)
                elif what == "vt":
                    act.activation(vh[p][:, 4 * c:4 * c + 4, 0:3:2, :],
                                   g0[:, :].rearrange("p (t h d) -> p t h d", t=4, h=2), ACT.Copy).then_inc(vh_ready, 1)

            def q_high(r, p, before):
                x = slice(CH * (r % 2), CH * (r % 2) + CH)
                act.wait_ge(qsum_ready, 4 * before + r + 1)
                act.activation(qh[2 * p + r // 2][0:96, x], qf[0:96, r % 2, :], ACT.Copy).then_inc(qh_ready, 1)

            def exp(s, n):
                c, j = STEPS[s]
                t = NS * n + s
                w = CH - _half(c, j)
                act.wait_ge(st_ready, t + 1)
                act.wait_ge(*(low_parts(n, s - 3) if s >= 3 else low_parts(n - 1, s - 3 + NS)))
                act.activation(p32[:, s % 3, 0:w], st[s % 2][:, 0:w], ACT.Exp)
                act.wait_ge(pv_done, t + 1)
                act.activation(ph[:, s % 3, 0:w], st[s % 2][:, 0:w], ACT.Exp).then_inc(pt_ready, 1)

            def chunk_out(n, e, c):
                act.wait_ge(pv_done, NS * n + (4 if c == 0 else NS) + 3)
                act.wait_ge(ot_ready, n + 2)
                act.activation(ou[e][:, CH * c:CH * c + CH], po[c][:, :], ACT.Copy).then_inc(ou_ready, 1)

            for n in range(PREP):
                if PROJ[n][0] != "q":
                    project(n, 0, 0)
                if n in (1, 5):
                    q_high(n // 4 * 2, 0, 0)
                    q_high(n // 4 * 2 + 1, 0, 0)
            exp(0, 0)
            with act.Fori(0, ITERS) as it:
                for q in range(2):
                    g = 2 * it + q
                    for e in range(2):
                        n = 2 * g + e
                        for s in range(NS):
                            exp((s + 1) % NS, n + (s + 1) // NS)
                            for k in at(PROJ_AT, e, s):
                                if PROJ[k][0] != "q":
                                    project(k, 1 - q, g + 1)
                            for r in at(QH_AT, e, s):
                                q_high(r, 1 - q, g + 1)
                            if s == 0:
                                chunk_out(n - 1, 1 - e, 1)
                            if s == 4:
                                chunk_out(n, e, 0)
            chunk_out(2 * PAIRS * B - 1, 1, 1)

        @block.vector
        def _(dve):
            def project(n, p, u, before, first=False):
                what, e, c = PROJ[n]
                x = slice(CH * c, CH * c + CH)
                if what == "q":
                    r = 2 * e + c
                    dve.wait_ge(g0_ready, PREP * before + n + 1)
                    if not first or r >= 2:
                        dve.wait_ge(ql_ready, 4 * before + r - 1)
                        dve.wait_ge(qh_ready, 4 * before + r - 1)
                    h = bass.ds(4 * u + 2 * p + e, 1)
                    lo = slice(DH + FREQS, P)
                    dve.scalar_tensor_tensor(out=qt[DH:DH + FREQS, r % 2, :], in0=g0[lo, :], scalar=m.bias[lo, h],
                                             in1=qa[lo, x], op0=ALU.add, op1=ALU.mult).then_inc(qt_ready, 1)
                    dve.scalar_tensor_tensor(out=qf[0:96, r % 2, :], in0=g0[0:96, :], scalar=m.bias[0:96, h],
                                             in1=qa[0:96, x], op0=ALU.add, op1=ALU.mult).then_inc(g0_by_dve, 1)
                elif what == "k":
                    for h in range(2):
                        dve.wait_ge(kh_ready, 4 * before + 2 * c + h + 1)
                        ins = dve.scalar_tensor_tensor(
                            out=kl[2 * p + h][0:DH, x], in0=g0[DH * h:DH * h + DH, :], scalar=QKV_C,
                            in1=kh[2 * p + h][0:DH, x].bitcast(F32), op0=ALU.mult, op1=ALU.subtract)
                        ins.then_inc(kl_ready, 1)
                elif what == "vt":
                    dve.wait_ge(vh_ready, 2 * before + c + 1)
                    part = slice(4 * c, 4 * c + 4)
                    dve.tensor_tensor(vl[p][:, part, 0:3:2, :], g0[:, :].rearrange("p (t h d) -> p t h d", t=4, h=2),
                                      vh[p][:, part, 0:3:2, :].bitcast(F32), ALU.subtract).then_inc(vl_ready, 1)

            def max_piece(p, n, par):
                dve.wait_ge(sm_ready, NPC * n + p + 1)
                dve.tensor_reduce(mxp[:, par, p:p + 1], sm[p % 2][:, 0:PIECES[p][2]], AX.X, ALU.max).then_inc(mx_done, 1)

            def join_max(n, par):
                dve.wait_ge(mx_done, NPC * (n + 1))
                dve.tensor_tensor(mxp[:, par, 4:8], mxp[:, par, 4:8], mxp[:, par, 8:12], ALU.max).then_inc(mx_ready, 1)

            def max_rows(n, par, use):
                dve.wait_ge(g1_ready, use + 1)
                dve.tensor_scalar(mrow[:, par, :], g1[0:TILES, 0:P], -1.0, None, ALU.mult).then_inc(g1_read, 1)

            def low_part(s, t):
                w = CH - _half(*STEPS[s])
                dve.wait_ge(pt_ready, t + 2)
                dve.wait_ge(pv_done, t + 1)
                dve.tensor_tensor(pl[:, s % 3, 0:w], p32[:, s % 3, 0:w], ph[:, s % 3, 0:w].bitcast(F32), ALU.subtract)\
                   .then_inc(pl_by_dve, 1)

            def reciprocal(n, e):
                dve.wait_ge(den_in, 16 * n + 32)
                dve.reciprocal(rcp[:, e, :], den[:, e, :]).then_inc(rcp_ready, 1)

            def accumulate(c, b, use):
                dve.wait_ge(g1_ready, use + 1)
                x = m.X[:, bass.ds(S * b + CH * c, CH)]
                dve.scalar_tensor_tensor(out=x, in0=g1[:, :], scalar=gate[:, bass.ds(b, 1)], in1=x, op0=ALU.mult, op1=ALU.add)\
                   .then_inc(g1_read, 1)

            for n in range(PREP):
                project(n, 0, 0, 0, first=True)
            for p in range(NPC):
                max_piece(p, 0, 0)
            join_max(0, 0)
            max_rows(0, 0, 0)
            with dve.Fori(0, ITERS) as it:
                for q in range(2):
                    g = 2 * it + q
                    u = ((it + q) >> 2) & 3
                    for e in range(2):
                        n = 2 * g + e
                        for s in range(NS):
                            if s in BY_DVE:
                                low_part(s, NS * n + s)
                            for p in pieces_at(s):
                                max_piece(p, n + 1, 1 - e)
                                if p == NPC - 1:
                                    join_max(n + 1, 1 - e)
                            for k in at(PROJ_AT, e, s):
                                project(k, 1 - q, u, g + 1)
                            if e == 1 and s in OUT_AT:
                                c = OUT_AT.index(s)
                                accumulate(c, (it + 3 + q) & 3, 4 * g + 2 + c)
                            if s == MROW_AT:
                                max_rows(n + 1, 1 - e, 4 * g + (4 if e else 1))
                            if s == RCP_AT:
                                reciprocal(n - 1, 1 - e)
            last = 2 * PAIRS * B - 1
            reciprocal(last, 1)
            for c in range(2):
                accumulate(c, 3, 4 * PAIRS * B + 1 + c)

        @block.gpsimd
        def _(pool):
            def low_part(s, n, before):
                t = NS * n + s
                w = CH - _half(*STEPS[s])
                if before:
                    pool.wait_ge(*before)
                pool.wait_ge(pt_ready, t + 2)
                pool.wait_ge(pv_done, t + 1)
                pool.tensor_tensor(pl[:, s % 3, 0:w], p32[:, s % 3, 0:w], ph[:, s % 3, 0:w].bitcast(F32), ALU.subtract)\
                    .then_inc(pl_by_pool, 1)

            def position_sum(r, projected, before):
                T = slice(DH, DH + FREQS)
                if before:
                    pool.wait_ge(*before)
                pool.wait_ge(g0_by_dve, 4 * projected + r + 1)
                pool.wait_ge(qt_ready, 4 * projected + r + 1)
                pool.tensor_tensor(qf[T, r % 2, :], qf[T, r % 2, :], qt[T, r % 2, :], ALU.add).then_inc(qsum_ready, 1)

            def q_low(r, p, projected):
                x = slice(CH * (r % 2), CH * (r % 2) + CH)
                pool.wait_ge(qh_ready, 4 * projected + r + 1)
                h = 2 * p + r // 2
                pool.tensor_tensor(ql[h][0:96, x], qf[0:96, r % 2, :], qh[h][0:96, x].bitcast(F32), ALU.subtract)\
                    .then_inc(ql_ready, 1)

            def normalise(n, e, before):
                rows = slice(64 * e, 64 * e + 64)
                pool.wait_ge(*before)
                pool.wait_ge(rb_in, 16 * n + 32)
                pool.tensor_tensor(ot[rows, :], ou[e][rows, :], rb[rows, :], ALU.mult).then_inc(ot_ready, 1)

            pool.sem_inc(pt_ready, 1)
            pool.sem_inc(pv_done, 2)
            pool.sem_inc(pl_by_dve, 3)
            pool.sem_inc(ou_ready, 1)
            pool.sem_inc(ot_ready, 2)
            pool.sem_inc(den_in, 16)
            pool.sem_inc(rb_in, 16)
            for r in range(4):
                position_sum(r, 0, (ql_ready, r) if r else None)
                q_low(r, 0, 0)
            pool.wait_ge(ql_ready, 4)
            with pool.Fori(0, ITERS) as it:
                for q in range(2):
                    g = 2 * it + q
                    for e in range(2):
                        n = 2 * g + e
                        r = 2 * e
                        before = (ot_ready, n + 2)
                        for s in range(NS):
                            if s in BY_POOL:
                                low_part(s, n, before)
                                before = low_parts(n, s)
                            if s in SUM_AT:
                                k = SUM_AT.index(s)
                                position_sum(r + k, g + 1, before)
                                q_low(r + k, 1 - q, g + 1)
                                before = (ql_ready, 4 * (g + 1) + r + k + 1)
                            if s == NORM_AT:
                                if e == 1:
                                    pool.wait_ge(g1_ready, 4 * g + 4)
                                normalise(n - 1, 1 - e, before)
                                before = (ot_ready, n + 3)
            last = 2 * PAIRS * B - 1
            normalise(last, 1, (ot_ready, last + 2))


class Layer:
    pass


def allocate_layers(nc, ctx):
    layers = []
    for n in range(DEPTH):
        sb = lambda name, s, d=F32: ctx.enter_context(nc.sbuf_tensor(f"{name}_of{n}", s, d))
        w = Layer()
        w.wh, w.wl = sb("wh", [P, 3 * CH], F32R), sb("wl", [P, 3 * CH], F32R)
        w.wo = sb("lwo", [P, LH // 2, P])
        w.tab = sb("tab", [P, TILES, 2, 2, LD])
        w.w1h, w.w1l = sb("w1h", [P, 2 * HID], F32R), sb("w1l", [P, 2 * HID], F32R)
        w.w2 = sb("w2", [P, NHID, D])
        layers.append(w)
    return layers


def load_layers(m, i):
    def work(nc, ctx, sem):
        w32 = [ctx.enter_context(nc.sbuf_tensor(f"w32_{n}", [P, 3 * CH], F32)) for n in range(DEPTH)]
        w132 = [ctx.enter_context(nc.sbuf_tensor(f"w132_{n}", [P, 2 * HID], F32)) for n in range(DEPTH)]
        scl = [ctx.enter_context(nc.sbuf_tensor(f"scl_{n}", [P, 2, 2, LD], F32)) for n in range(DEPTH)]
        loaded, split_high = sem("layers_loaded"), sem("layers_split_high")
        LOADS = 7

        def sync(sp):
            for n, w in enumerate(m.layers):
                sp.dma_start(w32[n][:, :], i["wqkv"][n]).then_inc(loaded, 16)
                sp.dma_start(w.wo[:, :, :], i["lwo"][n].rearrange("(q p) d -> p q d", p=P)).then_inc(loaded, 16)
                sp.dma_start(w.tab[:, :, :, :, :], i["rot"]).then_inc(loaded, 16)
                sp.dma_start(scl[n][:, :, :, :].rearrange("p a b d -> p (a b d)"),
                             i["qkscale"][n:n + 1].broadcast_to([P, 4 * LD])).then_inc(loaded, 16)
                sp.dma_start(w132[n][:, :], i["w1"][n]).then_inc(loaded, 16)
                full = HID // P
                sp.dma_start(w.w2[:, 0:full, :], i["w2"][n, 0:P * full].rearrange("(q p) d -> p q d", p=P)).then_inc(loaded, 16)
                sp.dma_start(w.w2[0:HID - P * full, full, :], i["w2"][n, P * full:HID]).then_inc(loaded, 16)

        def scalar(act):
            act.wait_ge(loaded, 16 * LOADS * DEPTH)
            for n, w in enumerate(m.layers):
                act.activation(w.wh[:, :], w32[n][:, :], ACT.Copy)
                act.activation(w.w1h[:, :], w132[n][:, :], ACT.Copy).then_inc(split_high, 1)

        def gpsimd(pool):
            pool.wait_ge(loaded, 16 * LOADS * DEPTH)
            for n, w in enumerate(m.layers):
                for a in range(2):
                    tt = w.tab[:, :, a, :, :]
                    pool.tensor_tensor(tt, tt, scl[n][:, a, :, :].unsqueeze(1).broadcast_to([P, TILES, 2, LD]), ALU.mult)
            for n, w in enumerate(m.layers):
                pool.wait_ge(split_high, n + 1)
                pool.tensor_tensor(w.wl[:, :], w32[n][:, :], w.wh[:, :].bitcast(F32), ALU.subtract)
                pool.tensor_tensor(w.w1l[:, :], w132[n][:, :], w.w1h[:, :].bitcast(F32), ALU.subtract)

        return {"sync": sync, "between": lambda act, n: None, "scalar": scalar, "vector": lambda dve: None, "gpsimd": gpsimd}
    return work


def add_local_attention(nc, m, layer):
    NT, X = B * TILES, 4
    NIT = NT // X
    KW = 192
    GH = 4
    with ExitStack() as ctx:
        sb = lambda n, s, d=F32: ctx.enter_context(nc.sbuf_tensor(f"{n}_l{layer}", s, d))
        ps = lambda n, s=(P, CH): ctx.enter_context(nc.psum_tensor(f"{n}_l{layer}", list(s), F32))
        sem = ctx.enter_context(semaphores(nc, f"_l{layer}"))
        w = m.layers[layer]
        wh, wl, wo, tab = w.wh, w.wl, w.wo, w.tab
        zt = sb("zt", [P, 2, 2, P], F32R)
        qk = sb("qk", [P, 2, 2, CH])
        t1 = sb("t1", [P, 2, CH])
        t2 = sb("t2", [P, 2, CH])
        sq = sb("sq", [P, 2, CH])
        ss = sb("ss", [P, 2 * LH])
        nhalf = sb("nhalf", [P, 2 * LH])
        r = sb("r", [P, X, 2 * LH])
        qT = sb("qT", [P, LH // 2, P])
        kT = sb("kT", [P, 2, LH // 2, KW])
        v = sb("v", [P, 4, CH])
        pb = sb("pb", [P, 2, GH, 2 * P])
        mx = sb("mx", [P, 2, GH])
        nm = sb("nm", [P, 2, GH])
        sums = sb("sums", [P, 2, GH])
        rs = sb("rs", [P, 2, GH])
        pT = sb("pT", [P, 2, CH])
        oT = sb("oT", [P, LH // 2, P])
        qk_ps = ps("qk_ps", (P, 2, CH))
        s_ps = ps("s_ps", (P, 2, CH))
        v_ps, ta_ps, tb_ps, o_ps = ps("v_ps"), ps("ta_ps"), ps("tb_ps"), ps("o_ps")

        ready = sem("lready")
        zt_hi, zt_ready = sem("zt_hi"), sem("zt_ready")
        qk_ready, qk_copied, sq_ready, summed, ss_ready, r_ready = (
            sem("qk_ready"), sem("qk_copied"), sem("sq_ready"), sem("summed"), sem("ss_ready"), sem("r_ready"))
        cos_done, sin_done, turned, rot_ready = sem("cos_done"), sem("sin_done"), sem("turned"), sem("rot_ready")
        v_ready, v_read = sem("v_ready"), sem("v_read")
        ta_ready, ta_read, tb_ready, tb_read, kT_ready, halo = (
            sem("ta_ready"), sem("ta_read"), sem("tb_ready"), sem("tb_read"), sem("kT_ready"), sem("halo"))
        t0_read = sem("t0_read")
        s_ready, mx_done, nm_ready, exp_done, rs_ready, pn_ready = (
            sem("s_ready"), sem("lmx_done"), sem("nm_ready"), sem("exp_done"), sem("rs_ready"), sem("pn_ready"))
        o_ready, oT_ready, wo_ready, z_done = sem("o_ready"), sem("oT_ready"), sem("wo_ready"), sem("z_done")
        block = ctx.enter_context(nc.Block())

        def zoff(it, x):
            k = x // X
            turn = (it + (NIT + k)) & (NIT - 1) if k else it
            return (turn >> 1) * ZW + (turn & 1) * (X * P) + P * (x % X)

        def tile_in_batch(it, x):
            k = x // X
            turn = (it + (NIT + k)) & (NIT - 1) if k else it
            return (turn & 1) * X + x % X

        def table(a, T, d):
            w = d.stop - d.start
            if isinstance(T, int):
                src = tab[:, T:T + 1, a, :, d]
            else:
                src = tab[:, bass.ds(T, 1), a, :, d]
            return src.rearrange("p o b d -> p (o b) d").unsqueeze(2).broadcast_to([P, 2, LH, w])

        @block.tensor
        def _(pe):
            def project(slot_ring):
                zh, zl = zt[:, slot_ring, 0, :], zt[:, slot_ring, 1, :]
                for n in range(3):
                    if n == 2:
                        yield
                    w = slice(CH * n, CH * n + CH)
                    out = qk_ps[:, n, :] if n < 2 else v_ps[:, :]
                    pe.matmul(out, zh, wh[:, w], start=True, stop=False)
                    pe.matmul(out, zh, wl[:, w], start=False, stop=False)
                    mm = pe.matmul(out, zl, wh[:, w], start=False, stop=True)
                    if n:
                        mm.then_inc(qk_ready if n == 1 else v_ready, 1)
                yield

            def scores(g, ring, mask):
                for e in range(2):
                    pe.matmul(s_ps[:, e, 0:2 * KW], m.identb[:, :], mask, start=True, stop=True)
                    for s in range(2):
                        rows = slice(LD * e, LD * e + LD)
                        mm = pe.matmul(s_ps[:, e, KW * s:KW * s + KW], qT[rows, 2 * g + s, :], kT[rows, ring, 2 * g + s, :],
                                       start=False, stop=True, skip_group_check=True)
                mm.then_inc(s_ready, 1)

            def turn_probs(g, s):
                bank, sm_ = (ta_ps, ta_ready) if s == 0 else (tb_ps, tb_ready)
                for e in range(2):
                    for a in range(2):
                        mm = pe.transpose(bank[:, P * (2 * e + a):P * (2 * e + a) + P],
                                          pb[:, g, 2 * s + e, P * a:P * a + P], m.ident[:, :])
                mm.then_inc(sm_, 1)

            def outputs(g, s, cur, prev):
                for e in range(2):
                    h = GH * g + 2 * s + e
                    d = slice(LD * h, LD * h + LD)
                    out = o_ps[LD * e:LD * e + LD, P * (2 * g + s):P * (2 * g + s) + P]
                    pe.matmul(out, v[:, prev, d], pT[:, s, 2 * P * e:2 * P * e + P], start=True, stop=False)
                    mm = pe.matmul(out, v[:, cur, d], pT[:, s, 2 * P * e + P:2 * P * e + 2 * P], start=False, stop=True)
                return mm

            def turn_qk():
                for n, (bank, sm_) in enumerate(((ta_ps, ta_ready), (tb_ps, tb_ready))):
                    for q in range(4):
                        mm = pe.transpose(bank[:, P * q:P * q + P], t1[:, n, P * q:P * q + P], m.ident[:, :])
                    mm.then_inc(sm_, 1)

            def first_outputs(t, cur, prev):
                pe.wait_ge(oT_ready, t + 1)
                pe.wait_ge(t0_read, t + 1)
                outputs(0, 0, cur, prev)
                pe.wait_ge(tb_read, 2 * t + 1)
                outputs(0, 1, cur, prev)

            def finish_probs(t):
                pe.wait_ge(pn_ready, 2 * t + 1)
                pe.wait_ge(t0_read, t + 1)
                turn_probs(1, 0)
                pe.wait_ge(tb_read, 2 * t + 1)
                turn_probs(1, 1)

            def finish_outputs(t, cur, prev):
                pe.wait_ge(ta_read, 2 * t + 2)
                outputs(1, 0, cur, prev)
                pe.wait_ge(tb_read, 2 * t + 2)
                outputs(1, 1, cur, prev).then_inc(o_ready, 1)

            def product(t, last=False):
                pe.wait_ge(oT_ready, t + 2)
                if last:
                    pe.wait_ge(z_done, t + 1)
                else:
                    pe.wait_ge(v_read, t + 3)
                for q in range(4):
                    mm = pe.matmul(v_ps[:, 0:P], wo[:, q, :], oT[:, q, :], start=(q == 0), stop=(q == 3))
                mm.then_inc(wo_ready, 1)

            pe.wait_ge(ready, 2)
            for k in range(2):
                pe.wait_ge(zt_ready, k + 1)
                if k == 1:
                    pe.wait_ge(qk_copied, 1)
                    pe.wait_ge(v_read, 1)
                for _ in project(k):
                    pass
            pe.wait_ge(rot_ready, 1)
            turn_qk()
            with pe.Fori(0, NIT) as it:
                for x in range(X):
                    t = it * X + x
                    mask = m.lmask[:, bass.ds(it & 1, 1), :].rearrange("p a w -> p (a w)") if x == 0 else m.lmask[:, 1, :]
                    pe.wait_ge(ta_read, 2 * t + 1)
                    pe.wait_ge(kT_ready, t + 1)
                    pe.wait_ge(halo, t + 1)
                    pe.wait_ge(exp_done, 2 * t + 1)
                    scores(0, x % 2, mask)
                    first_outputs(t, (x + 3) % 4, (x + 2) % 4)
                    finish_probs(t)
                    nxt = project(x % 2)
                    pe.wait_ge(zt_ready, t + 3)
                    pe.wait_ge(qk_copied, t + 2)
                    next(nxt)
                    pe.wait_ge(v_read, t + 2)
                    pe.wait_ge(z_done, t + 1)
                    next(nxt)
                    finish_outputs(t, (x + 3) % 4, (x + 2) % 4)
                    pe.wait_ge(exp_done, 2 * t + 2)
                    scores(1, x % 2, mask)
                    product(t)
                    pe.wait_ge(rot_ready, t + 2)
                    pe.wait_ge(ta_read, 2 * t + 2)
                    pe.wait_ge(tb_read, 2 * t + 2)
                    turn_qk()
                    pe.wait_ge(pn_ready, 2 * t + 2)
                    pe.wait_ge(ta_read, 2 * t + 3)
                    turn_probs(0, 0)
                    pe.wait_ge(kT_ready, t + 2)
                    turn_probs(0, 1)
            first_outputs(NT, 3, 2)
            finish_probs(NT)
            finish_outputs(NT, 3, 2)
            product(NT, last=True)

        @block.scalar
        def _(act):
            def exps(g, t, ring):
                act.wait_ge(nm_ready, 2 * t + g + 1)
                for e in range(2):
                    for s in range(2):
                        h = GH * g + 2 * s + e
                        ins = act.activation(pb[:, g, 2 * s + e, 64:2 * P], s_ps[:, e, KW * s:KW * s + KW], ACT.Exp,
                                             bias=nm[:, g, 2 * e + s:2 * e + s + 1], scale=r[:, ring, h:h + 1],
                                             accum_out=sums[:, g, 2 * s + e:2 * s + e + 1])
                ins.then_inc(exp_done, 1)

            def from_ta(dst, use):
                act.wait_ge(ta_ready, use)
                act.activation(dst, ta_ps[:, :], ACT.Copy).then_inc(ta_read, 1)

            def take_out(t):
                act.wait_ge(o_ready, t + 1)
                act.wait_ge(wo_ready, t + 1)
                act.activation(oT[:, :, :].rearrange("p q t -> p (q t)"), o_ps[:, :], ACT.Copy).then_inc(oT_ready, 1)

            def copy_qk(count, ring):
                act.wait_ge(qk_ready, count)
                act.activation(qk[:, ring, :, :], qk_ps[:, :, :], ACT.Copy).then_inc(qk_copied, 1)

            def square(count, ring):
                act.wait_ge(qk_copied, count)
                act.activation(sq[:, :, :], qk[:, ring, :, :], ACT.Square).then_inc(sq_ready, 1)

            def take_v(t1_, slot):
                act.wait_ge(v_ready, t1_)
                act.activation(v[:, slot, :], v_ps[:, :], ACT.Copy).then_inc(v_read, 1)

            def take_qk(use, t1_, ring):
                from_ta(qT[:, :, :].rearrange("p q t -> p (q t)"), use)
                act.wait_ge(tb_ready, use)
                act.activation(kT[:, ring, :, 64:KW], tb_ps[:, :].rearrange("p (q t) -> p q t", q=4), ACT.Copy)\
                   .then_inc(kT_ready, 1)

            act.wait_ge(ready, 2)
            copy_qk(1, 0)
            take_v(1, 0)
            square(1, 0)
            copy_qk(2, 1)
            take_v(2, 1)
            act.wait_ge(ss_ready, 1)
            square(2, 1)
            take_qk(1, 1, 0)
            with act.Fori(0, NIT) as it:
                for x in range(X):
                    t = it * X + x
                    from_ta(pT[:, 0, :], 3 * t + 2)
                    exps(0, t, x)
                    act.wait_ge(rot_ready, t + 1)
                    copy_qk(t + 3, x % 2)
                    take_out(t)
                    take_v(t + 3, (x + 2) % 4)
                    act.wait_ge(ss_ready, t + 2)
                    square(t + 3, x % 2)
                    take_qk(3 * t + 3, t + 2, (x + 1) % 2)
                    exps(1, t, x)
            from_ta(pT[:, 0, :], 3 * NT + 2)
            take_out(NT)

        @block.vector
        def _(dve):
            def split_tile(off, ring, count):
                z = m.Z[:, bass.ds(off, P)] if not isinstance(off, int) else m.Z[:, off:off + P]
                dve.tensor_copy(zt[:, ring, 0, :], z).then_inc(zt_hi, 1)
                dve.wait_ge(zt_hi, count)
                dve.tensor_tensor(zt[:, ring, 1, :], z, zt[:, ring, 0, :].bitcast(F32), ALU.subtract).then_inc(zt_ready, 1)

            def turn_cos(T, count, ring):
                dve.wait_ge(qk_copied, count)
                dve.tensor_tensor(t1[:, :, :].rearrange("p n (h d) -> p n h d", d=LD),
                                  qk[:, ring, :, :].rearrange("p n (h d) -> p n h d", d=LD),
                                  table(0, T, slice(0, LD)), ALU.mult).then_inc(cos_done, 1)

            def squares(count):
                dve.wait_ge(sq_ready, count)
                dve.tensor_reduce(ss[:, :], sq[:, :, :].rearrange("p n (h d) -> p (n h) d", d=LD), AX.X, ALU.add)\
                   .then_inc(summed, 1)
                dve.wait_ge(summed, count)
                dve.tensor_scalar(ss[:, :], ss[:, :], 1e-24, None, ALU.max).then_inc(ss_ready, 1)

            def turn(count):
                dve.wait_ge(cos_done, count)
                dve.wait_ge(sin_done, count)
                dve.tensor_tensor(t1[:, :, :], t1[:, :, :], t2[:, :, :], ALU.add).then_inc(turned, 1)

            def normalise_k(ring, count):
                dve.wait_ge(turned, count)
                dve.wait_ge(r_ready, count)
                k = t1[:, 1, :].rearrange("p (h d) -> p h d", d=LD)
                dve.tensor_tensor(k, k, r[:, ring, LH:2 * LH].unsqueeze(2).broadcast_to([P, LH, LD]), ALU.mult)\
                   .then_inc(rot_ready, 1)

            def take_halo(ring, count):
                dve.wait_ge(kT_ready, count)
                dve.tensor_copy(kT[:, 1 - ring, :, 0:64], kT[:, ring, :, P:KW]).then_inc(halo, 1)

            def maxima(g, t, ring):
                dve.wait_ge(s_ready, 2 * t + g + 1)
                dve.tensor_reduce(mx[:, g, :].rearrange("p (e s) -> p e s", e=2),
                                  s_ps[:, :, 0:2 * KW].rearrange("p e (s w) -> p e s w", s=2), AX.X, ALU.max).then_inc(mx_done, 1)
                dve.wait_ge(mx_done, 2 * t + g + 1)
                rq = r[:, ring, GH * g:GH * g + GH].rearrange("p (s e) -> p e s", e=2)
                dve.scalar_tensor_tensor(out=nm[:, g, :].rearrange("p (e s) -> p e s", e=2),
                                         in0=mx[:, g, :].rearrange("p (e s) -> p e s", e=2), scalar=-1.0, in1=rq,
                                         op0=ALU.mult, op1=ALU.mult).then_inc(nm_ready, 1)

            def reciprocal(g, count):
                dve.wait_ge(exp_done, count)
                dve.reciprocal(rs[:, g, :], sums[:, g, :]).then_inc(rs_ready, 1)

            def from_tb(use):
                dve.wait_ge(tb_ready, use)
                dve.tensor_copy(pT[:, 1, :], tb_ps[:, :]).then_inc(tb_read, 1)

            def add_to_z(off, t):
                dve.wait_ge(wo_ready, t + 2)
                for rows, o in ((slice(0, 64), 0), (slice(64, P), 1)):
                    z = m.Z[rows, bass.ds(off + o, P)] if not isinstance(off, int) else m.Z[rows, off + o:off + o + P]
                    ins = dve.tensor_tensor(z, z, v_ps[rows, 0:P], ALU.add)
                ins.then_inc(z_done, 1)

            dve.memset(pb[:, :, :, 0:P], 0.0)
            dve.memset(pb[:, :, :, P:2 * P], 0.0)
            dve.memset(pT[:, :, :], 0.0)
            dve.memset(v[:, 2:4, :], 0.0)
            dve.memset(kT[:, 0, :, 0:64], 0.0)
            dve.memset(sums[:, 1, :], 1.0)
            dve.memset(nhalf[:, :], -0.5).then_inc(ready, 1)
            split_tile(0, 0, 1)
            split_tile(P, 1, 2)
            turn_cos(0, 1, 0)
            squares(1)
            dve.wait_ge(v_ready, 1)
            split_tile(2 * P, 0, 3)
            turn(1)
            normalise_k(0, 1)
            dve.wait_ge(r_ready, 1)
            squares(2)
            take_halo(0, 1)
            with dve.Fori(0, NIT) as it:
                for x in range(X):
                    t = it * X + x
                    reciprocal(1, 2 * t + 1)
                    dve.wait_ge(ta_ready, 3 * t + 1)
                    dve.wait_ge(tb_ready, 3 * t + 1)
                    turn_cos(tile_in_batch(it, x + 1), t + 2, (x + 1) % 2)
                    maxima(0, t, x)
                    from_tb(3 * t + 2)
                    turn(t + 2)
                    normalise_k((x + 1) % X, t + 2)
                    reciprocal(0, 2 * t + 2)
                    maxima(1, t, x)
                    dve.wait_ge(r_ready, t + 2)
                    squares(t + 3)
                    add_to_z(zoff(it, x - 1), t)
                    split_tile(zoff(it, x + 3), (x + 1) % 2, t + 4)
                    take_halo((x + 1) % 2, t + 2)
                    dve.wait_ge(ta_ready, 3 * t + 4)
                    dve.tensor_copy(pT[:, 0, :], ta_ps[:, :]).then_inc(t0_read, 1)
                    from_tb(3 * t + 4)
            reciprocal(1, 2 * NT + 1)
            from_tb(3 * NT + 2)
            add_to_z((B - 1) * ZW + (TILES - 1) * P, NT)

        @block.gpsimd
        def _(pool):
            def norms(ring, count):
                pool.wait_ge(ss_ready, count)
                pool.tensor_tensor(r[:, ring, :], ss[:, :], nhalf[:, :], ALU.pow).then_inc(r_ready, 1)

            def normalise(g, count):
                pool.wait_ge(rs_ready, count)
                p = pb[:, g, :, 64:2 * P]
                pool.tensor_tensor(p, p, rs[:, g, :].unsqueeze(2).broadcast_to([P, GH, KW]), ALU.mult).then_inc(pn_ready, 1)

            def turn_sin(T, ring):
                q = qk[:, ring, :, :].rearrange("p n (h d) -> p n h d", d=LD)
                o = t2[:, :, :].rearrange("p n (h d) -> p n h d", d=LD)
                lo, hi = slice(0, LD // 2), slice(LD // 2, LD)
                pool.tensor_tensor(o[:, :, :, lo], q[:, :, :, hi], table(1, T, lo), ALU.mult)
                pool.tensor_tensor(o[:, :, :, hi], q[:, :, :, lo], table(1, T, hi), ALU.mult).then_inc(sin_done, 1)

            pool.sem_inc(exp_done, 1)
            pool.sem_inc(oT_ready, 1)
            pool.sem_inc(z_done, 1)
            pool.sem_inc(tb_read, 1)
            pool.sem_inc(t0_read, 1)
            pool.sem_inc(wo_ready, 1)
            pool.sem_inc(ready, 1)
            pool.wait_ge(ready, 2)
            pool.wait_ge(qk_copied, 1)
            turn_sin(0, 0)
            norms(0, 1)
            pool.wait_ge(turned, 1)
            pool.wait_ge(qk_copied, 2)
            turn_sin(1, 1)
            with pool.Fori(0, NIT) as it:
                for x in range(X):
                    t = it * X + x
                    normalise(1, 2 * t + 1)
                    norms((x + 1) % X, t + 2)
                    normalise(0, 2 * t + 2)
                    pool.wait_ge(qk_copied, t + 3)
                    turn_sin(tile_in_batch(it, x + 2), x % 2)
            normalise(1, 2 * NT + 1)


def add_mlp(nc, m, layer):
    with ExitStack() as ctx:
        sb = lambda n, s, d=F32: ctx.enter_context(nc.sbuf_tensor(f"{n}_m{layer}", s, d))
        ps = lambda n: ctx.enter_context(nc.psum_tensor(f"{n}_m{layer}", [P, CH], F32))
        sem = ctx.enter_context(semaphores(nc, f"_m{layer}"))
        w = m.layers[layer]
        wh, wl, w2 = w.w1h, w.w1l, w.w2
        gl = sb("gl", [P, NHID, CH])
        u = sb("u", [P, 2, NHID, CH])
        bank = [ps(f"b{k}") for k in range(2 * NHID)]
        y_ps = [ps(f"y{k}") for k in range(2)]
        g_ready, a_ready, gelu_done, u_ready, y_ready, z_done = (
            sem("g_ready"), sem("a_ready"), sem("gelu_done"), sem("u_ready"), sem("y_ready"), sem("mz_done"))
        ms = [min(P, HID - P * j) for j in range(NHID)]
        block = ctx.enter_context(nc.Block())

        @block.tensor
        def _(pe):
            def hidden(n, half, b, first):
                xh = m.HH[:, bass.ds(2 * b + half, 1), :].rearrange("p a w -> p (a w)")
                xl = m.HL[:, bass.ds(2 * b + half, 1), :].rearrange("p a w -> p (a w)")
                for j in range(NHID):
                    for k, sm_ in ((1, g_ready), (0, a_ready)):
                        w = slice(HID * k + P * j, HID * k + P * j + ms[j])
                        out = bank[2 * j + k][0:ms[j], :]
                        if not first:
                            pe.wait_ge(u_ready, NHID * n + j + 1 - NHID)
                        pe.matmul(out, wh[:, w], xh, start=True, stop=False)
                        pe.matmul(out, wh[:, w], xl, start=False, stop=False)
                        pe.matmul(out, wl[:, w], xh, start=False, stop=True).then_inc(sm_, 1)

            def down(n, half):
                pe.wait_ge(z_done, 2 * n + 2)
                for j in range(NHID):
                    pe.wait_ge(u_ready, NHID * n + j + 1)
                    mm = pe.matmul(y_ps[half][:, :], w2[0:ms[j], j, :], u[0:ms[j], half, j, :], start=(j == 0), stop=(j == NHID - 1))
                mm.then_inc(y_ready, 1)

            hidden(0, 0, 0, True)
            with pe.Fori(0, B) as b:
                hidden(2 * b + 1, 1, b, False)
                down(2 * b, 0)
                hidden(2 * b + 2, 0, (b + 1) & (B - 1), False)
                down(2 * b + 1, 1)

        @block.scalar
        def _(act):
            def gelus(n, first):
                for j in range(NHID):
                    act.wait_ge(g_ready, NHID * n + j + 1)
                    if not first:
                        act.wait_ge(u_ready, NHID * n + j + 1 - NHID)
                    act.activation(gl[0:ms[j], j, :], bank[2 * j + 1][0:ms[j], :], ACT.Gelu,
                                   bias=m.b1[0:ms[j], layer, 1, j:j + 1]).then_inc(gelu_done, 1)
            gelus(0, True)
            with act.Fori(0, B) as b:
                gelus(2 * b + 1, False)
                gelus(2 * b + 2, False)

        @block.vector
        def _(dve):
            def gate(n, half):
                for j in range(NHID):
                    dve.wait_ge(gelu_done, NHID * n + j + 1)
                    dve.wait_ge(a_ready, NHID * n + j + 1)
                    dve.scalar_tensor_tensor(out=u[0:ms[j], half, j, :], in0=bank[2 * j][0:ms[j], :],
                                             scalar=m.b1[0:ms[j], layer, 0, j:j + 1], in1=gl[0:ms[j], j, :],
                                             op0=ALU.add, op1=ALU.mult).then_inc(u_ready, 1)

            def add_to_z(n, half, b):
                dve.wait_ge(y_ready, n + 1)
                for lo, o in ((0, 0), (64, 1)):
                    z = m.Z[lo:lo + 64, bass.ds(ZW * b + CH * half + o, CH)]
                    dve.scalar_tensor_tensor(out=z, in0=y_ps[half][lo:lo + 64, :], scalar=m.vecs[lo:lo + 64, 3 + 3 * layer:4 + 3 * layer],
                                             in1=z, op0=ALU.add, op1=ALU.add).then_inc(z_done, 1)

            dve.sem_inc(z_done, 2)
            gate(0, 0)
            with dve.Fori(0, B) as b:
                gate(2 * b + 1, 1)
                add_to_z(2 * b, 0, b)
                dve.wait_ge(y_ready, 2 * b + 1)
                gate(2 * b + 2, 0)
                add_to_z(2 * b + 1, 1, b)


def add_output(nc, m, out):
    with ExitStack() as ctx:
        sem = ctx.enter_context(semaphores(nc))
        summed, stored = sem("o_summed"), sem("o_stored")
        block = ctx.enter_context(nc.Block())

        @block.vector
        def _(dve):
            for b in range(B):
                for rows, o in ((slice(0, 64), 0), (slice(64, P), 1)):
                    x = m.X[rows, S * b:S * b + S]
                    dve.scalar_tensor_tensor(out=x, in0=m.Z[rows, ZW * b + o:ZW * b + o + S], scalar=m.mod[rows, 5, b:b + 1],
                                             in1=x, op0=ALU.mult, op1=ALU.add).then_inc(summed, 1)

        @block.sync
        def _(sp):
            for b in range(B):
                sp.wait_ge(summed, 2 * b + 2)
                sp.dma_start(out[:, S * b:S * b + S], m.X[:, S * b:S * b + S]).then_inc(stored, 16)
            sp.wait_ge(stored, 16 * B)


def host_constants():
    f = np.float32
    ident = np.eye(P, dtype=f)
    mean = np.full((P, P), 1.0 / D, f)
    N = B * S // CH
    oneh = np.zeros((P, N, N), f)
    sel = np.zeros((N, N, P), f)
    for n in range(N):
        oneh[:, n, n] = 1.0 / D
        sel[n, n, :] = 1.0
    a = np.arange(P)
    nat = np.where(a[None, :] > a[:, None], BIG, 0.0)
    tr = nat.T
    key = np.arange(192)[None, :] - 64
    loc = np.where((key > a[:, None]) | (key < a[:, None] - WIN), BIG, 0.0)
    loc0 = np.where(key < 0, BIG, loc)
    masks = np.concatenate([nat, tr, loc0, loc], 1).astype(f)
    w = 1250.0 ** (-(np.arange(FREQS) // 2 * 2) / FREQS)
    ang = w[:, None] * np.arange(S)[None, :]
    even = (np.arange(FREQS) % 2 == 0)[:, None]
    tk = np.where(even, np.cos(ang), np.sin(ang)).astype(f)
    qa = np.zeros((P, S))
    qa[0:DH] = QKV_C / 8
    qa[DH:DH + FREQS] = QKV_C / 32 * np.sin(ang)
    qa[DH + FREQS:] = QKV_C / 32 * np.where(even, np.cos(ang), -np.cos(ang))
    hidx = np.arange(0, LD, 2, dtype=f)
    inv = (f(1.0) / np.power(f(10000.0), hidx / f(LD))).astype(f)
    tok = np.arange(S, dtype=f)
    fr = tok[:, None] * inv[None, :]
    fr = np.concatenate([fr, fr], 1)
    base = ((hidx + f(0.4 * LD)) / f(1.4 * LD)).astype(f)
    power = ((tok - S // 2) / f(WIN // 2)).astype(f)
    sc = np.power(base[None, :], power[:, None]).astype(f)
    sc = np.concatenate([sc, sc], 1)
    sign = np.where(np.arange(LD) < LD // 2, -1.0, 1.0).astype(f)
    cos, sin = np.cos(fr), np.sin(fr) * sign
    rot = np.stack([np.stack([cos * sc * 8, cos / sc]), np.stack([sin * sc * 8, sin / sc])])
    rot = rot.reshape(2, 2, TILES, P, LD).transpose(3, 2, 0, 1, 4).astype(f)
    return {"rot": rot, "ident": ident, "mean": mean, "oneh": oneh, "sel": sel, "masks": masks, "tk": tk, "qa": qa.astype(f)}


def build(nc, i, scratch, dinv, out):
    with ExitStack() as ctx:
        sb = lambda n, s, d=F32: ctx.enter_context(nc.sbuf_tensor(n, s, d))
        m = Mem()
        m.X = sb("X", [P, B * S])
        m.ident = sb("ident", [P, P])
        m.identb = sb("identb", [P, P], BF16)
        m.masks = sb("masks", [P, 2 * P + 2 * 192], BF16)
        m.mean = sb("mean", [P, P])
        m.oneh = sb("oneh", [P, 8, 8])
        m.sel = sb("sel", [8, 8, P], F32R)
        m.bias = sb("bias", [P, H])
        m.mod = sb("mod", [P, 6, B])
        m.vecs = sb("vecs", [P, 8])
        m.b1 = sb("b1", [P, DEPTH, 2, NHID])
        m.eps = m.vecs[:, 7:8]
        m.lmask = sb("lmask", [P, 2, 2 * 192], BF16)
        add_mod_and_weights(nc, m, i, scratch)
        with ExitStack() as att:
            m.HH = att.enter_context(nc.sbuf_tensor("HH", [P, 8, CH], F32R))
            m.HL = att.enter_context(nc.sbuf_tensor("HL", [P, 8, CH], F32R))
            m.att = allocate_attention(nc, att)
            add_layernorm(nc, m, "ln1", lambda n: m.X[:, CH * n:CH * n + CH],
                          lambda n: m.mod[:, 1, n // 2:n // 2 + 1], lambda n: m.mod[:, 0, n // 2:n // 2 + 1], "split", prepare_attention(m, i))
            add_attention(nc, m, i, scratch, dinv)
        with ExitStack() as ffn:
            m.Z = ffn.enter_context(nc.sbuf_tensor("Z", [P, (B + 1) * ZW], F32))
            m.Z3 = m.Z[:, 0:B * ZW].rearrange("p (b w) -> p b w", b=B)
            m.layers = allocate_layers(nc, ffn)
            one = lambda k: (lambda n: m.vecs[:, k:k + 1])
            add_layernorm(nc, m, "ln2", lambda n: m.X[:, CH * n:CH * n + CH],
                          lambda n: m.mod[:, 4, n // 2:n // 2 + 1], lambda n: m.mod[:, 3, n // 2:n // 2 + 1], "Z", load_layers(m, i))
            for layer in range(DEPTH):
                add_local_attention(nc, m, layer)
                with ExitStack() as mlp:
                    m.HH = mlp.enter_context(nc.sbuf_tensor(f"HH{layer}", [P, 8, CH], F32R))
                    m.HL = mlp.enter_context(nc.sbuf_tensor(f"HL{layer}", [P, 8, CH], F32R))
                    add_layernorm(nc, m, f"ln3{layer}",
                                  lambda n: m.Z[:, ZW * (n // 2) + CH * (n % 2):ZW * (n // 2) + CH * (n % 2) + CH],
                                  one(1 + 3 * layer), one(2 + 3 * layer), "split")
                    add_mlp(nc, m, layer)
            add_output(nc, m, out)


def kernel(**inputs):
    import numpy as _np
    import concourse.bacc as _bacc
    from concourse import mybir as _mybir
    from concourse.bass_utils import run_bass_kernel_spmd as _run

    v = {k.replace("L0_", ""): _np.asarray(a) for k, a in inputs.items()}
    f = _np.float32
    qkv, pos = v["attn_qkv"], v["attn_positional"]
    swap = _np.arange(FREQS) ^ 1
    posT = _np.concatenate([pos.transpose(2, 1, 0), pos[swap].transpose(2, 1, 0)], 2)
    vecs = _np.zeros((P, 8), f)
    vecs[:, 0] = v["attn_out_bias"]
    for l in range(DEPTH):
        vecs[:, 1 + 3 * l] = v["ffn_ln_g"][l]
        vecs[:, 2 + 3 * l] = v["ffn_ln_b"][l]
        vecs[:, 3 + 3 * l] = v["ffn_b2"][l]
    vecs[:, 7] = 1e-5
    b1 = _np.zeros((DEPTH, 2, NHID * P), f)
    b1[:, :, :HID] = v["ffn_b1"].reshape(DEPTH, 2, HID)
    half = (_np.arange(LD) + LD // 2) % LD
    qs = _np.stack([v["ffn_q_scale"], v["ffn_k_scale"]], 1)
    qks = _np.stack([qs, qs[:, :, half]], 1).reshape(DEPTH, 4 * LD)
    data = {
        "xT": v["attn_input"].transpose(2, 0, 1).reshape(D, B * S),
        "qkv": qkv, "wqT": qkv[:, 0].transpose(2, 1, 0), "posT": posT, "biasT": v["attn_q_bias"].T,
        "cT": v["c"].T, "wmod": v["wmod"], "vecs": vecs,
        "b1": b1.reshape(DEPTH, 2, NHID, P).transpose(3, 0, 1, 2),
        "wo": v["attn_out_kernel"], "wqkv": v["ffn_wqkv"], "lwo": v["ffn_wo"], "w1": v["ffn_w1"], "w2": v["ffn_w2"],
        "qkscale": qks,
    } | host_constants()
    nc = _bacc.Bacc("TRN2", target_bir_lowering=False, num_devices=1)
    arrays, aps = {}, {}
    for name, a in data.items():
        a = _np.ascontiguousarray(a)
        arrays[f"in_{name}_dram"] = a
        aps[name] = nc.dram_tensor(f"in_{name}_dram", a.shape, _mybir.dt.from_np(a.dtype), kind="ExternalInput").ap()
    scratch = nc.dram_tensor("split_weights", (PAIRS, P, 2 * 4 * P), F32, kind="Internal").ap()
    dinv = nc.dram_tensor("denominators", (2, S), F32, kind="Internal").ap()
    out = nc.dram_tensor("out_0_dram", (P, B * S), F32, kind="ExternalOutput").ap()
    build(nc, aps, scratch, dinv, out)
    r = _run(nc, [arrays], core_ids=[0])
    got = r.results[0]["out_0_dram"]
    return _np.ascontiguousarray(got.reshape(D, B, S).transpose(1, 2, 0))
```
